# Optimizing a Trainium2 kernel written in Bass

```python
import numpy as np
import jax
import jax.numpy as jnp

def _softmax(x, axis=-1):
    return jax.nn.softmax(x, axis=axis)

def _gelu(x):
    return jax.nn.gelu(x, approximate=True)

def _silu(x):
    return jax.nn.silu(x)

def _sigmoid(x):
    return jax.nn.sigmoid(x)

def _layernorm(x, axis=-1, eps=1e-05):
    m = jnp.mean(x, axis=axis, keepdims=True)
    v = jnp.var(x, axis=axis, keepdims=True)
    return (x - m) / jnp.sqrt(v + eps)

def _scatter_add(tgt, idx, src, axis=0):
    return tgt.at[idx].add(src)

def _segment_sum(src, seg, n):
    return jax.ops.segment_sum(src, seg, n)
kernel_name = 'mk_lm_tower_d1_tok_ids2048_r4_d1a29d'

def setup_inputs(seed: int=0):
    np.random.seed(seed)
    _w = jnp.asarray

    def _rec_inputs():
        import jax
        import jax.numpy as jnp
        _rk = jax.random.key(seed)
        x = jax.random.randint(jax.random.fold_in(_rk, 1), (8, 512), 0, 12564, jnp.int32)
        return x
    x = _rec_inputs()

    def _L0_tok_setup():
        import jax, jax.numpy as jnp
        import numpy as np
        VOCAB = 50257
        EMBED_DIM = 512
        N_LAYERS = 2
        LOCAL_D = EMBED_DIM // 2 // N_LAYERS
        EMBD_D = EMBED_DIM - LOCAL_D * (2 * N_LAYERS - 1)
        KERNEL = 3
        B, T = (16, 512)

        def positional_encoding(max_len, d_model):
            depth = d_model // 2
            positions = jnp.arange(max_len, dtype=jnp.float32)[:, None]
            depths = jnp.arange(depth, dtype=jnp.float32)[None, :] / depth
            angle_rads = positions * (1.0 / 10000.0 ** depths)
            return jnp.concatenate([jnp.sin(angle_rads), jnp.cos(angle_rads)], axis=-1)

        def softpos_axis1(x, spos):
            n_subpos = spos.shape[0]
            m = x[:, :n_subpos, :]
            sel = jax.nn.softmax(m, axis=1)
            ext = jnp.einsum('bjt,jk->bkt', sel, spos)
            return jnp.concatenate([x, ext], axis=1)
        key = jax.random.key(seed)
        ks = jax.random.split(key, 6)
        return {'sequences': jax.random.randint(ks[0], (B, T), 0, VOCAB), 'emb_table': jax.random.normal(ks[1], (VOCAB, EMBD_D), dtype=jnp.float32), 'conv_w': jax.random.normal(ks[2], (LOCAL_D, EMBD_D, KERNEL), dtype=jnp.float32) * 0.05, 'conv_b': jax.random.normal(ks[3], (LOCAL_D,), dtype=jnp.float32) * 0.05, 'spos0': jax.random.normal(ks[4], (LOCAL_D, LOCAL_D), dtype=jnp.float32) * 0.05, 'spos1': jax.random.normal(ks[5], (LOCAL_D, LOCAL_D), dtype=jnp.float32) * 0.05}
    _L0_tok_all = _L0_tok_setup()
    _L0_tok_in = {k: v for k, v in _L0_tok_all.items() if k in ('emb_table', 'conv_w', 'conv_b', 'spos0', 'spos1')}
    del _L0_tok_all

    def _L0_attn_setup():
        import jax, jax.numpy as jnp
        import numpy as np
        EMBED_DIM = 512
        NUM_HEADS = 16
        HEAD_DIM = EMBED_DIM // NUM_HEADS
        SCALE = HEAD_DIM ** (-0.5)
        NEG = -9000000000000000.0

        def _act_quant(x):
            s = 127.0 / jnp.clip(jnp.max(jnp.abs(x), axis=-1, keepdims=True), 1e-05)
            return jnp.clip(jnp.round(x * s), -128.0, 127.0) / s

        def _weight_quant(w):
            s = 1.0 / jnp.clip(jnp.mean(jnp.abs(w)), 1e-05)
            return jnp.clip(jnp.round(w * s), -1.0, 1.0) / s

        def _bitlinear(x, w):
            xq = x + jax.lax.stop_gradient(_act_quant(x) - x)
            wq = w + jax.lax.stop_gradient(_weight_quant(w) - w)
            return jnp.einsum('bnc,oc->bno', xq, wq)
        key = jax.random.key(seed)
        k1, k2, k3 = jax.random.split(key, 3)
        x = jax.random.normal(k1, (2, 512, EMBED_DIM), dtype=jnp.float32)
        w_qkv = jax.random.normal(k2, (3 * EMBED_DIM, EMBED_DIM), dtype=jnp.float32) * EMBED_DIM ** (-0.5)
        w_proj = jax.random.normal(k3, (EMBED_DIM, EMBED_DIM), dtype=jnp.float32) * EMBED_DIM ** (-0.5)
        return {'x': x, 'w_qkv': w_qkv, 'w_proj': w_proj}
    _L0_attn_all = _L0_attn_setup()
    _L0_attn_in = {k: v for k, v in _L0_attn_all.items() if k in ('w_qkv', 'w_proj')}
    del _L0_attn_all

    def _L0_ffn_setup():
        import jax, jax.numpy as jnp
        import numpy as np
        K = 2

        def gelu(v):
            return jax.nn.gelu(v, approximate=False)
        key = jax.random.key(seed)
        ks = jax.random.split(key, 10)
        B, S, D, H, E = (4, 512, 512, 256, 8)
        SH = 2 * H
        u = lambda k_, shape, b: jax.random.uniform(k_, shape, jnp.float32, -b, b)
        return {'x': jax.random.normal(ks[0], (B, S, D), jnp.float32), 'gate_w': u(ks[1], (D, E), 1.0 / D), 'w1': u(ks[2], (E, D, H), 1.0 / D), 'b1': u(ks[3], (E, H), 1.0 / np.sqrt(D)), 'w2': u(ks[4], (E, H, D), 1.0 / H), 'b2': u(ks[5], (E, D), 1.0 / np.sqrt(H)), 'shared_w1': u(ks[6], (D, SH), 1.0 / D), 'shared_b1': u(ks[7], (SH,), 1.0 / np.sqrt(D)), 'shared_w2': u(ks[8], (SH, D), 1.0 / SH), 'shared_b2': u(ks[9], (D,), 1.0 / np.sqrt(SH))}
    _L0_ffn_all = _L0_ffn_setup()
    _L0_ffn_in = {k: v for k, v in _L0_ffn_all.items() if k in ('gate_w', 'w1', 'b1', 'w2', 'b2', 'shared_w1', 'shared_b1', 'shared_w2', 'shared_b2')}
    del _L0_ffn_all
    return {'x': x, 'L0_tok_emb_table': _L0_tok_in['emb_table'], 'L0_tok_conv_w': _L0_tok_in['conv_w'], 'L0_tok_conv_b': _L0_tok_in['conv_b'], 'L0_tok_spos0': _L0_tok_in['spos0'], 'L0_tok_spos1': _L0_tok_in['spos1'], 'L0_attn_w_qkv': _L0_attn_in['w_qkv'], 'L0_attn_w_proj': _L0_attn_in['w_proj'], 'L0_ffn_gate_w': _L0_ffn_in['gate_w'], 'L0_ffn_w1': _L0_ffn_in['w1'], 'L0_ffn_b1': _L0_ffn_in['b1'], 'L0_ffn_w2': _L0_ffn_in['w2'], 'L0_ffn_b2': _L0_ffn_in['b2'], 'L0_ffn_shared_w1': _L0_ffn_in['shared_w1'], 'L0_ffn_shared_b1': _L0_ffn_in['shared_b1'], 'L0_ffn_shared_w2': _L0_ffn_in['shared_w2'], 'L0_ffn_shared_b2': _L0_ffn_in['shared_b2']}

def reference(x, L0_tok_emb_table, L0_tok_conv_w, L0_tok_conv_b, L0_tok_spos0, L0_tok_spos1, L0_attn_w_qkv, L0_attn_w_proj, L0_ffn_gate_w, L0_ffn_w1, L0_ffn_b1, L0_ffn_w2, L0_ffn_b2, L0_ffn_shared_w1, L0_ffn_shared_b1, L0_ffn_shared_w2, L0_ffn_shared_b2):
    import jax
    import jax.numpy as jnp

    def _L0_tok_ref(sequences, emb_table, conv_w, conv_b, spos0, spos1):
        import jax, jax.numpy as jnp
        import numpy as np
        VOCAB = 50257
        EMBED_DIM = 512
        N_LAYERS = 2
        LOCAL_D = EMBED_DIM // 2 // N_LAYERS
        EMBD_D = EMBED_DIM - LOCAL_D * (2 * N_LAYERS - 1)
        KERNEL = 3
        B, T = (16, 512)

        def positional_encoding(max_len, d_model):
            depth = d_model // 2
            positions = jnp.arange(max_len, dtype=jnp.float32)[:, None]
            depths = jnp.arange(depth, dtype=jnp.float32)[None, :] / depth
            angle_rads = positions * (1.0 / 10000.0 ** depths)
            return jnp.concatenate([jnp.sin(angle_rads), jnp.cos(angle_rads)], axis=-1)

        def softpos_axis1(x, spos):
            n_subpos = spos.shape[0]
            m = x[:, :n_subpos, :]
            sel = jax.nn.softmax(m, axis=1)
            ext = jnp.einsum('bjt,jk->bkt', sel, spos)
            return jnp.concatenate([x, ext], axis=1)
        seq_len = sequences.shape[1]
        x = emb_table[sequences] * jnp.sqrt(jnp.float32(EMBD_D))
        x = x + positional_encoding(seq_len, EMBD_D)[None]
        x = jnp.transpose(x, (0, 2, 1))
        dilation = 1
        x_pad = jnp.pad(x, ((0, 0), (0, 0), ((KERNEL - 1) * dilation, 0)))
        xc = jax.lax.conv_general_dilated(x_pad, conv_w, window_strides=(1,), padding='VALID', rhs_dilation=(dilation,), dimension_numbers=('NCH', 'OIH', 'NCH'))
        xc = xc + conv_b[None, :, None]
        y0 = softpos_axis1(x, spos0)
        y1 = softpos_axis1(xc, spos1)
        return jnp.concatenate([y0, y1], axis=1)

    def _L0_attn_ref(x, w_qkv, w_proj):
        import jax, jax.numpy as jnp
        import numpy as np
        EMBED_DIM = 512
        NUM_HEADS = 16
        HEAD_DIM = EMBED_DIM // NUM_HEADS
        SCALE = HEAD_DIM ** (-0.5)
        NEG = -9000000000000000.0

        def _act_quant(x):
            s = 127.0 / jnp.clip(jnp.max(jnp.abs(x), axis=-1, keepdims=True), 1e-05)
            return jnp.clip(jnp.round(x * s), -128.0, 127.0) / s

        def _weight_quant(w):
            s = 1.0 / jnp.clip(jnp.mean(jnp.abs(w)), 1e-05)
            return jnp.clip(jnp.round(w * s), -1.0, 1.0) / s

        def _bitlinear(x, w):
            xq = x + jax.lax.stop_gradient(_act_quant(x) - x)
            wq = w + jax.lax.stop_gradient(_weight_quant(w) - w)
            return jnp.einsum('bnc,oc->bno', xq, wq)
        B, N, C = x.shape
        H, D = (NUM_HEADS, HEAD_DIM)
        qkv = _bitlinear(x, w_qkv).reshape(B, N, 3, H, D)
        q, k, v = (qkv[:, :, 0], qkv[:, :, 1], qkv[:, :, 2])
        attn = jnp.einsum('bnhd,bmhd->bhnm', q, k) * SCALE
        causal = jnp.tril(jnp.ones((N, N), dtype=bool))
        attn = jnp.where(causal, attn, NEG)
        attn = jax.nn.softmax(attn, axis=-1)
        out = jnp.einsum('bhnm,bmhd->bnhd', attn, v).reshape(B, N, C)
        return _bitlinear(out, w_proj)

    def _L0_ffn_ref(x, gate_w, w1, b1, w2, b2, shared_w1, shared_b1, shared_w2, shared_b2):
        import jax, jax.numpy as jnp
        import numpy as np
        K = 2

        def gelu(v):
            return jax.nn.gelu(v, approximate=False)
        B, S, D = x.shape
        E = gate_w.shape[1]
        xf = x.reshape(-1, D)
        logits = xf @ gate_w
        top_logits, top_idx = jax.lax.top_k(logits, K)
        top_gates = jax.nn.softmax(top_logits, axis=-1)
        gates = jnp.sum(jax.nn.one_hot(top_idx, E, dtype=xf.dtype) * top_gates[..., None], axis=1)
        h = gelu(jnp.einsum('nd,edh->neh', xf, w1) + b1)
        out_e = jnp.einsum('neh,ehd->ned', h, w2) + b2
        routed = jnp.einsum('ne,ned->nd', gates, out_e)
        shared = gelu(xf @ shared_w1 + shared_b1) @ shared_w2 + shared_b2
        return (routed + shared).reshape(B, S, D)
    h = _L0_tok_ref(x, L0_tok_emb_table, L0_tok_conv_w, L0_tok_conv_b, L0_tok_spos0, L0_tok_spos1)
    h = h + _L0_attn_ref(_layernorm(h, axis=-1), L0_attn_w_qkv, L0_attn_w_proj)
    h = h + _L0_ffn_ref(_layernorm(h, axis=-1), L0_ffn_gate_w, L0_ffn_w1, L0_ffn_b1, L0_ffn_w2, L0_ffn_b2, L0_ffn_shared_w1, L0_ffn_shared_b1, L0_ffn_shared_w2, L0_ffn_shared_b2)
    return h

_drawn_inputs = setup_inputs


def setup_inputs(seed=0):
    import zlib

    import numpy as np

    out = dict(_drawn_inputs(seed))
    spreads = {}
    factors = {'L0_tok_conv_b': 8.0,
     'L0_tok_spos0': 8.0,
     'L0_tok_spos1': 8.0,
     'L0_attn_w_qkv': 8.0,
     'L0_attn_w_proj': 7.975,
     'L0_ffn_gate_w': 64.0,
     'L0_ffn_w1': 64.0,
     'L0_ffn_b1': 64.0,
     'L0_ffn_w2': 64.0,
     'L0_ffn_b2': 59.547,
     'L0_ffn_shared_w1': 64.0,
     'L0_ffn_shared_b1': 64.0,
     'L0_ffn_shared_w2': 64.0,
     'L0_ffn_shared_b2': 62.084}
    for name, (base, spread) in spreads.items():
        noise = np.random.default_rng([zlib.crc32(name.encode()), seed]).standard_normal(out[name].shape)
        drawn = base * np.exp(spread * noise) if base else spread * noise
        out[name] = jnp.asarray(drawn.astype(out[name].dtype))
    for name, factor in factors.items():
        out[name] = (out[name] * factor).astype(out[name].dtype)
    return out
```

```python
from contextlib import ExitStack

import numpy as np

import concourse.bass as bass
from concourse import mybir

P = 128
ALU = mybir.AluOpType
ACT = mybir.ActivationFunctionType
AX = mybir.AxisListType.X
F32 = mybir.dt.float32
F16 = mybir.dt.float16
BF16 = mybir.dt.bfloat16
I32 = mybir.dt.int32

B, T = 8, 512
CH = 128
N = 4 * CH
C = T
H, DH = 16, 32
NT, KT = N // P, C // P
G, HG = 4, 4
E_, HID = 8, 256
SH = 512
TAPS = 3
PAD = TAPS - 1
EPS = 1e-5
QMAX = 127.0
CLIP = 1e-5
ROUND = 1.5 * 2.0 ** 23
MASKED = -(2.0 ** 100)
ATT_SCALE = DH ** -0.5
KPARTS = 3 * DH
MROWS = 5
MUNIT = 2.0 ** 15


def build(nc, ids, emb, pe_tab, conv_w, conv_b, spos0, spos1, wqkv, wproj, gate_w, w1, b1, w2, b2,
          sw1, sb1, sw2, sb2, ident_in, mask_in, maskT_in, tri_in, lanes_in, out):
    h1_dram = nc.dram_tensor("h1_rows", [B * N, C], F32, kind="Internal").ap()
    x2_dram = nc.dram_tensor("x2_rows", [B * N, 2 * C], F16, kind="Internal").ap()
    attention_phase(nc, ids, emb, pe_tab, conv_w, conv_b, spos0, spos1, wqkv, wproj,
                    ident_in, mask_in, maskT_in, h1_dram, x2_dram)
    ffn_phase(nc, ident_in, tri_in, lanes_in, gate_w, w1, b1, w2, b2, sw1, sb1, sw2, sb2, h1_dram, x2_dram, out)


def attention_phase(nc, ids, emb, pe_tab, conv_w, conv_b, spos0, spos1, wqkv, wproj,
                    ident_in, mask_in, maskT_in, h1_dram, x2_dram):
    ctx = ExitStack()
    with ctx:
        def sb(name, shape, dt):
            return ctx.enter_context(nc.sbuf_tensor(name, shape, dt))

        def ps(name, shape, dt):
            return ctx.enter_context(nc.psum_tensor(name, shape, dt))

        def sem(name):
            return ctx.enter_context(nc.semaphore(name))

        idx = sb("idx", [P, B * NT], I32)
        emb_all = sb("emb_all", [P, B * NT, CH], F32)
        pe_tm = sb("pe_tm", [P, NT, CH], F32)
        convw = sb("convw", [P, TAPS, CH], F32)
        convb = sb("convb", [P, 1], F32)
        sp0 = sb("sp0", [P, CH], F32)
        sp1 = sb("sp1", [P, CH], F32)
        ident = sb("ident", [P, P], F32)
        identb = sb("identb", [P, P], BF16)
        identh = sb("identh", [P, P], F16)
        maskf = sb("maskf", [P, 2, P], F32)
        maskb = sb("maskb", [P, 2, P], BF16)
        ones = sb("ones", [P, P], F32)
        neghalf = sb("neghalf", [P, NT], F32)
        wstage = sb("wstage", [P, KT, 4 * C], F32)
        wq = sb("wq", [P, KT, 4 * C], BF16)
        wsum = sb("wsum", [P, 2], F32)
        wmean = sb("wmean", [P, 2], F32)
        winv = sb("winv", [P, 2], F32)
        escale = sb("escale", [P, 1], F32)

        x_tm = sb("x_tm", [P, NT, CH], F32)
        cmax = sb("cmax", [P, NT], F32)
        tmp4 = sb("tmp4", [P, NT], F32)
        xs = sb("xs", [P, NT, CH], F32)
        ex = sb("ex", [P, NT, CH], F32)
        csum = sb("csum", [P, NT], F32)
        crec = sb("crec", [P, NT], F32)
        sel = sb("sel", [P, NT, CH], F32)
        selT = sb("selT", [P, T], F32)
        h = sb("h", [P, NT, PAD + C], F32)

        stats = sb("stats", [P, NT, 6], F32)
        mv = sb("mv", [P, NT, 2], F32)
        vare = sb("vare", [P, NT], F32)
        rstd = sb("rstd", [P, NT], F32)
        negmean = sb("negmean", [P, NT], F32)
        hc = sb("hc", [P, NT, C], F32)
        amax = sb("amax", [P, NT], F32)
        aval = sb("aval", [P, NT], F32)
        arec = sb("arec", [P, NT], F32)
        astep = sb("astep", [P, NT], F32)
        fscale = sb("fscale", [P, NT], F32)
        xqi = sb("xqi", [P, NT, C], BF16)
        xqT = sb("xqT", [P, KT, N], BF16)
        abc = sb("abc", [P, N], F32)
        diag = sb("diag", [P, NT, P], F32)

        qk32 = sb("qk32", [P, 2, N], F32)
        parts = sb("parts", [P, 2, 2, G, N], F16)
        QS = sb("QS", [P, G, HG, N], F16)
        KS = sb("KS", [P, G, HG, N], F16)
        V = sb("V", [P, NT, C], F32)
        mx = sb("mx", [P, 2, NT, HG], F32)
        mh = sb("mh", [P, NT, HG], F16)
        mr = sb("mr", [P, NT, HG], F32)
        mr2 = sb("mr2", [P, NT, HG], F32)
        mm = sb("mm", [P, NT, HG, DH], F16)
        mT = sb("mT", [P, N], F16)
        pT = sb("pT", [P, 2, HG, N], F32)
        rden = sb("rden", [P, N], F32)
        oT = sb("oT", [P, G, N], F32)

        h1 = wstage[:, 0, :].rearrange("p (r c) -> p r c", r=NT)
        x2 = wstage[:, 1, :].rearrange("p (r c) -> p r c", r=NT)
        x2p = sb("x2p", [P, NT, 2, C], F16)

        ps_s1 = ps("ps_s1", [P, 2, 512], F32)
        ps_s2 = ps("ps_s2", [P, 2, 512], F32)
        ps_o = ps("ps_o", [P, 512], F32)
        ps_den = ps("ps_den", [P, 512], F32)
        ps_w = ps("ps_w", [P, 2, 512], F32)

        loaded = sem("loaded")
        gathered = sem("gathered")
        consts_set = sem("consts_set")
        idents_cast = sem("idents_cast")
        w_step = sem("w_step")
        passed = sem("passed")
        w_summed = sem("w_summed")
        w_ready = sem("w_ready")

        dve_step = (sem("dve_step"), 27)
        pool_step = (sem("pool_step"), 24)
        work_full = (sem("work_full"), 32)
        x_ready = (sem("x_ready"), 1)
        xs_ready = (sem("xs_ready"), 2)
        ex_ready = (sem("ex_ready"), 2)
        sel_ready = (sem("sel_ready"), 2)
        selT_ready = (sem("selT_ready"), 2)
        h_ready = (sem("h_ready"), NT)
        var_ready = (sem("var_ready"), 2)
        rstd_ready = (sem("rstd_ready"), 2)
        hc_ready = (sem("hc_ready"), NT)
        f_ready = (sem("f_ready"), 2)
        qf_ready = (sem("qf_ready"), 2 * NT)
        qi_ready = (sem("qi_ready"), 2 * NT)
        qTa_ready = (sem("qTa_ready"), 2)
        qTb_ready = (sem("qTb_ready"), 2)
        diag_ready = (sem("diag_ready"), 1)
        abc_ready = (sem("abc_ready"), 1)
        qk32_ready = (sem("qk32_ready"), 2 * G)
        parts_ready = (sem("parts_ready"), 2 * G)
        v_ready = (sem("v_ready"), NT)
        stacked = (sem("stacked"), 16 * 24)
        s1_ready = (sem("s1_ready"), 32)
        s1_read = (sem("s1_read"), 32)
        mm_ready = (sem("mm_ready"), G)
        mT_ready = (sem("mT_ready"), G)
        m_stacked = (sem("m_stacked"), 16 * G * HG)
        s2_ready = (sem("s2_ready"), 32)
        p_ready = (sem("p_ready"), 32)
        pv_done = (sem("pv_done"), 16)
        o_normed = (sem("o_normed"), G)
        oTr_ready = (sem("oTr_ready"), 1)
        h1_ready = (sem("h1_ready"), NT)
        x2_ready = (sem("x2_ready"), NT)
        x2p_ready = (sem("x2p_ready"), NT)
        h1_stored = (sem("h1_stored"), 16 * NT)
        x2_stored = (sem("x2_stored"), 16 * NT)

        def until(eng, signal, b, k):
            s, per = signal
            eng.wait_ge(s, b * per + k)
            if eng is nc.gpsimd or eng is nc.sync:
                eng.sem_inc(passed, 1)

        U_XT, U_SELT0, U_EXT0, U_CONV, U_CONVT, U_SELT1, U_EXT1, U_QIT = range(8)
        U_ABC = U_QIT + 2
        U_QKV = U_ABC + 1
        U_M = U_QKV + 12
        U_OQT = U_M + G
        U_PROJ = U_OQT + 2
        DRAINED = {U_XT: (h_ready, 1), U_SELT0: (selT_ready, 1), U_EXT0: (h_ready, 2), U_CONV: (h_ready, 3),
                   U_CONVT: (xs_ready, 2), U_SELT1: (selT_ready, 2), U_EXT1: (h_ready, 4),
                   U_QIT: (qTa_ready, 1), U_QIT + 1: (qTb_ready, 1), U_ABC: (abc_ready, 1),
                   U_OQT: (qTa_ready, 2), U_OQT + 1: (qTb_ready, 2)}
        for i in range(4):
            DRAINED[U_QKV + 3 * i] = (qk32_ready, 2 * i + 1)
            DRAINED[U_QKV + 3 * i + 1] = (qk32_ready, 2 * i + 2)
            DRAINED[U_QKV + 3 * i + 2] = (v_ready, i + 1)
            DRAINED[U_M + i] = (mT_ready, i + 1)
            DRAINED[U_PROJ + i] = (h1_ready, i + 1)
        assert U_PROJ + NT == work_full[1] and sorted(DRAINED) == list(range(work_full[1]))

        def work(u, dt=F32):
            bank = ps_w[:, u % 2, :]
            return bank if dt == F32 else bank.bitcast(dt)

        block = ctx.enter_context(nc.Block())

        @block.sync
        def _(sp):
            for dst, src in ((idx[:, :], ids), (ident[:, :], ident_in), (maskf[:, 0, :], mask_in),
                             (maskf[:, 1, :], maskT_in),
                             (wstage[:, :, 0:3 * C], wqkv.rearrange("(k p) o -> p k o", p=P)),
                             (wstage[:, :, 3 * C:], wproj.rearrange("(k p) o -> p k o", p=P)),
                             (pe_tm[:, :, :], pe_tab.rearrange("(t p) c -> p t c", p=P)),
                             (sp0[:, :], spos0), (sp1[:, :], spos1), (convw[:, :, :], conv_w), (convb[:, :], conv_b)):
                sp.dma_start(dst, src).then_inc(loaded, 16)
            with sp.Fori(0, B) as b:
                until(sp, parts_ready, b, 2 * G)
                until(sp, s2_ready, b, 0)
                for stack, w, order in ((QS, 0, (0, 0, 1)), (KS, 1, (0, 1, 0))):
                    for r, part in enumerate(order):
                        for j in range(HG):
                            sp.dma_start(stack[DH * r:DH * r + DH, :, j, :],
                                         parts[DH * j:DH * j + DH, w, part, :, :]).then_inc(stacked[0], 16)
                for g in range(G):
                    until(sp, mT_ready, b, g + 1)
                    for j in range(HG):
                        sp.dma_start(QS[KPARTS:KPARTS + MROWS, g, j, :],
                                     mT[DH * j:DH * j + MROWS, :]).then_inc(m_stacked[0], 16)
                for r in range(NT):
                    until(sp, h1_ready, b, r + 1)
                    sp.dma_start(h1_dram[bass.ds(b * N + r * P, P), :], h1[:, r, :]).then_inc(h1_stored[0], 16)
                    until(sp, x2p_ready, b, r + 1)
                    sp.dma_start(x2_dram[bass.ds(b * N + r * P, P), :],
                                 x2p[:, r, :, :].rearrange("p a c -> p (a c)")).then_inc(x2_stored[0], 16)
            sp.wait_ge(h1_stored[0], B * h1_stored[1])
            sp.wait_ge(x2_stored[0], B * x2_stored[1])

        @block.gpsimd
        def _(pool):
            nc.gpsimd.memset(neghalf[:, :], -0.5).then_inc(consts_set, 1)
            nc.gpsimd.memset(ones[:, :], 1.0).then_inc(consts_set, 1)
            nc.gpsimd.memset(h[:, :, 0:PAD], 0.0).then_inc(consts_set, 1)
            nc.gpsimd.memset(mm[:, :, :, :], 0.0).then_inc(consts_set, 1)
            pool.wait_ge(consts_set, 4)
            nc.gpsimd.memset(KS[KPARTS:P, :, :, :], MUNIT).then_inc(consts_set, 1)
            pool.wait_ge(consts_set, 5)
            pool.wait_ge(loaded, 16 * 11)
            for t in range(B * NT):
                nc.gpsimd.indirect_dma_start(
                    out=emb_all[:, t, :], out_offset=None, in_=emb,
                    in_offset=bass.IndirectOffsetOnAxis(ap=idx[:, t:t + 1], axis=0)).then_inc(gathered, 16)
            with pool.Fori(0, B) as b:
                step = [0]

                def link(ins):
                    step[0] += 1
                    ins.then_inc(pool_step[0], 1)
                    until(pool, pool_step, b, step[0])

                def rsqrt(use):
                    until(pool, var_ready, b, use + 1)
                    nc.gpsimd.tensor_tensor(rstd[:, :], vare[:, :], neghalf[:, :], ALU.pow).then_inc(rstd_ready[0], 1)

                def to_integers(use):
                    for r in range(NT):
                        until(pool, qf_ready, b, use * NT + r + 1)
                        nc.gpsimd.tensor_scalar(xqi[:, r, :], hc[:, r, :], ROUND, None,
                                                ALU.subtract).then_inc(qi_ready[0], 1)

                rsqrt(0)
                to_integers(0)
                until(pool, stacked, b, 0)
                for n in range(2 * G):
                    g, w = n // 2, n % 2
                    until(pool, qk32_ready, b, n + 1)
                    link(nc.gpsimd.tensor_copy(parts[:, w, 0, g, :], qk32[:, w, :]))
                    nc.gpsimd.tensor_tensor(parts[:, w, 1, g, :], qk32[:, w, :], parts[:, w, 0, g, :],
                                            ALU.subtract).then_inc(parts_ready[0], 1)
                for g in range(G):
                    until(pool, s1_read, b, 8 * g + 8)
                    m = mx[:, g % 2, :, :]
                    link(nc.gpsimd.tensor_scalar(mh[:, :, :], m, -1.0 / (4 * MUNIT), None, ALU.mult))
                    link(nc.gpsimd.tensor_scalar(mr[:, :, :], mh[:, :, :], -4.0 * MUNIT, None, ALU.mult))
                    link(nc.gpsimd.tensor_tensor(mr2[:, :, :], mr[:, :, :], m, ALU.subtract))
                    until(pool, mT_ready, b, g)
                    nc.gpsimd.tensor_scalar(mm[:, :, :, 4], mr2[:, :, :], 1.0 / MUNIT, None, ALU.mult)
                    nc.gpsimd.tensor_copy(mm[:, :, :, 0:4],
                                          mh[:, :, :].unsqueeze(3).to_broadcast([P, NT, HG, 4])).then_inc(mm_ready[0], 1)
                to_integers(1)
                rsqrt(1)
                until(pool, x2_stored, b, 0)
                for r in range(NT):
                    until(pool, x2_ready, b, r + 1)
                    link(nc.gpsimd.tensor_copy(x2p[:, r, 0, :], x2[:, r, :]))
                    nc.gpsimd.tensor_tensor(x2p[:, r, 1, :], x2[:, r, :], x2p[:, r, 0, :],
                                            ALU.subtract).then_inc(x2p_ready[0], 1)
                assert step[0] == pool_step[1], step

        @block.scalar
        def _(act):
            act.wait_ge(consts_set, 5)
            act.wait_ge(loaded, 16 * 11)
            with act.Fori(0, B) as b:
                def full(u):
                    until(act, work_full, b, u + 1)

                until(act, xs_ready, b, 1)
                nc.scalar.activation(ex[:, :, :], xs[:, :, :], ACT.Exp).then_inc(ex_ready[0], 1)
                full(U_XT)
                nc.scalar.copy(h[:, 0, PAD:], work(U_XT)).then_inc(h_ready[0], 1)
                full(U_EXT0)
                nc.scalar.copy(h[:, 1, PAD:], work(U_EXT0)).then_inc(h_ready[0], 1)
                full(U_CONV)
                nc.scalar.activation(h[:, 2, PAD:], work(U_CONV), ACT.Identity,
                                     bias=convb[:, 0:1]).then_inc(h_ready[0], 1)
                until(act, xs_ready, b, 2)
                nc.scalar.activation(ex[:, :, :], xs[:, :, :], ACT.Exp).then_inc(ex_ready[0], 1)
                full(U_EXT1)
                nc.scalar.copy(h[:, 3, PAD:], work(U_EXT1)).then_inc(h_ready[0], 1)
                until(act, var_ready, b, 1)
                for r in range(NT):
                    nc.scalar.activation(hc[:, r, :], h[:, r, PAD:], ACT.Identity,
                                         bias=negmean[:, r:r + 1]).then_inc(hc_ready[0], 1)
                until(act, f_ready, b, 1)
                for r in range(NT):
                    nc.scalar.activation(hc[:, r, :], hc[:, r, :], ACT.Copy, bias=ROUND,
                                         scale=fscale[:, r:r + 1]).then_inc(qf_ready[0], 1)
                full(U_QIT + 1)
                nc.scalar.copy(xqT[:, 2:4, :].rearrange("p k n -> p (k n)"),
                               work(U_QIT + 1, BF16)).then_inc(qTb_ready[0], 1)
                full(U_ABC)
                nc.scalar.copy(abc[:, :], work(U_ABC)).then_inc(abc_ready[0], 1)
                for i in range(NT):
                    full(U_QKV + 3 * i + 2)
                    nc.scalar.activation(V[:, i, :], work(U_QKV + 3 * i + 2), ACT.Copy,
                                         scale=astep[:, i:i + 1]).then_inc(v_ready[0], 1)
                for g in range(G):
                    full(U_M + g)
                    until(act, m_stacked, b, 16 * HG * g)
                    nc.scalar.copy(mT[:, :], work(U_M + g, F16)[:, 0:N]).then_inc(mT_ready[0], 1)
                    for s in range(NT):
                        k = NT * g + s
                        w = N - s * P
                        until(act, pv_done, b, max(k - 1, 0))
                        for pr in range(2):
                            until(act, s2_ready, b, 2 * k + pr + 1)
                            nc.scalar.activation(pT[:, k % 2, 2 * pr:2 * pr + 2, 0:w], ps_s2[:, :, 0:w], ACT.Exp,
                                                 scale=escale[:, 0:1]).then_inc(p_ready[0], 1)
                until(act, f_ready, b, 2)
                for i in range(NT):
                    nc.scalar.activation(hc[:, i, :], (ps_s1, ps_s2)[i // 2][:, i % 2, :], ACT.Copy, bias=ROUND,
                                         scale=fscale[:, i:i + 1]).then_inc(qf_ready[0], 1)
                full(U_OQT + 1)
                nc.scalar.copy(xqT[:, 2:4, :].rearrange("p k n -> p (k n)"),
                               work(U_OQT + 1, BF16)).then_inc(qTb_ready[0], 1)

        @block.vector
        def _(dve):
            nw = [0]

            def wlink(ins):
                nw[0] += 1
                ins.then_inc(w_step, 1)
                dve.wait_ge(w_step, nw[0])

            dve.wait_ge(loaded, 16 * 11)
            nc.vector.tensor_copy(identb[:, :], ident[:, :]).then_inc(idents_cast, 1)
            nc.vector.tensor_copy(identh[:, :], ident[:, :]).then_inc(idents_cast, 1)
            nc.vector.tensor_copy(maskb[:, :, :], maskf[:, :, :]).then_inc(idents_cast, 1)
            cols = (slice(0, 3 * C), slice(3 * C, 4 * C))
            for t in range(2):
                nc.vector.tensor_reduce(wsum[:, t:t + 1], wstage[:, :, cols[t]], axis=mybir.AxisListType.XY,
                                        op=ALU.add, apply_absolute_value=True).then_inc(w_summed, 1)
            dve.wait_ge(w_summed, 3)
            for t in range(2):
                wlink(nc.vector.tensor_scalar(wmean[:, t:t + 1], ps_o[:, t:t + 1],
                                              1.0 / (C * (cols[t].stop - cols[t].start)), CLIP, ALU.mult, ALU.max))
            wlink(nc.vector.reciprocal(winv[:, :], wmean[:, :]))
            wlink(nc.vector.tensor_scalar(escale[:, :], wmean[:, 0:1], wmean[:, 0:1], ATT_SCALE, ALU.mult, ALU.mult))
            for t in range(2):
                w = wstage[:, :, cols[t]]
                wlink(nc.vector.tensor_scalar(w, w, winv[:, t:t + 1], ROUND, ALU.mult, ALU.add))
                wlink(nc.vector.tensor_scalar(w, w, ROUND, 1.0, ALU.subtract, ALU.min))
                nc.vector.tensor_scalar(wq[:, :, cols[t]], w, -1.0, None, ALU.max).then_inc(w_ready, 1)
            dve.wait_ge(gathered, 16 * B * NT)
            dve.wait_ge(consts_set, 5)
            with dve.Fori(0, B) as b:
                step = [0]

                def link(ins):
                    step[0] += 1
                    ins.then_inc(dve_step[0], 1)
                    until(dve, dve_step, b, step[0])

                def full(u):
                    until(dve, work_full, b, u + 1)

                def softmax(use, src, again):
                    link(nc.vector.tensor_reduce(cmax[:, :], src, axis=AX, op=ALU.max))
                    nc.vector.tensor_tensor(xs[:, :, :], src, cmax[:, :].unsqueeze(2).to_broadcast([P, NT, CH]),
                                            ALU.subtract).then_inc(xs_ready[0], 1)
                    until(dve, ex_ready, b, use + 1)
                    link(nc.vector.tensor_reduce(csum[:, :], ex[:, :, :], axis=AX, op=ALU.add))
                    link(nc.vector.reciprocal(crec[:, :], csum[:, :]))
                    if again:
                        until(dve, selT_ready, b, 1)
                    nc.vector.tensor_tensor(sel[:, :, :], ex[:, :, :],
                                            crec[:, :].unsqueeze(2).to_broadcast([P, NT, CH]),
                                            ALU.mult).then_inc(sel_ready[0], 1)
                    u = (U_SELT0, U_SELT1)[use]
                    full(u)
                    nc.vector.tensor_copy(selT[:, :], work(u)).then_inc(selT_ready[0], 1)

                def statistics(rows, signal, use):
                    for r in range(NT):
                        until(dve, signal, b, r + 1)
                        nc.vector.bn_stats(stats[:, r, :], rows[r]).then_inc(dve_step[0], 1)
                        step[0] += 1
                    until(dve, dve_step, b, step[0])
                    dve.sem_inc(passed, 1)
                    for r in range(NT):
                        last = nc.vector.bn_aggr(mv[:, r, :], stats[:, r, :])
                    link(last)
                    nc.vector.tensor_scalar(negmean[:, :], mv[:, :, 0], -1.0, None, ALU.mult)
                    nc.vector.tensor_scalar(vare[:, :], mv[:, :, 1], EPS, None, ALU.add).then_inc(var_ready[0], 1)

                nc.vector.scalar_tensor_tensor(x_tm[:, :, :], emb_all[:, bass.ds(b * NT, NT), :], float(np.sqrt(np.float32(CH))),
                                               pe_tm[:, :, :], ALU.mult, ALU.add).then_inc(x_ready[0], 1)
                until(dve, x_ready, b, 1)
                softmax(0, x_tm[:, :, :], False)
                full(U_CONVT)
                softmax(1, work(U_CONVT).rearrange("p (t c) -> p t c", t=NT), True)
                statistics([h[:, r, PAD:] for r in range(NT)], h_ready, 0)
                for r in range(NT):
                    until(dve, hc_ready, b, r + 1)
                    last = nc.vector.tensor_reduce(amax[:, r:r + 1], hc[:, r, :], axis=AX, op=ALU.max,
                                                   apply_absolute_value=True)
                link(last)
                until(dve, rstd_ready, b, 1)
                link(nc.vector.tensor_tensor(tmp4[:, :], amax[:, :], rstd[:, :], ALU.mult))
                link(nc.vector.tensor_scalar(aval[:, :], tmp4[:, :], CLIP, None, ALU.max))
                link(nc.vector.reciprocal(arec[:, :], aval[:, :]))
                nc.vector.tensor_scalar(astep[:, :], aval[:, :], 1.0 / QMAX, None, ALU.mult)
                nc.vector.scalar_tensor_tensor(fscale[:, :], arec[:, :], QMAX, rstd[:, :], ALU.mult,
                                               ALU.mult).then_inc(f_ready[0], 1)
                until(dve, f_ready, b, 1)
                for r in range(NT):
                    last = nc.vector.tensor_scalar(diag[:, r, :], ident[:, :], astep[:, r:r + 1], None, ALU.mult)
                last.then_inc(diag_ready[0], 1)
                full(U_QIT)
                nc.vector.tensor_copy(xqT[:, 0:2, :].rearrange("p k n -> p (k n)"),
                                      work(U_QIT, BF16)).then_inc(qTa_ready[0], 1)
                until(dve, abc_ready, b, 1)
                for n in range(2 * G):
                    u = U_QKV + 3 * (n // 2) + n % 2
                    full(u)
                    if n >= 2:
                        until(dve, parts_ready, b, n - 1)
                    nc.vector.tensor_tensor(qk32[:, n % 2, :], work(u), abc[:, :],
                                            ALU.mult).then_inc(qk32_ready[0], 1)

                def row_maxima(g, first, last):
                    if first == 0 and g >= 1:
                        until(dve, mm_ready, b, g - 1)
                    for n in range(first, last):
                        i, pr = n // 2, n % 2
                        until(dve, s1_ready, b, 8 * g + n + 1)
                        nc.vector.tensor_reduce(mx[:, g % 2, i, 2 * pr:2 * pr + 2], ps_s1[:, :, 0:(i + 1) * P], axis=AX,
                                                op=ALU.max).then_inc(s1_read[0], 1)

                row_maxima(0, 0, 8)
                for g in range(G):
                    if g + 1 < G:
                        row_maxima(g + 1, 0, 8)
                    until(dve, pv_done, b, NT * (g + 1))
                    link(nc.vector.reciprocal(rden[:, :], ps_den[:, :]))
                    nc.vector.tensor_tensor(oT[:, g, :], ps_o[:, :], rden[:, :], ALU.mult).then_inc(o_normed[0], 1)
                until(dve, oTr_ready, b, 1)
                for k in range(2):
                    last = nc.vector.tensor_reduce(amax[:, 2 * k:2 * k + 2], (ps_s1, ps_s2)[k][:, :, :], axis=AX,
                                                   op=ALU.max, apply_absolute_value=True)
                link(last)
                link(nc.vector.tensor_scalar(aval[:, :], amax[:, :], wmean[:, 0:1], CLIP, ALU.mult, ALU.max))
                link(nc.vector.reciprocal(arec[:, :], aval[:, :]))
                nc.vector.tensor_scalar(astep[:, :], aval[:, :], wmean[:, 1:2], 1.0 / QMAX, ALU.mult, ALU.mult)
                nc.vector.tensor_scalar(fscale[:, :], arec[:, :], wmean[:, 0:1], QMAX, ALU.mult,
                                        ALU.mult).then_inc(f_ready[0], 1)
                until(dve, f_ready, b, 2)
                full(U_OQT)
                nc.vector.tensor_copy(xqT[:, 0:2, :].rearrange("p k n -> p (k n)"),
                                      work(U_OQT, BF16)).then_inc(qTa_ready[0], 1)
                until(dve, h1_stored, b, 0)
                for i in range(NT):
                    full(U_PROJ + i)
                    nc.vector.scalar_tensor_tensor(h1[:, i, :], work(U_PROJ + i), astep[:, i:i + 1], h[:, i, PAD:],
                                                   ALU.mult, ALU.add).then_inc(h1_ready[0], 1)
                statistics([h1[:, r, :] for r in range(NT)], h1_ready, 1)
                until(dve, rstd_ready, b, 2)
                until(dve, x2p_ready, b, 0)
                for r in range(NT):
                    nc.vector.tensor_scalar(x2[:, r, :], h1[:, r, :], mv[:, r, 0:1], rstd[:, r:r + 1],
                                            ALU.subtract, ALU.mult).then_inc(x2_ready[0], 1)
                assert step[0] == dve_step[1], step

        @block.tensor
        def _(pe):
            pe.wait_ge(consts_set, 5)
            pe.wait_ge(idents_cast, 3)
            pe.wait_ge(w_summed, 2)
            nc.tensor.matmul(ps_o[:, 0:2], ones[:, :], wsum[:, :], start=True, stop=True).then_inc(w_summed, 1)
            pe.wait_ge(w_ready, 2)
            with pe.Fori(0, B) as b:
                def bank_free(u):
                    if u < 2:
                        until(pe, h1_ready, b, 0)
                    else:
                        until(pe, DRAINED[u - 2][0], b, DRAINED[u - 2][1])

                def done(ins):
                    ins.then_inc(work_full[0], 1)

                def transposes(u, src):
                    bank_free(u)
                    for t in range(NT):
                        last = nc.tensor.transpose(work(u)[:, t * P:(t + 1) * P], src(t), ident[:, :])
                    done(last)

                until(pe, x_ready, b, 1)
                transposes(U_XT, lambda t: x_tm[:, t, :])
                until(pe, sel_ready, b, 1)
                transposes(U_SELT0, lambda t: sel[:, t, :])
                until(pe, selT_ready, b, 1)
                bank_free(U_EXT0)
                done(nc.tensor.matmul(work(U_EXT0), sp0[:, :], selT[:, :], start=True, stop=True))
                bank_free(U_CONV)
                until(pe, h_ready, b, 1)
                for k in range(TAPS):
                    last = nc.tensor.matmul(work(U_CONV), convw[:, k, :], h[:, 0, k:k + T],
                                            start=(k == 0), stop=(k == TAPS - 1))
                done(last)
                until(pe, h_ready, b, 3)
                transposes(U_CONVT, lambda t: h[:, 2, PAD + t * P:PAD + (t + 1) * P])
                until(pe, sel_ready, b, 2)
                transposes(U_SELT1, lambda t: sel[:, t, :])
                until(pe, selT_ready, b, 2)
                bank_free(U_EXT1)
                done(nc.tensor.matmul(work(U_EXT1), sp1[:, :], selT[:, :], start=True, stop=True))

                def transpose_integers(u0, use):
                    for half in range(2):
                        bank_free(u0 + half)
                        for r in range(NT):
                            if half == 0:
                                until(pe, qi_ready, b, use * NT + r + 1)
                            for kk in range(2):
                                k = 2 * half + kk
                                last = nc.tensor.transpose(work(u0 + half, BF16)[:, kk * N + r * P:kk * N + (r + 1) * P],
                                                           xqi[:, r, k * P:(k + 1) * P], identb[:, :])
                        done(last)

                transpose_integers(U_QIT, 0)
                bank_free(U_ABC)
                until(pe, diag_ready, b, 1)
                for r in range(NT):
                    last = nc.tensor.matmul(work(U_ABC)[:, r * P:(r + 1) * P], ones[:, :], diag[:, r, :],
                                            start=True, stop=True)
                done(last)
                until(pe, qTa_ready, b, 1)
                until(pe, qTb_ready, b, 1)
                for g in range(G):
                    for w in range(3):
                        u = U_QKV + 3 * g + w
                        bank_free(u)
                        for k in range(KT):
                            if w < 2:
                                lhsT, rhs = wq[:, k, w * C + g * P:w * C + (g + 1) * P], xqT[:, k, :]
                            else:
                                lhsT, rhs = xqT[:, k, g * P:(g + 1) * P], wq[:, k, 2 * C:3 * C]
                            last = nc.tensor.matmul(work(u), lhsT, rhs, start=(k == 0), stop=(k == KT - 1))
                        done(last)

                def scores_for_maxima(g):
                    for n in range(8):
                        i, pr = n // 2, n % 2
                        until(pe, s1_read, b, 8 * g + n)
                        for e in range(2):
                            j = 2 * pr + e
                            nc.tensor.matmul(ps_s1[:, e, 0:(i + 1) * P], QS[0:KPARTS, g, j, i * P:(i + 1) * P],
                                             KS[0:KPARTS, g, j, 0:(i + 1) * P], start=True, stop=False)
                            last = nc.tensor.matmul(ps_s1[:, e, i * P:(i + 1) * P], identb[:, :], maskb[:, 0, :],
                                                    start=False, stop=True)
                        last.then_inc(s1_ready[0], 1)

                def maxima_rows(g):
                    u = U_M + g
                    bank_free(u)
                    until(pe, mm_ready, b, g + 1)
                    for i in range(NT):
                        last = nc.tensor.transpose(work(u, F16)[:, i * P:(i + 1) * P],
                                                   mm[:, i, :, :].rearrange("p j r -> p (j r)"), identh[:, :])
                    done(last)

                def scores(g, s):
                    k = NT * g + s
                    w = N - s * P
                    for pr in range(2):
                        until(pe, p_ready, b, 2 * k + pr)
                        for e in range(2):
                            j = 2 * pr + e
                            nc.tensor.matmul(ps_s2[:, e, 0:w], KS[0:KPARTS + MROWS, g, j, s * P:(s + 1) * P],
                                             QS[0:KPARTS + MROWS, g, j, s * P:N], start=True, stop=False)
                            last = nc.tensor.matmul(ps_s2[:, e, 0:P], identb[:, :], maskb[:, 1, :],
                                                    start=False, stop=True)
                        last.then_inc(s2_ready[0], 1)

                def values(g, s):
                    k = NT * g + s
                    w = N - s * P
                    until(pe, p_ready, b, 2 * k + 2)
                    if s == 0:
                        until(pe, o_normed, b, g)
                    for j in range(HG):
                        nc.tensor.matmul(ps_o[DH * j:DH * j + DH, s * P:N],
                                         V[:, s, (HG * g + j) * DH:(HG * g + j + 1) * DH], pT[:, k % 2, j, 0:w],
                                         start=(s == 0), stop=(s == NT - 1))
                    for j in range(HG):
                        last = nc.tensor.matmul(ps_den[DH * j:DH * j + DH, s * P:N], ones[:, 0:DH],
                                                pT[:, k % 2, j, 0:w], start=(s == 0), stop=(s == NT - 1))
                    last.then_inc(pv_done[0], 1)

                until(pe, stacked, b, stacked[1])
                until(pe, qf_ready, b, 0)
                scores_for_maxima(0)
                maxima_rows(0)
                until(pe, v_ready, b, NT)
                for g in range(G):
                    if g + 1 < G:
                        scores_for_maxima(g + 1)
                    until(pe, m_stacked, b, 16 * HG * (g + 1))
                    for s in range(NT):
                        scores(g, s)
                        if s:
                            values(g, s - 1)
                    values(g, NT - 1)
                    if g + 1 < G:
                        maxima_rows(g + 1)
                for i in range(NT):
                    if i == 0:
                        until(pe, s1_read, b, 32)
                        until(pe, p_ready, b, 32)
                    until(pe, o_normed, b, G)
                    for g in range(G):
                        last = nc.tensor.transpose((ps_s1, ps_s2)[i // 2][:, i % 2, g * P:(g + 1) * P],
                                                   oT[:, g, i * P:(i + 1) * P], ident[:, :])
                last.then_inc(oTr_ready[0], 1)
                transpose_integers(U_OQT, 1)
                until(pe, qTa_ready, b, 2)
                until(pe, qTb_ready, b, 2)
                for i in range(NT):
                    bank_free(U_PROJ + i)
                    for k in range(KT):
                        last = nc.tensor.matmul(work(U_PROJ + i), xqT[:, k, i * P:(i + 1) * P], wq[:, k, 3 * C:],
                                                start=(k == 0), stop=(k == KT - 1))
                    done(last)


def ffn_phase(nc, ident_in, tri_in, lanes_in, gate_w, w1, b1, w2, b2, sw1, sb1, sw2, sb2, h1_dram, x2_dram, out):
    TT = B * N // P
    TILES = 2 * TT + E_
    FS = SH // P
    FE = HID // P
    W1N, W2N = KT * 2 * HID, FE * 2 * C
    WROW = (W1N + W2N) // 2 + FE
    TOP = 2.0 ** 10
    base_dram = nc.dram_tensor("base_rows", [B * N, C], F32, kind="Internal").ap()
    y_dram = nc.dram_tensor("expert_rows", [TILES * P, C], F32, kind="Internal").ap()
    ctx = ExitStack()
    with ctx:
        def sb(name, shape, dt):
            return ctx.enter_context(nc.sbuf_tensor(name, shape, dt))

        def sem(name):
            return ctx.enter_context(nc.semaphore(name))

        identf = sb("f_identf", [P, P], F32)
        ident = sb("f_ident", [P, P], F16)
        trif = sb("f_trif", [P, P], F32)
        lanes = sb("f_lanes", [P, P], F32)
        part = sb("f_part", [P, 1], F32)
        ones = sb("f_ones", [P, P], BF16)
        tri = sb("f_tri", [P, P], BF16)
        ew = sb("f_ew", [P, E_, WROW], I32)
        sw1p = sb("f_sw1p", [P, KT, 2, SH], F16)
        sw2p = sb("f_sw2p", [P, FS, 2, C], F16)
        gwp = sb("f_gwp", [P, KT, 2, E_], F16)
        gws = sb("f_gws", [P, KT, E_], F32)
        sb1c = sb("f_sb1c", [P, FS], F32)
        sb2r = sb("f_sb2r", [P, C], F32)
        b2r = sb("f_b2r", [P, E_, C], F32)
        base = sb("f_base", [P, NT, C], F32)
        big = sb("f_big", [P, 8704], F32)
        lo_hot = big[:, 0:4096].bitcast(BF16).rearrange("p (n m) -> p n m", m=P)
        hi_hot = big[:, 4096:8704].bitcast(BF16).rearrange("p (n a m) -> p n a m", a=2, m=TILES)
        wmax = sb("f_wmax", [P, 8], F32)
        wall = sb("f_wall", [P, 8], F32)
        wpow = sb("f_wpow", [P, 8], F32)
        wup = sb("f_wup", [P, 8], F32)
        wdown = sb("f_wdown", [P, 8], F32)
        hb = sb("f_hb", [P, 2], F32)
        hpow = sb("f_hpow", [P, 2], F32)
        hup = sb("f_hup", [P, 2], F32)
        hdn = sb("f_hdn", [P, 2], F32)
        ydn = sb("f_ydn", [P, 2], F32)

        x2t = sb("f_x2t", [P, NT, 2 * C], F16)
        h1t = sb("f_h1t", [P, NT, C], F32)
        xT = sb("f_xT", [P, KT, 2, N], F16)
        act_h = sb("f_act", [P, 2, N], F32)
        gp = sb("f_gp", [P, FS, 2, N], F16)

        L = sb("f_L", [P, TT, E_], F32)
        eqs = sb("f_eqs", [P, TT, E_], F32)
        oh = sb("f_oh", [P, 2, TT, E_], F32)
        L2 = sb("f_L2", [P, TT, E_], F32)
        v12 = sb("f_v12", [P, 2, TT], F32)
        m12 = sb("f_m12", [P, 2, TT], F32)
        dlt = sb("f_dlt", [P, TT], F32)
        exd = sb("f_exd", [P, TT], F32)
        gate = sb("f_gate", [P, 2, TT], F32)
        prior = sb("f_prior", [P, E_], F32)
        both = sb("f_both", [P, TT, E_], BF16)
        pre = sb("f_pre", [P, TT, E_], F32)
        scan = sb("f_scan", [P, 2, TT, E_], F32)
        ntile = sb("f_ntile", [P, E_], F32)
        nt2 = sb("f_nt2", [P, E_], F32)
        tend = sb("f_tend", [P, 2, E_], F32)
        posn = sb("f_posn", [P, TT, E_], F32)
        slot = sb("f_slot", [P, 2, TT], F32)
        hi = sb("f_hi", [P, 2, TT], F32)
        lo = sb("f_lo", [P, 2, TT], F32)
        slot_i = sb("f_slot_i", [P, 2, TT], I32)
        tsel = sb("f_tsel", [P, TILES, E_], F32)
        texp = sb("f_texp", [P, TILES], F32)
        texp_i = sb("f_texp_i", [P, TILES], I32)
        tok_i = sb("f_tok_i", [P, TILES + 2], I32)
        tok_f = sb("f_tok_f", [P, TILES], F32)

        now = sb("f_now", [P, 6], I32)
        xg = sb("f_xg", [P, 2, 2 * C], F16)
        xgT = sb("f_xgT", [P, 2, KT, 2, P], F16)
        wcur = big[:, 0:2 * WROW].bitcast(I32).rearrange("p (z w) -> p z w", z=2)
        ga = sb("f_ga", [P, 2, FE, P], F32)
        gq = sb("f_gq", [P, 2, FE, 2, P], F16)
        yt = big[:, 4608:4608 + 2 * C].rearrange("p (z c) -> p z c", z=2)
        bt = big[:, 5632:5632 + 2 * C].rearrange("p (z c) -> p z c", z=2)
        yg = x2t[:, :, :].rearrange("p i c -> p (i c)").bitcast(F32).rearrange("p (z k c) -> p z k c", z=2, k=2)
        acc = h1t[:, 0:2, :]
        res = h1t[:, 2:4, :]
        PS = ctx.enter_context(nc.psum_tensor("f_ps", [P, 8, 512], F32))

        loaded = sem("f_loaded")
        gated = sem("f_gated")
        set_up = sem("f_set_up")
        cast = sem("f_cast")
        passed = sem("f_passed")
        max_ready = sem("f_max_ready")
        all_max = sem("f_all_max")
        vstep = sem("f_vstep")
        scaled = sem("f_scaled")
        high_ready = sem("f_high_ready")
        stage_free = sem("f_stage_free")
        routed = sem("f_routed")
        route_pe = sem("f_route_pe")
        route_dve = sem("f_route_dve")
        route_act = sem("f_route_act")
        x2_loaded = (sem("f_x2_loaded"), 16)
        h1_loaded = (sem("f_h1_loaded"), 16)
        tr_done = (sem("f_tr_done"), KT)
        xT_even = (sem("f_xT_even"), 2)
        xT_odd = (sem("f_xT_odd"), 2)
        lg_done = (sem("f_lg_done"), 1)
        lg_read = (sem("f_lg_read"), 1)
        up_done = (sem("f_up_done"), FS)
        gelu_done = (sem("f_gelu_done"), FS)
        ghi_done = (sem("f_ghi_done"), FS)
        glo_done = (sem("f_glo_done"), FS)
        down_done = (sem("f_down_done"), NT)
        h1b_done = (sem("f_h1b_done"), NT)
        base_done = (sem("f_base_done"), NT)
        base_stored = (sem("f_base_stored"), 16)
        c_now = (sem("c_now"), 1)
        d_now = (sem("d_now"), 4)
        c_gather = [(sem("c_gather0"), 16), (sem("c_gather1"), 16)]
        c_tr = (sem("c_tr"), 1)
        c_xT = (sem("c_xT"), 1)
        c_w1 = (sem("c_w1"), 1)
        c_w2 = (sem("c_w2"), 1)
        c_up = (sem("c_up"), 1)
        c_gelu = (sem("c_gelu"), 1)
        c_hi = (sem("c_hi"), 1)
        c_lo = (sem("c_lo"), 1)
        c_down = (sem("c_down"), 1)
        c_y = (sem("c_y"), 1)
        c_store = [(sem("c_store0"), 16), (sem("c_store1"), 16)]
        d_gather = [(sem("d_gather0"), 32), (sem("d_gather1"), 32)]
        d_base = [(sem("d_base0"), 16), (sem("d_base1"), 16)]
        d_acc = (sem("d_acc"), 1)
        d_res = (sem("d_res"), 1)
        d_store = [(sem("d_store0"), 16), (sem("d_store1"), 16)]

        def until(eng, signal, b, k):
            s, per = signal
            eng.wait_ge(s, b * per + k)
            if eng is nc.gpsimd or eng is nc.sync:
                eng.sem_inc(passed, 1)

        def weights(row):
            w1v = row[:, 0:W1N // 2].bitcast(F16).rearrange("p (k a n) -> p k a n", k=KT, a=2)
            w2v = row[:, W1N // 2:(W1N + W2N) // 2].bitcast(F16).rearrange("p (f a n) -> p f a n", f=FE, a=2)
            b1v = row[:, (W1N + W2N) // 2:WROW].bitcast(F32)
            return w1v, w2v, b1v

        NLOAD = 5
        block = ctx.enter_context(nc.Block())
        stage = {0: big[:, 0:8192].rearrange("p (e k n) -> p e k n", e=E_, k=KT),
                 1: big[:, 0:8192].rearrange("p (e f n) -> p e f n", e=E_, f=FE),
                 2: big[:, 0:KT * SH].rearrange("p (k n) -> p k n", k=KT),
                 3: big[:, KT * SH:KT * SH + FS * C].rearrange("p (f n) -> p f n", f=FS),
                 4: gws[:, :, :]}

        @block.sync
        def _(sp):
            for dst, src in ((identf[:, :], ident_in), (trif[:, :], tri_in), (lanes[:, :], lanes_in),
                             (gws[:, :, :], gate_w.rearrange("(k p) e -> p k e", p=P)),
                             (sb1c[:, :], sb1), (ew[:, :, WROW - FE:].bitcast(F32), b1),
                             (sb2r[:, :], sb2.rearrange("(a n) -> a n", a=1).to_broadcast([P, C])),
                             (b2r[:, :, :].rearrange("p e n -> p (e n)"),
                              b2.rearrange("(a e) n -> a (e n)", a=1).to_broadcast([P, E_ * C]))):
                sp.dma_start(dst, src).then_inc(loaded, 16)
            for e in range(E_):
                sp.dma_start(stage[0][:, e, :, :], w1[e, :, :].rearrange("(k p) n -> p k n", p=P)).then_inc(gated, 16)
            sp.wait_ge(stage_free, 1)
            for e in range(E_):
                sp.dma_start(stage[1][:, e, :, :], w2[e, :, :].rearrange("(f p) n -> p f n", p=P)).then_inc(gated, 16)
            sp.wait_ge(stage_free, 2)
            sp.dma_start(stage[2], sw1.rearrange("(k p) n -> p k n", p=P)).then_inc(gated, 16)
            sp.dma_start(stage[3], sw2.rearrange("(f p) n -> p f n", p=P)).then_inc(gated, 16)
            with sp.Fori(0, B) as b:
                until(sp, tr_done, b, 0)
                sp.dma_start(x2t[:, :, :],
                             x2_dram[bass.ds(b * N, N), :].rearrange("(i p) c -> p i c", p=P)).then_inc(x2_loaded[0], 16)
                until(sp, base_done, b, 0)
                sp.dma_start(h1t[:, :, :],
                             h1_dram[bass.ds(b * N, N), :].rearrange("(i p) c -> p i c", p=P)).then_inc(h1_loaded[0], 16)
                until(sp, base_done, b, NT)
                sp.dma_start(base_dram[bass.ds(b * N, N), :].rearrange("(i p) c -> p i c", p=P),
                             base[:, :, :]).then_inc(base_stored[0], 16)
            with sp.Fori(0, TILES // 2) as t:
                for z in range(2):
                    until(sp, c_y, 2 * t, z + 1)
                    sp.dma_start(y_dram[bass.ds((2 * t + z) * P, P), :], yt[:, z, :]).then_inc(c_store[z][0], 16)
            sp.wait_ge(base_stored[0], 16 * B)
            with sp.Fori(0, TT // 2) as t:
                for z in range(2):
                    until(sp, d_acc, 2 * t, 0)
                    sp.dma_start(bt[:, z, :], base_dram[bass.ds((2 * t + z) * P, P), :]).then_inc(d_base[z][0], 16)
                for z in range(2):
                    until(sp, d_res, 2 * t, z + 1)
                    sp.dma_start(out[bass.ds((2 * t + z) * P, P), :], res[:, z, :]).then_inc(d_store[z][0], 16)
            for z in range(2):
                sp.wait_ge(c_store[z][0], 16 * TILES // 2)
                sp.wait_ge(d_store[z][0], 16 * TT // 2)

        @block.gpsimd
        def _(pool):
            nc.gpsimd.iota(part[:, :], pattern=[[0, 1]], base=0, channel_multiplier=1,
                           allow_small_or_imprecise_dtypes=True).then_inc(set_up, 1)
            nc.gpsimd.memset(ones[:, :], 1.0).then_inc(set_up, 1)
            nc.gpsimd.memset(tok_i[:, TILES:], 0).then_inc(set_up, 1)
            for k, (c0, c1) in enumerate(((0, 1), (1, 2), (2, 7))):
                pool.wait_ge(max_ready, k + 1)
                nc.gpsimd.partition_all_reduce(wall[:, c0:c1], wmax[:, c0:c1], P,
                                               bass.bass_isa.ReduceOp.max).then_inc(all_max, 1)
            pool.wait_ge(loaded, 16 * 8)
            pool.wait_ge(route_dve, 1)
            with pool.Fori(0, B) as b:
                until(pool, h1_loaded, b, 16)
                for f in range(FS):
                    nc.gpsimd.tensor_tensor(h1t[:, f, :], h1t[:, f, :], sb2r[:, :], ALU.add).then_inc(h1b_done[0], 1)
                    until(pool, gelu_done, b, f + 1)
                    nc.gpsimd.tensor_scalar(gp[:, f, 0, :], act_h[:, f % 2, :], hup[:, 1:2], None,
                                            ALU.mult).then_inc(ghi_done[0], 1)

            def gather(t, z):
                nc.gpsimd.tensor_copy(now[:, z:z + 1], tok_i[:, bass.ds(2 * t + z, 1)]).then_inc(c_now[0], 1)
                until(pool, c_now, 2 * t, z + 1)
                nc.gpsimd.indirect_dma_start(
                    out=xg[:, z, :], out_offset=None, in_=x2_dram,
                    in_offset=bass.IndirectOffsetOnAxis(ap=now[:, z:z + 1], axis=0)).then_inc(c_gather[z][0], 16)

            pool.wait_ge(set_up, 3)
            pool.wait_ge(routed, 2)
            gather(0, 0)
            gather(0, 1)
            with pool.Fori(0, TILES // 2) as t:
                for z in range(2):
                    until(pool, c_gelu, 2 * t, z + 1)
                    nc.gpsimd.tensor_scalar(gq[:, z, :, 0, :], ga[:, z, :, :], hup[:, 0:1], None,
                                            ALU.mult).then_inc(c_hi[0], 1)
                    until(pool, c_tr, 2 * t, z + 1)
                    gather(t + 1, z)
            for z in range(2):
                pool.wait_ge(c_store[z][0], 16 * TILES // 2)
            with pool.Fori(0, TT // 2) as t:
                for z in range(2):
                    until(pool, d_res, 2 * t, 0)
                    for k in range(2):
                        nc.gpsimd.tensor_copy(now[:, 2 + 2 * z + k:3 + 2 * z + k],
                                              slot_i[:, k, bass.ds(2 * t + z, 1)]).then_inc(d_now[0], 1)
                    until(pool, d_now, t, 2 * z + 2)
                    for k in range(2):
                        nc.gpsimd.indirect_dma_start(
                            out=yg[:, z, k, :], out_offset=None, in_=y_dram,
                            in_offset=bass.IndirectOffsetOnAxis(ap=now[:, 2 + 2 * z + k:3 + 2 * z + k], axis=0)
                        ).then_inc(d_gather[z][0], 16)
            for z in range(2):
                pool.wait_ge(c_gather[z][0], 16 * (TILES // 2 + 1))

        @block.scalar
        def _(act):
            act.wait_ge(scaled, 1)
            for e in range(E_):
                nc.scalar.activation(weights(ew[:, e, :])[0][:, :, 0, :], stage[0][:, e, :, :], ACT.Copy,
                                     scale=wup[:, 0:1]).then_inc(high_ready, 1)
            act.wait_ge(scaled, 2)
            for e in range(E_):
                nc.scalar.activation(weights(ew[:, e, :])[1][:, :, 0, :], stage[1][:, e, :, :], ACT.Copy,
                                     scale=wup[:, 1:2]).then_inc(high_ready, 1)
            act.wait_ge(scaled, 3)
            for dst, src, col in ((sw1p[:, :, 0, :], stage[2], 2), (sw2p[:, :, 0, :], stage[3], 3), (gwp[:, :, 0, :], stage[4], 4)):
                nc.scalar.activation(dst, src, ACT.Copy, scale=wup[:, col:col + 1]).then_inc(high_ready, 1)
            act.wait_ge(loaded, 16 * 8)
            with act.Fori(0, B) as b:
                for k in (0, 2):
                    until(act, tr_done, b, k + 1)
                    nc.scalar.copy(xT[:, k, :, :].rearrange("p a n -> p (a n)"),
                                   PS[:, k, :].bitcast(F16)).then_inc(xT_even[0], 1)
                for f in range(FS):
                    until(act, up_done, b, f + 1)
                    if f >= 2:
                        until(act, glo_done, b, f - 1)
                    nc.scalar.activation(act_h[:, f % 2, :], PS[:, 4 + f % 2, :], ACT.Gelu, bias=sb1c[:, f:f + 1],
                                         scale=wdown[:, 2:3]).then_inc(gelu_done[0], 1)
            act.wait_ge(routed, 1)
            nc.scalar.activation(exd[:, :], dlt[:, :], ACT.Exp).then_inc(route_act, 1)

            def rows_out(t, z):
                until(act, c_tr, 2 * t, z + 1)
                nc.scalar.copy(xgT[:, z, :, :, :].rearrange("p k a n -> p (k a n)"),
                               PS[:, z, :].bitcast(F16)).then_inc(c_xT[0], 1)

            def gelus(t, z):
                expert = act.value_load(texp_i[0:1, bass.ds(2 * t + z, 1)], min_val=0, max_val=E_ - 1)
                until(act, c_up, 2 * t, z + 1)
                for f in range(FE):
                    last = nc.scalar.activation(ga[:, z, f, :], PS[:, 2 + z, f * P:(f + 1) * P], ACT.Gelu,
                                                bias=ew[:, bass.ds(expert, 1), WROW - FE + f].bitcast(F32),
                                                scale=wdown[:, 0:1])
                last.then_inc(c_gelu[0], 1)

            act.wait_ge(routed, 2)
            rows_out(0, 0)
            rows_out(0, 1)
            gelus(0, 0)
            with act.Fori(0, TILES // 2 - 1) as t:
                rows_out(t + 1, 0)
                gelus(t, 1)
                rows_out(t + 1, 1)
                gelus(t + 1, 0)
            gelus(TILES // 2 - 1, 1)

        @block.vector
        def _(dve):
            n = [0]

            def link(ins):
                n[0] += 1
                ins.then_inc(vstep, 1)
                dve.wait_ge(vstep, n[0])

            def powers(src, pw):
                link(nc.vector.tensor_scalar(pw, src, 2.0 ** -100, None, ALU.max))
                link(nc.vector.tensor_scalar(pw.bitcast(I32), pw.bitcast(I32), 0x7F800000, None, ALU.bitwise_and))

            def scales(k, c0, c1):
                dve.wait_ge(all_max, k)
                powers(wall[:, c0:c1], wpow[:, c0:c1])
                link(nc.vector.reciprocal(wup[:, c0:c1], wpow[:, c0:c1]))
                link(nc.vector.tensor_scalar(wup[:, c0:c1], wup[:, c0:c1], TOP, None, ALU.mult))
                nc.vector.tensor_scalar(wdown[:, c0:c1], wpow[:, c0:c1], 1.0 / TOP, None, ALU.mult).then_inc(scaled, 1)

            def largest(src, col, axis=mybir.AxisListType.XY):
                return nc.vector.tensor_reduce(wmax[:, col:col + 1], src, axis=axis, op=ALU.max, apply_absolute_value=True)

            dve.wait_ge(loaded, 16 * 8)
            nc.vector.tensor_copy(ident[:, :], identf[:, :])
            nc.vector.tensor_copy(tri[:, :], trif[:, :]).then_inc(cast, 1)
            for k in range(2):
                dve.wait_ge(gated, 16 * E_ * (k + 1))
                largest(big[:, 0:8192], k, AX).then_inc(max_ready, 1)
                scales(k + 1, k, k + 1)
                for e in range(E_):
                    dve.wait_ge(high_ready, k * E_ + e + 1)
                    w = weights(ew[:, e, :])[k]
                    last = nc.vector.scalar_tensor_tensor(w[:, :, 1, :], stage[k][:, e, :, :], wup[:, k:k + 1],
                                                          w[:, :, 0, :], ALU.mult, ALU.subtract)
                last.then_inc(stage_free, 1)
            dve.wait_ge(gated, 16 * (2 * E_ + 2))
            largest(stage[2], 2)
            largest(stage[3], 3)
            largest(stage[4], 4)
            largest(ew[:, :, WROW - FE:WROW].bitcast(F32), 5)
            largest(sb1c[:, :], 6, AX).then_inc(max_ready, 1)
            scales(3, 2, 7)
            for col, (dst, src) in ((2, (sw1p, stage[2])), (3, (sw2p, stage[3])), (4, (gwp, stage[4]))):
                dve.wait_ge(high_ready, 2 * E_ + col - 1)
                last = nc.vector.scalar_tensor_tensor(dst[:, :, 1, :], src, wup[:, col:col + 1], dst[:, :, 0, :],
                                                      ALU.mult, ALU.subtract)
            last.then_inc(stage_free, 1)
            link(nc.vector.scalar_tensor_tensor(hb[:, 0:1], wall[:, 0:1], float(C), wall[:, 5:6], ALU.mult, ALU.add))
            link(nc.vector.scalar_tensor_tensor(hb[:, 1:2], wall[:, 2:3], float(C), wall[:, 6:7], ALU.mult, ALU.add))
            powers(hb[:, :], hpow[:, :])
            link(nc.vector.reciprocal(hup[:, :], hpow[:, :]))
            link(nc.vector.tensor_scalar(hup[:, :], hup[:, :], 2.0 ** 14, None, ALU.mult))
            link(nc.vector.tensor_scalar(hdn[:, :], hpow[:, :], 2.0 ** -14, None, ALU.mult))
            link(nc.vector.tensor_tensor(ydn[:, 0:1], hdn[:, 0:1], wdown[:, 1:2], ALU.mult))
            nc.vector.tensor_tensor(ydn[:, 1:2], hdn[:, 1:2], wdown[:, 3:4], ALU.mult).then_inc(route_dve, 1)
            dve.wait_ge(route_dve, 1)

            with dve.Fori(0, B) as b:
                for k in (1, 3):
                    until(dve, tr_done, b, k + 1)
                    nc.vector.tensor_copy(xT[:, k, :, :].rearrange("p a n -> p (a n)"),
                                          PS[:, k, :].bitcast(F16)).then_inc(xT_odd[0], 1)
                until(dve, lg_done, b, 1)
                nc.vector.tensor_scalar(L[:, bass.ds(b * NT, NT), :], PS[:, 5, 0:NT * E_].rearrange("p (i e) -> p i e", e=E_),
                                        wdown[:, 4:5], None, ALU.mult).then_inc(lg_read[0], 1)
                for f in range(FS):
                    until(dve, ghi_done, b, f + 1)
                    nc.vector.scalar_tensor_tensor(gp[:, f, 1, :], act_h[:, f % 2, :], hup[:, 1:2], gp[:, f, 0, :],
                                                   ALU.mult, ALU.subtract).then_inc(glo_done[0], 1)
                until(dve, base_stored, b, 0)
                for i in range(NT):
                    until(dve, down_done, b, i + 1)
                    until(dve, h1b_done, b, i + 1)
                    nc.vector.scalar_tensor_tensor(base[:, i, :], PS[:, 6 + i % 2, :], ydn[:, 1:2], h1t[:, i, :],
                                                   ALU.mult, ALU.add).then_inc(base_done[0], 1)
            dve.wait_ge(lg_read[0], B)
            dve.wait_ge(set_up, 3)
            def bc(ap):
                return ap.unsqueeze(2).to_broadcast([P, TT, E_])

            for e in range(E_):
                nc.vector.memset(prior[:, e:e + 1], float(E_ - e)).then_inc(vstep, 1)
            n[0] += E_
            dve.wait_ge(vstep, n[0])
            pr = prior[:, :].unsqueeze(1).to_broadcast([P, TT, E_])
            for k, src in enumerate((L, L2)):
                link(nc.vector.tensor_reduce(v12[:, k, :], src[:, :, :], axis=AX, op=ALU.max))
                link(nc.vector.tensor_tensor(eqs[:, :, :], src[:, :, :], bc(v12[:, k, :]), ALU.is_equal))
                link(nc.vector.tensor_tensor(eqs[:, :, :], eqs[:, :, :], pr, ALU.mult))
                link(nc.vector.tensor_reduce(m12[:, k, :], eqs[:, :, :], axis=AX, op=ALU.max))
                link(nc.vector.tensor_tensor(oh[:, k, :, :], eqs[:, :, :], bc(m12[:, k, :]), ALU.is_equal))
                if k == 0:
                    link(nc.vector.scalar_tensor_tensor(L2[:, :, :], oh[:, 0, :, :], MASKED, L[:, :, :], ALU.mult, ALU.add))
            nc.vector.tensor_tensor(dlt[:, :], v12[:, 1, :], v12[:, 0, :], ALU.subtract).then_inc(routed, 1)
            nc.vector.tensor_tensor(both[:, :, :], oh[:, 0, :, :], oh[:, 1, :, :], ALU.add).then_inc(route_dve, 1)
            dve.wait_ge(route_pe, 1)
            link(nc.vector.tensor_copy(pre[:, :, :], PS[:, 0, 0:TT * E_].rearrange("p (t e) -> p t e", e=E_)))
            link(nc.vector.tensor_copy(scan[:, 0, :, :], PS[:, 1, 0:TT * E_].rearrange("p (t e) -> p t e", e=E_)))
            link(nc.vector.tensor_tensor(pre[:, :, :], pre[:, :, :], scan[:, 0, :, :], ALU.subtract))
            cur, d = 0, 1
            while d < TT:
                nc.vector.tensor_copy(scan[:, 1 - cur, 0:d, :], scan[:, cur, 0:d, :])
                link(nc.vector.tensor_tensor(scan[:, 1 - cur, d:, :], scan[:, cur, d:, :], scan[:, cur, 0:TT - d, :], ALU.add))
                cur, d = 1 - cur, 2 * d
            link(nc.vector.tensor_scalar(ntile[:, :], scan[:, cur, TT - 1, :], 1.0 / P, (P - 1.0) / P - 0.5 + 0.5 / P, ALU.mult, ALU.add))
            link(nc.vector.tensor_scalar(nt2[:, :], ntile[:, :], ROUND, ROUND, ALU.add, ALU.subtract))
            link(nc.vector.tensor_copy(tend[:, 0, :], nt2[:, :]))
            tc, d = 0, 1
            while d < E_:
                nc.vector.tensor_copy(tend[:, 1 - tc, 0:d], tend[:, tc, 0:d])
                link(nc.vector.tensor_tensor(tend[:, 1 - tc, d:], tend[:, tc, d:], tend[:, tc, 0:E_ - d], ALU.add))
                tc, d = 1 - tc, 2 * d
            link(nc.vector.tensor_tensor(ntile[:, :], tend[:, tc, :], nt2[:, :], ALU.subtract))
            link(nc.vector.tensor_tensor(posn[:, :, :], pre[:, :, :], scan[:, cur, :, :], ALU.add))
            link(nc.vector.scalar_tensor_tensor(posn[:, :, :], ntile[:, :].unsqueeze(1).to_broadcast([P, TT, E_]), float(P),
                                                posn[:, :, :], ALU.mult, ALU.add))
            for k in range(2):
                link(nc.vector.tensor_tensor(eqs[:, :, :], oh[:, k, :, :], posn[:, :, :], ALU.mult))
                link(nc.vector.tensor_reduce(slot[:, k, :], eqs[:, :, :], axis=AX, op=ALU.add))
            link(nc.vector.tensor_copy(slot_i[:, :, :], slot[:, :, :]))
            link(nc.vector.tensor_scalar(hi[:, :, :], slot[:, :, :], 1.0 / P, 0.5 / P - 0.5, ALU.mult, ALU.add))
            link(nc.vector.tensor_scalar(hi[:, :, :], hi[:, :, :], ROUND, ROUND, ALU.add, ALU.subtract))
            link(nc.vector.scalar_tensor_tensor(lo[:, :, :], hi[:, :, :], -float(P), slot[:, :, :], ALU.mult, ALU.add))
            K2 = 2 * TT
            link(nc.vector.tensor_tensor(lo_hot, lanes[:, :].unsqueeze(1).to_broadcast([P, K2, P]),
                                         lo[:, :, :].rearrange("p k t -> p (k t)").unsqueeze(2).to_broadcast([P, K2, P]), ALU.is_equal))
            link(nc.vector.tensor_tensor(hi_hot[:, :, 1, :], lanes[:, 0:TILES].unsqueeze(1).to_broadcast([P, K2, TILES]),
                                         hi[:, :, :].rearrange("p k t -> p (k t)").unsqueeze(2).to_broadcast([P, K2, TILES]), ALU.is_equal))
            link(nc.vector.tensor_scalar(hi_hot[:, :, 0, :], hi_hot[:, :, 1, :], part[:, 0:1], None, ALU.mult))
            for k in range(2):
                half = hi_hot[:, k * TT:(k + 1) * TT, 1, :]
                last = nc.vector.tensor_tensor(half, half, lanes[:, 0:TT].unsqueeze(2).to_broadcast([P, TT, TILES]), ALU.mult)
            last.then_inc(route_dve, 1)
            link(nc.vector.tensor_tensor(tsel[:, :, 0:E_ - 1], lanes[:, 0:TILES].unsqueeze(2).to_broadcast([P, TILES, E_ - 1]),
                                         tend[:, tc, 0:E_ - 1].unsqueeze(1).to_broadcast([P, TILES, E_ - 1]), ALU.is_ge))
            link(nc.vector.tensor_reduce(texp[:, :], tsel[:, :, 0:E_ - 1], axis=AX, op=ALU.add))
            link(nc.vector.tensor_copy(texp_i[:, :], texp[:, :]))
            dve.wait_ge(route_pe, 2)
            link(nc.vector.tensor_copy(tok_f[:, :], PS[:, 2, 0:TILES]))
            link(nc.vector.scalar_tensor_tensor(tok_f[:, :], PS[:, 2, TILES:2 * TILES], float(P), tok_f[:, :], ALU.mult, ALU.add))
            nc.vector.tensor_copy(tok_i[:, 0:TILES], tok_f[:, :]).then_inc(routed, 1)
            dve.wait_ge(route_act, 1)
            link(nc.vector.tensor_scalar(gate[:, 0, :], exd[:, :], 1.0, None, ALU.add))
            link(nc.vector.reciprocal(gate[:, 0, :], gate[:, 0, :]))
            link(nc.vector.tensor_tensor(gate[:, 1, :], exd[:, :], gate[:, 0, :], ALU.mult))
            dve.wait_ge(routed, 2)

            def load_w(t, z, which, used, n, k):
                expert = dve.value_load(texp_i[0:1, bass.ds(2 * t + z, 1)], min_val=0, max_val=E_ - 1)
                a, c = ((0, W1N // 2), (W1N // 2, (W1N + W2N) // 2))[which]
                if used is not None:
                    until(dve, used, n, k)
                nc.vector.tensor_copy(wcur[:, z, a:c], ew[:, bass.ds(expert, 1), a:c].rearrange("p o w -> p (o w)")
                                      ).then_inc((c_w1, c_w2)[which][0], 1)

            def low(t, z):
                until(dve, c_hi, 2 * t, z + 1)
                nc.vector.scalar_tensor_tensor(gq[:, z, :, 1, :], ga[:, z, :, :], hup[:, 0:1], gq[:, z, :, 0, :],
                                               ALU.mult, ALU.subtract).then_inc(c_lo[0], 1)

            def rows(t, z):
                expert = dve.value_load(texp_i[0:1, bass.ds(2 * t + z, 1)], min_val=0, max_val=E_ - 1)
                until(dve, c_down, 2 * t, z + 1)
                until(dve, c_store[z], t, 0)
                nc.vector.scalar_tensor_tensor(yt[:, z, :], PS[:, 4 + z, :], ydn[:, 0:1],
                                               b2r[:, bass.ds(expert, 1), :].rearrange("p o n -> p (o n)"),
                                               ALU.mult, ALU.add).then_inc(c_y[0], 1)

            for z in range(2):
                for which in range(2):
                    load_w(0, z, which, None, 0, 0)
            low(0, 0)
            with dve.Fori(0, TILES // 2 - 1) as t:
                load_w(t + 1, 0, 0, c_up, 2 * t, 1)
                low(t, 1)
                rows(t, 0)
                load_w(t + 1, 0, 1, c_down, 2 * t, 1)
                load_w(t + 1, 1, 0, c_up, 2 * t, 2)
                low(t + 1, 0)
                rows(t, 1)
                load_w(t + 1, 1, 1, c_down, 2 * t, 2)
            low(TILES // 2 - 1, 1)
            rows(TILES // 2 - 1, 0)
            rows(TILES // 2 - 1, 1)

            with dve.Fori(0, TT // 2) as t:
                for z in range(2):
                    until(dve, d_gather[z], t, 32)
                    until(dve, d_base[z], t, 16)
                    nc.vector.scalar_tensor_tensor(acc[:, z, :], yg[:, z, 0, :], gate[:, 0, bass.ds(2 * t + z, 1)],
                                                   bt[:, z, :], ALU.mult, ALU.add).then_inc(d_acc[0], 1)
                    until(dve, d_acc, 2 * t, z + 1)
                    until(dve, d_store[z], t, 0)
                    nc.vector.scalar_tensor_tensor(res[:, z, :], yg[:, z, 1, :], gate[:, 1, bass.ds(2 * t + z, 1)],
                                                   acc[:, z, :], ALU.mult, ALU.add).then_inc(d_res[0], 1)

        @block.tensor
        def _(pe):
            PAIRS = ((0, 0), (0, 1), (1, 0))
            pe.wait_ge(set_up, 3)
            pe.wait_ge(cast, 1)
            pe.wait_ge(stage_free, 3)
            with pe.Fori(0, B) as b:
                until(pe, x2_loaded, b, 16)
                for k in range(KT):
                    for i in range(NT):
                        for a in range(2):
                            last = nc.tensor.transpose(PS[:, k, :].bitcast(F16)[:, a * N + i * P:a * N + (i + 1) * P],
                                                       x2t[:, i, a * C + k * P:a * C + (k + 1) * P], ident[:, :])
                    last.then_inc(tr_done[0], 1)
                until(pe, xT_even, b, 2)
                until(pe, xT_odd, b, 2)
                until(pe, gelu_done, b, 0)
                for i in range(NT):
                    m = 0
                    for k in range(KT):
                        for xa, wa in PAIRS:
                            last = nc.tensor.matmul(PS[:, 5, i * E_:(i + 1) * E_], xT[:, k, xa, i * P:(i + 1) * P],
                                                    gwp[:, k, wa, :], start=(m == 0), stop=(m == 3 * KT - 1))
                            m += 1
                last.then_inc(lg_done[0], 1)
                for f in range(FS):
                    if f == 1:
                        until(pe, lg_read, b, 1)
                    if f >= 2:
                        until(pe, gelu_done, b, f - 1)
                    m = 0
                    for k in range(KT):
                        for xa, wa in PAIRS:
                            last = nc.tensor.matmul(PS[:, 4 + f % 2, :], sw1p[:, k, wa, f * P:(f + 1) * P], xT[:, k, xa, :],
                                                    start=(m == 0), stop=(m == 3 * KT - 1))
                            m += 1
                    last.then_inc(up_done[0], 1)
                until(pe, glo_done, b, FS)
                for i in range(NT):
                    if i < 2:
                        until(pe, base_done, b, 0)
                    else:
                        until(pe, base_done, b, i - 1)
                    m = 0
                    for f in range(FS):
                        for ga_, wa in PAIRS:
                            last = nc.tensor.matmul(PS[:, 6 + i % 2, :], gp[:, f, ga_, i * P:(i + 1) * P], sw2p[:, f, wa, :],
                                                    start=(m == 0), stop=(m == 3 * FS - 1))
                            m += 1
                    last.then_inc(down_done[0], 1)
            pe.wait_ge(route_dve, 2)
            te = both[:, :, :].rearrange("p t e -> p (t e)")
            nc.tensor.matmul(PS[:, 0, 0:TT * E_], tri[:, :], te, start=True, stop=True)
            nc.tensor.matmul(PS[:, 1, 0:TT * E_], ones[:, :], te, start=True, stop=True).then_inc(route_pe, 1)
            pe.wait_ge(route_dve, 3)
            for m in range(2 * TT):
                last = nc.tensor.matmul(PS[:, 2, 0:2 * TILES], lo_hot[:, m, :], hi_hot[:, m, :, :].rearrange("p a m -> p (a m)"),
                                        start=(m == 0), stop=(m == 2 * TT - 1))
            last.then_inc(route_pe, 1)
            pe.wait_ge(routed, 2)

            def turn(t, z):
                until(pe, c_gather[z], t, 16)
                for k in range(KT):
                    for a in range(2):
                        q = (2 * k + a) * P
                        last = nc.tensor.transpose(PS[:, z, :].bitcast(F16)[:, q:q + P],
                                                   xg[:, z, a * C + k * P:a * C + (k + 1) * P], ident[:, :])
                last.then_inc(c_tr[0], 1)

            def up(t, z):
                w1v = weights(wcur[:, z, :])[0]
                until(pe, c_xT, 2 * t, z + 1)
                until(pe, c_w1, 2 * t, z + 1)
                for f in range(FE):
                    m = 0
                    for k in range(KT):
                        for xa, wa in PAIRS:
                            last = nc.tensor.matmul(PS[:, 2 + z, f * P:(f + 1) * P], w1v[:, k, wa, f * P:(f + 1) * P],
                                                    xgT[:, z, k, xa, :], start=(m == 0), stop=(m == 3 * KT - 1))
                            m += 1
                last.then_inc(c_up[0], 1)

            def down(t, z):
                w2v = weights(wcur[:, z, :])[1]
                until(pe, c_lo, 2 * t, z + 1)
                until(pe, c_w2, 2 * t, z + 1)
                m = 0
                for f in range(FE):
                    for ga_, wa in PAIRS:
                        last = nc.tensor.matmul(PS[:, 4 + z, :], gq[:, z, f, ga_, :], w2v[:, f, wa, :],
                                                start=(m == 0), stop=(m == 3 * FE - 1))
                        m += 1
                last.then_inc(c_down[0], 1)

            T_LAST = TILES // 2 - 1
            turn(0, 0)
            turn(0, 1)
            up(0, 0)
            with pe.Fori(0, T_LAST) as t:
                turn(t + 1, 0)
                up(t, 1)
                down(t, 0)
                turn(t + 1, 1)
                up(t + 1, 0)
                down(t, 1)
            up(T_LAST, 1)
            down(T_LAST, 0)
            down(T_LAST, 1)


def kernel(**inputs):
    import numpy as _np
    import concourse.bacc as _bacc
    from concourse import mybir as _mybir
    from concourse.bass_utils import run_bass_kernel_spmd as _run

    t = {k.replace("L0_", ""): _np.asarray(v) for k, v in inputs.items()}
    depth = CH // 2
    pos = _np.arange(T, dtype=_np.float32)[:, None]
    rate = (1.0 / _np.power(_np.float32(10000.0), _np.arange(depth, dtype=_np.float32)[None, :] / _np.float32(depth))).astype(_np.float32)
    ang = (pos * rate).astype(_np.float32)
    tri = _np.triu(_np.ones((P, P), _np.float32), 1) * _np.float32(MASKED)
    arrays = {
        "ids": t["x"].reshape(B * NT, P).T,
        "emb": t["tok_emb_table"],
        "pe_tab": _np.concatenate([_np.sin(ang), _np.cos(ang)], axis=1).astype(_np.float32),
        "conv_w": t["tok_conv_w"].transpose(1, 2, 0),
        "conv_b": t["tok_conv_b"].reshape(CH, 1),
        "spos0": t["tok_spos0"],
        "spos1": t["tok_spos1"],
        "wqkv": t["attn_w_qkv"].T,
        "wproj": t["attn_w_proj"].T,
        "gate_w": t["ffn_gate_w"],
        "w1": t["ffn_w1"],
        "b1": t["ffn_b1"].reshape(E_, HID // P, P).transpose(2, 0, 1),
        "w2": t["ffn_w2"],
        "b2": t["ffn_b2"],
        "sw1": t["ffn_shared_w1"],
        "sb1": t["ffn_shared_b1"].reshape(SH // P, P).T,
        "sw2": t["ffn_shared_w2"],
        "sb2": t["ffn_shared_b2"],
        "ident_in": _np.eye(P, dtype=_np.float32),
        "mask_in": tri,
        "maskT_in": tri.T,
        "tri_in": _np.triu(_np.ones((P, P), _np.float32), 1),
        "lanes_in": _np.tile(_np.arange(P, dtype=_np.float32), (P, 1)),
    }
    nc = _bacc.Bacc("TRN2", target_bir_lowering=False, num_devices=1)
    sent, args = {}, []
    for name, a in arrays.items():
        a = _np.ascontiguousarray(a)
        sent[f"in_{name}"] = a
        args.append(nc.dram_tensor(f"in_{name}", a.shape, _mybir.dt.from_np(a.dtype), kind="ExternalInput").ap())
    args.append(nc.dram_tensor("out_h", (B * N, C), _mybir.dt.float32, kind="ExternalOutput").ap())
    build(nc, *args)
    r = _run(nc, [sent], core_ids=[0])
    return r.results[0]["out_h"].reshape(B, N, C)
```

```python
from contextlib import ExitStack

import numpy as np

import concourse.bass as bass
from concourse import mybir

P = 128
ALU = mybir.AluOpType
ACT = mybir.ActivationFunctionType
AX = mybir.AxisListType.X
F32 = mybir.dt.float32
F16 = mybir.dt.float16
BF16 = mybir.dt.bfloat16
I32 = mybir.dt.int32

B, T = 8, 512
CH = 128
N = 4 * CH
C = T
H, DH = 16, 32
NT, KT = N // P, C // P
G, HG = 4, 4
E_, HID = 8, 256
SH = 512
TAPS = 3
PAD = TAPS - 1
EPS = 1e-5
QMAX = 127.0
CLIP = 1e-5
ROUND = 1.5 * 2.0 ** 23
MASKED = -(2.0 ** 100)
ATT_SCALE = DH ** -0.5
KPARTS = 3 * DH
MROWS = 5
MUNIT = 2.0 ** 15


def build(nc, ids, emb, pe_tab, conv_w, conv_b, spos0, spos1, wqkv, wproj, gate_w, w1, b1, w2, b2,
          sw1, sb1, sw2, sb2, ident_in, mask_in, maskT_in, tri_in, lanes_in, out):
    h1_dram = nc.dram_tensor("h1_rows", [B * N, C], F32, kind="Internal").ap()
    x2_dram = nc.dram_tensor("x2_rows", [B * N, 2 * C], F16, kind="Internal").ap()
    attention_phase(nc, ids, emb, pe_tab, conv_w, conv_b, spos0, spos1, wqkv, wproj,
                    ident_in, mask_in, maskT_in, h1_dram, x2_dram)
    ffn_phase(nc, ident_in, tri_in, lanes_in, gate_w, w1, b1, w2, b2, sw1, sb1, sw2, sb2, h1_dram, x2_dram, out)


def attention_phase(nc, ids, emb, pe_tab, conv_w, conv_b, spos0, spos1, wqkv, wproj,
                    ident_in, mask_in, maskT_in, h1_dram, x2_dram):
    ctx = ExitStack()
    with ctx:
        def sb(name, shape, dt):
            return ctx.enter_context(nc.sbuf_tensor(name, shape, dt))

        def ps(name, shape, dt):
            return ctx.enter_context(nc.psum_tensor(name, shape, dt))

        def sem(name):
            return ctx.enter_context(nc.semaphore(name))

        idx = sb("idx", [P, B * NT], I32)
        emb_all = sb("emb_all", [P, B * NT, CH], F32)
        pe_tm = sb("pe_tm", [P, NT, CH], F32)
        convw = sb("convw", [P, TAPS, CH], F32)
        convb = sb("convb", [P, 1], F32)
        sp0 = sb("sp0", [P, CH], F32)
        sp1 = sb("sp1", [P, CH], F32)
        ident = sb("ident", [P, P], F32)
        identb = sb("identb", [P, P], BF16)
        identh = sb("identh", [P, P], F16)
        maskf = sb("maskf", [P, 2, P], F32)
        maskb = sb("maskb", [P, 2, P], BF16)
        ones = sb("ones", [P, P], F32)
        neghalf = sb("neghalf", [P, NT], F32)
        wstage = sb("wstage", [P, KT, 4 * C], F32)
        wq = sb("wq", [P, KT, 4 * C], BF16)
        wsum = sb("wsum", [P, 2], F32)
        wmean = sb("wmean", [P, 2], F32)
        winv = sb("winv", [P, 2], F32)
        escale = sb("escale", [P, 1], F32)

        x_tm = sb("x_tm", [P, NT, CH], F32)
        cmax = sb("cmax", [P, NT], F32)
        tmp4 = sb("tmp4", [P, NT], F32)
        xs = sb("xs", [P, NT, CH], F32)
        csum = sb("csum", [P, NT], F32)
        crec = sb("crec", [P, NT], F32)
        selT = sb("selT", [P, T], F32)
        h = sb("h", [P, NT, PAD + C], F32)

        class Rows:
            def __init__(self, tag, hc):
                self.stats = sb(tag + "stats", [P, NT, 6], F32)
                self.mv = sb(tag + "mv", [P, NT, 2], F32)
                self.vare = sb(tag + "vare", [P, NT], F32)
                self.rstd = sb(tag + "rstd", [P, NT], F32)
                self.negmean = sb(tag + "negmean", [P, NT], F32)
                self.hc = hc
                self.amax = sb(tag + "amax", [P, NT], F32)
                self.aval = sb(tag + "aval", [P, NT], F32)
                self.arec = sb(tag + "arec", [P, NT], F32)
                self.astep = sb(tag + "astep", [P, NT], F32)
                self.fscale = sb(tag + "fscale", [P, NT], F32)
                self.xqi = sb(tag + "xqi", [P, NT, C], BF16)
                self.xqT = sb(tag + "xqT", [P, KT, N], BF16)

        fr = Rows("f", sb("fhc", [P, NT, C], F32))
        bk = Rows("b", wstage[:, 2, :].rearrange("p (r c) -> p r c", r=NT))
        abc = sb("abc", [P, N], F32)
        diag = sb("diag", [P, NT, P], F32)

        qk32 = sb("qk32", [P, 2, N], F32)
        parts = sb("parts", [P, 2, 2, G, N], F16)
        QS = sb("QS", [P, G, HG, N], F16)
        KS = sb("KS", [P, G, HG, N], F16)
        V = sb("V", [P, NT, C], F32)
        Vn = sb("Vn", [P, NT, C], F32)
        mx = sb("mx", [P, 2, NT, HG], F32)
        mh = sb("mh", [P, NT, HG], F16)
        mr = sb("mr", [P, NT, HG], F32)
        mr2 = sb("mr2", [P, NT, HG], F32)
        mm = sb("mm", [P, NT, HG, DH], F16)
        mT = sb("mT", [P, N], F16)
        pT = sb("pT", [P, 2, HG, N], F32)
        rden = sb("rden", [P, N], F32)
        oT = wstage[:, 3, :].rearrange("p (g n) -> p g n", g=G)

        h1 = wstage[:, 0, :].rearrange("p (r c) -> p r c", r=NT)
        x2 = wstage[:, 1, :].rearrange("p (r c) -> p r c", r=NT)
        x2p = sb("x2p", [P, 2, 2, C], F16)

        ps_s1 = ps("ps_s1", [P, 2, 512], F32)
        ps_s2 = ps("ps_s2", [P, 2, 512], F32)
        ps_o = ps("ps_o", [P, 512], F32)
        ps_den = ps("ps_den", [P, 512], F32)
        ps_f = ps("ps_f", [P, 512], F32)
        ps_b = ps("ps_b", [P, 512], F32)

        loaded = sem("loaded")
        gathered = sem("gathered")
        consts_set = sem("consts_set")
        idents_cast = sem("idents_cast")
        w_step = sem("w_step")
        passed = sem("passed")
        w_summed = sem("w_summed")
        w_ready = sem("w_ready")

        def signal(name, per, giver):
            given[giver].append(sem(name))
            return given[giver][-1], per

        given = {"pe": [], "act": [], "dve": [], "pool": [], "sp": []}
        FU = 22
        front_full = signal("front_full", FU, "pe")
        x_ready = signal("x_ready", 1, "dve")
        xs_ready = signal("xs_ready", 2, "dve")
        ex_ready = signal("ex_ready", 2, "act")
        sel_ready = signal("sel_ready", 2, "dve")
        selT_ready = signal("selT_ready", 2, "dve")
        h_ready = signal("h_ready", NT, "act")
        h_kept = signal("h_kept", 16, "sp")
        h_fetched = signal("h_fetched", 16, "sp")
        tok_step = signal("tok_step", 6, "dve")
        fr_step = signal("fr_step", NT + 1 + 4, "dve")
        bk_step = signal("bk_step", NT + 1 + 3, "dve")
        norm_step = signal("norm_step", G, "dve")
        part_step = signal("part_step", 2 * G, "pool")
        max_step = signal("max_step", 3 * G, "pool")
        x2_step = signal("x2_step", NT, "pool")
        fvar_ready = signal("fvar_ready", 1, "dve")
        frstd_ready = signal("frstd_ready", 1, "pool")
        fc_ready = signal("fc_ready", NT, "act")
        ff_ready = signal("ff_ready", 1, "dve")
        fq_ready = signal("fq_ready", NT, "act")
        fi_ready = signal("fi_ready", NT, "pool")
        fT_ready = signal("fT_ready", 2, "act")
        diag_ready = signal("diag_ready", 1, "dve")
        abc_ready = signal("abc_ready", 1, "act")
        qk32_ready = signal("qk32_ready", 2 * G, "dve")
        parts_ready = signal("parts_ready", 2 * G, "pool")
        v_ready = signal("v_ready", NT, "act")
        stacked = [signal("stacked0", 16 * 24, "sp"), signal("stacked1", 16 * 24, "sp")]
        v_moved = signal("v_moved", 16, "sp")
        s1_ready = signal("s1_ready", 32, "pe")
        s1_read = signal("s1_read", 32, "dve")
        mm_ready = signal("mm_ready", G, "pool")
        m_full = signal("m_full", G, "pe")
        mT_ready = signal("mT_ready", G, "act")
        m_stacked = signal("m_stacked", 16 * G * HG, "sp")
        s2_ready = signal("s2_ready", 32, "pe")
        p_ready = signal("p_ready", 32, "act")
        pv_done = signal("pv_done", 16, "pe")
        o_normed = signal("o_normed", G, "dve")
        back_full = signal("back_full", 10, "pe")
        bc_ready = signal("bc_ready", NT, "act")
        bf_ready = signal("bf_ready", 1, "dve")
        bq_ready = signal("bq_ready", NT, "act")
        bi_ready = signal("bi_ready", NT, "pool")
        bT_ready = signal("bT_ready", 2, "act")
        h1_ready = signal("h1_ready", NT, "dve")
        bvar_ready = signal("bvar_ready", 1, "dve")
        brstd_ready = signal("brstd_ready", 1, "pool")
        x2_ready = signal("x2_ready", NT, "dve")
        x2p_ready = signal("x2p_ready", NT, "pool")
        h1_stored = signal("h1_stored", 16 * NT, "sp")
        x2_stored = signal("x2_stored", 16 * NT, "sp")

        def start_at_one(eng, giver):
            for s in given[giver]:
                eng.sem_inc(s, 1)

        def until(eng, signal, b, k):
            s, per = signal
            eng.wait_ge(s, b * per + k + 1)
            if eng in (nc.gpsimd, nc.sync) and not isinstance(b, int):
                eng.sem_inc(passed, 1)

        U_XT, U_SELT0, U_EXT0, U_CONV, U_CONVT, U_SELT1, U_EXT1, U_QIT = range(8)
        U_ABC = U_QIT + 2
        U_QK = U_ABC + 1
        U_V = U_QK + 2 * G
        DRAINED = [(h_ready, 1), (selT_ready, 1), (h_ready, 2), (h_ready, 3), (xs_ready, 2), (selT_ready, 2),
                   (h_ready, 4), (fT_ready, 1), (fT_ready, 2), (abc_ready, 1)] \
            + [(qk32_ready, n + 1) for n in range(2 * G)] + [(v_ready, n + 1) for n in range(NT)]
        B_OT, B_QT, B_PROJ = 0, NT, NT + 2
        B_DRAINED = [(bc_ready, n + 1) for n in range(NT)] + [(bT_ready, 1), (bT_ready, 2)] \
            + [(h1_ready, n + 1) for n in range(NT)]
        assert len(DRAINED) == FU == U_V + NT and len(B_DRAINED) == back_full[1] == B_PROJ + NT

        def sequences(eng, attention_step, front_at, back_at, front_all, back_all):
            def one(b, front, back):
                for s in range(16):
                    attention_step(b, s, front or s < 12)
                    if back:
                        back_at(b - 1, s)
                    if front:
                        front_at(b + 1, s)

            front_all(0)
            one(0, True, False)
            with eng.Fori(1, B - 1) as b:
                one(b, True, True)
            one(B - 1, False, True)
            back_all(B - 1)

        block = ctx.enter_context(nc.Block())

        @block.sync
        def _(sp):
            start_at_one(sp, "sp")
            for dst, src in ((idx[:, :], ids), (ident[:, :], ident_in), (maskf[:, 0, :], mask_in),
                             (maskf[:, 1, :], maskT_in),
                             (wstage[:, :, 0:3 * C], wqkv.rearrange("(k p) o -> p k o", p=P)),
                             (wstage[:, :, 3 * C:], wproj.rearrange("(k p) o -> p k o", p=P)),
                             (pe_tm[:, :, :], pe_tab.rearrange("(t p) c -> p t c", p=P)),
                             (sp0[:, :], spos0), (sp1[:, :], spos1), (convw[:, :, :], conv_w), (convb[:, :], conv_b)):
                sp.dma_start(dst, src).then_inc(loaded, 16)

            def stack(b, half, used):
                until(sp, parts_ready, b, G * (half + 1))
                if used:
                    until(sp, s2_ready, b - 1, 16 * (half + 1))
                gs = slice(2 * half, 2 * half + 2)
                for st, w, order in ((QS, 0, (0, 0, 1)), (KS, 1, (0, 1, 0))):
                    for r, part in enumerate(order):
                        for j in range(HG):
                            sp.dma_start(st[DH * r:DH * r + DH, gs, j, :],
                                         parts[DH * j:DH * j + DH, w, part, gs, :]).then_inc(stacked[half][0], 16)

            def move_v(b, used):
                until(sp, v_ready, b, NT)
                if used:
                    until(sp, pv_done, b - 1, 16)
                sp.dma_start(V[:, :, :], Vn[:, :, :]).then_inc(v_moved[0], 16)

            def rows_of(b):
                return h1_dram[bass.ds(b * N, N), :].rearrange("(r p) c -> p r c", p=P)

            def keep_h(b):
                until(sp, h_ready, b, NT)
                sp.dma_start(rows_of(b), h[:, :, PAD:]).then_inc(h_kept[0], 16)

            def fetch_h(b):
                until(sp, h_kept, b, 16)
                if not (isinstance(b, int) and b == 0):
                    until(sp, h1_stored, b - 1, 16 * NT)
                sp.dma_start(h1[:, :, :], rows_of(b)).then_inc(h_fetched[0], 16)

            def maxima_rows(b, g):
                until(sp, mT_ready, b, g + 1)
                for j in range(HG):
                    sp.dma_start(QS[KPARTS:KPARTS + MROWS, g, j, :],
                                 mT[DH * j:DH * j + MROWS, :]).then_inc(m_stacked[0], 16)

            def attention_step(b, s, more):
                if s % NT == NT - 1 and more:
                    g = s // NT + 1
                    maxima_rows(b + g // G, g % G)

            def front_at(b, s):
                if s == 5:
                    keep_h(b)
                if s == 9:
                    stack(b, 0, True)
                if s == 15:
                    stack(b, 1, True)
                    move_v(b, True)

            def store(b, i):
                until(sp, h1_ready, b, i + 1)
                sp.dma_start(h1_dram[bass.ds(b * N + i * P, P), :], h1[:, i, :]).then_inc(h1_stored[0], 16)

            def store_x2(b, i):
                until(sp, x2p_ready, b, i + 1)
                sp.dma_start(x2_dram[bass.ds(b * N + i * P, P), :],
                             x2p[:, i % 2, :, :].rearrange("p a c -> p (a c)")).then_inc(x2_stored[0], 16)

            def back_at(b, s):
                if s == 0:
                    fetch_h(b)
                if s in (7, 8):
                    store(b, 2 * (s - 7))
                    store(b, 2 * (s - 7) + 1)
                if s in (10, 11):
                    store_x2(b, 2 * (s - 10))
                    store_x2(b, 2 * (s - 10) + 1)

            def front_all(b):
                sp.wait_ge(w_ready, 2)
                keep_h(b)
                stack(b, 0, False)
                stack(b, 1, False)
                move_v(b, False)
                maxima_rows(b, 0)

            def back_all(b):
                for s in range(16):
                    back_at(b, s)

            sequences(sp, attention_step, front_at, back_at, front_all, back_all)
            until(sp, h1_stored, B - 1, h1_stored[1])
            until(sp, x2_stored, B - 1, x2_stored[1])

        @block.gpsimd
        def _(pool):
            start_at_one(pool, "pool")
            nc.gpsimd.memset(neghalf[:, :], -0.5).then_inc(consts_set, 1)
            nc.gpsimd.memset(ones[:, :], 1.0).then_inc(consts_set, 1)
            nc.gpsimd.memset(h[:, :, 0:PAD], 0.0).then_inc(consts_set, 1)
            nc.gpsimd.memset(mm[:, :, :, :], 0.0).then_inc(consts_set, 1)
            pool.wait_ge(consts_set, 4)
            nc.gpsimd.memset(KS[KPARTS:P, :, :, :], MUNIT).then_inc(consts_set, 1)
            pool.wait_ge(consts_set, 5)
            pool.wait_ge(loaded, 16 * 11)
            for t in range(B * NT):
                nc.gpsimd.indirect_dma_start(
                    out=emb_all[:, t, :], out_offset=None, in_=emb,
                    in_offset=bass.IndirectOffsetOnAxis(ap=idx[:, t:t + 1], axis=0)).then_inc(gathered, 16)

            def rsqrt(rows, asked, given_, b):
                until(pool, asked, b, 1)
                nc.gpsimd.tensor_tensor(rows.rstd[:, :], rows.vare[:, :], neghalf[:, :], ALU.pow).then_inc(given_[0], 1)

            def to_integers(rows, asked, given_, b):
                for r in range(NT):
                    until(pool, asked, b, r + 1)
                    nc.gpsimd.tensor_scalar(rows.xqi[:, r, :], rows.hc[:, r, :], ROUND, None,
                                            ALU.subtract).then_inc(given_[0], 1)

            def parts_of(b, n):
                g, w = n // 2, n % 2
                until(pool, qk32_ready, b, n + 1)
                nc.gpsimd.tensor_copy(parts[:, w, 0, g, :], qk32[:, w, :]).then_inc(part_step[0], 1)
                until(pool, part_step, b, n + 1)
                nc.gpsimd.tensor_tensor(parts[:, w, 1, g, :], qk32[:, w, :], parts[:, w, 0, g, :],
                                        ALU.subtract).then_inc(parts_ready[0], 1)

            def maxima(b, g):
                until(pool, s1_read, b, 8 * g + 8)
                m = mx[:, g % 2, :, :]
                nc.gpsimd.tensor_scalar(mh[:, :, :], m, -1.0 / (4 * MUNIT), None, ALU.mult).then_inc(max_step[0], 1)
                until(pool, max_step, b, 3 * g + 1)
                nc.gpsimd.tensor_scalar(mr[:, :, :], mh[:, :, :], -4.0 * MUNIT, None, ALU.mult).then_inc(max_step[0], 1)
                until(pool, max_step, b, 3 * g + 2)
                nc.gpsimd.tensor_tensor(mr2[:, :, :], mr[:, :, :], m, ALU.subtract).then_inc(max_step[0], 1)
                until(pool, max_step, b, 3 * g + 3)
                until(pool, m_full, b, g)
                nc.gpsimd.tensor_scalar(mm[:, :, :, 4], mr2[:, :, :], 1.0 / MUNIT, None, ALU.mult)
                nc.gpsimd.tensor_copy(mm[:, :, :, 0:4],
                                      mh[:, :, :].unsqueeze(3).to_broadcast([P, NT, HG, 4])).then_inc(mm_ready[0], 1)

            def attention_step(b, s, more):
                if s % NT == NT - 1 and more:
                    g = s // NT + 1
                    maxima(b + g // G, g % G)

            def front_at(b, s):
                if s == 5:
                    rsqrt(fr, fvar_ready, frstd_ready, b)
                if s == 6:
                    to_integers(fr, fq_ready, fi_ready, b)
                if s == 8:
                    if not (isinstance(b, int) and b == 0):
                        until(pool, stacked[0], b - 1, stacked[0][1])
                        until(pool, stacked[1], b - 1, stacked[1][1])
                    for n in range(G):
                        parts_of(b, n)
                if s == 10:
                    for n in range(G, 2 * G):
                        parts_of(b, n)

            def halves(b, r):
                until(pool, x2_ready, b, r + 1)
                nc.gpsimd.tensor_copy(x2p[:, r % 2, 0, :], x2[:, r, :]).then_inc(x2_step[0], 1)
                until(pool, x2_step, b, r + 1)
                nc.gpsimd.tensor_tensor(x2p[:, r % 2, 1, :], x2[:, r, :], x2p[:, r % 2, 0, :],
                                        ALU.subtract).then_inc(x2p_ready[0], 1)

            def back_at(b, s):
                if s == 2:
                    to_integers(bk, bq_ready, bi_ready, b)
                if s == 7:
                    rsqrt(bk, bvar_ready, brstd_ready, b)
                if s in (9, 11):
                    if s == 11:
                        until(pool, x2_stored, b, 16 * 2)
                    elif not (isinstance(b, int) and b == 0):
                        until(pool, x2_stored, b - 1, 16 * NT)
                    for r in (s - 9, s - 8):
                        halves(b, r)

            def front_all(b):
                for s in range(16):
                    front_at(b, s)
                maxima(b, 0)

            def back_all(b):
                for s in range(16):
                    back_at(b, s)

            sequences(pool, attention_step, front_at, back_at, front_all, back_all)

        @block.scalar
        def _(act):
            start_at_one(act, "act")
            act.wait_ge(consts_set, 5)
            act.wait_ge(loaded, 16 * 11)

            def full(b, u):
                until(act, front_full, b, u + 1)

            def exps(b, use):
                until(act, xs_ready, b, use + 1)
                nc.scalar.activation(xs[:, :, :], xs[:, :, :], ACT.Exp).then_inc(ex_ready[0], 1)

            def integers_out(rows, half, bank, given_):
                nc.scalar.copy(rows.xqT[:, 2 * half:2 * half + 2, :].rearrange("p k n -> p (k n)"),
                               bank[:, :].bitcast(BF16)).then_inc(given_[0], 1)

            def front_at(b, s):
                if s == 0:
                    exps(b, 0)
                    full(b, U_XT)
                    until(act, h_kept, b - 1, 16) if not (isinstance(b, int) and b == 0) else None
                    nc.scalar.copy(h[:, 0, PAD:], ps_f[:, :]).then_inc(h_ready[0], 1)
                if s == 1:
                    full(b, U_EXT0)
                    nc.scalar.copy(h[:, 1, PAD:], ps_f[:, :]).then_inc(h_ready[0], 1)
                if s == 2:
                    full(b, U_CONV)
                    nc.scalar.activation(h[:, 2, PAD:], ps_f[:, :], ACT.Identity,
                                         bias=convb[:, 0:1]).then_inc(h_ready[0], 1)
                if s == 3:
                    exps(b, 1)
                if s == 4:
                    full(b, U_EXT1)
                    nc.scalar.copy(h[:, 3, PAD:], ps_f[:, :]).then_inc(h_ready[0], 1)
                if s == 5:
                    until(act, fvar_ready, b, 1)
                    for r in range(NT):
                        nc.scalar.activation(fr.hc[:, r, :], h[:, r, PAD:], ACT.Identity,
                                             bias=fr.negmean[:, r:r + 1]).then_inc(fc_ready[0], 1)
                if s == 6:
                    until(act, ff_ready, b, 1)
                    for r in range(NT):
                        nc.scalar.activation(fr.hc[:, r, :], fr.hc[:, r, :], ACT.Copy, bias=ROUND,
                                             scale=fr.fscale[:, r:r + 1]).then_inc(fq_ready[0], 1)
                if s == 7:
                    for half in range(2):
                        full(b, U_QIT + half)
                        integers_out(fr, half, ps_f, fT_ready)
                    full(b, U_ABC)
                    nc.scalar.copy(abc[:, :], ps_f[:, :]).then_inc(abc_ready[0], 1)
                if s == 11:
                    for i in range(NT):
                        full(b, U_V + i)
                        if i == 0 and not (isinstance(b, int) and b == 0):
                            until(act, v_moved, b - 1, 16)
                        nc.scalar.activation(Vn[:, i, :], ps_f[:, :], ACT.Copy,
                                             scale=fr.astep[:, i:i + 1]).then_inc(v_ready[0], 1)

            def maxima_out(b, g, first):
                until(act, m_full, b, g + 1)
                if not first:
                    until(act, m_stacked, b, 16 * HG * g)
                nc.scalar.copy(mT[:, :], ps_b[:, :].bitcast(F16)[:, 0:N]).then_inc(mT_ready[0], 1)

            def attention_step(b, s, more):
                k, w = s, N - (s % NT) * P
                if not (isinstance(b, int) and b == 0 and s < 2):
                    until(act, pv_done, b, k - 1)
                for pr in range(2):
                    until(act, s2_ready, b, 2 * k + pr + 1)
                    nc.scalar.activation(pT[:, k % 2, 2 * pr:2 * pr + 2, 0:w], ps_s2[:, :, 0:w], ACT.Exp,
                                         scale=escale[:, 0:1]).then_inc(p_ready[0], 1)
                if s % NT == NT - 1 and more:
                    g = s // NT + 1
                    maxima_out(b + g // G, g % G, False)

            def back_at(b, s):
                if s == 0:
                    for i in range(NT):
                        until(act, back_full, b, B_OT + i + 1)
                        nc.scalar.copy(bk.hc[:, i, :], ps_b[:, :]).then_inc(bc_ready[0], 1)
                if s == 1:
                    until(act, bf_ready, b, 1)
                    for r in range(NT):
                        nc.scalar.activation(bk.hc[:, r, :], bk.hc[:, r, :], ACT.Copy, bias=ROUND,
                                             scale=bk.fscale[:, r:r + 1]).then_inc(bq_ready[0], 1)
                if s == 2:
                    for half in range(2):
                        until(act, back_full, b, B_QT + half + 1)
                        integers_out(bk, half, ps_b, bT_ready)

            def front_all(b):
                for s in range(16):
                    front_at(b, s)
                maxima_out(b, 0, True)

            def back_all(b):
                for s in range(16):
                    back_at(b, s)

            sequences(act, attention_step, front_at, back_at, front_all, back_all)

        @block.vector
        def _(dve):
            start_at_one(dve, "dve")
            nw = [0]

            def wlink(ins):
                nw[0] += 1
                ins.then_inc(w_step, 1)
                dve.wait_ge(w_step, nw[0])

            dve.wait_ge(loaded, 16 * 11)
            nc.vector.tensor_copy(identb[:, :], ident[:, :]).then_inc(idents_cast, 1)
            nc.vector.tensor_copy(identh[:, :], ident[:, :]).then_inc(idents_cast, 1)
            nc.vector.tensor_copy(maskb[:, :, :], maskf[:, :, :]).then_inc(idents_cast, 1)
            cols = (slice(0, 3 * C), slice(3 * C, 4 * C))
            for t in range(2):
                nc.vector.tensor_reduce(wsum[:, t:t + 1], wstage[:, :, cols[t]], axis=mybir.AxisListType.XY,
                                        op=ALU.add, apply_absolute_value=True).then_inc(w_summed, 1)
            dve.wait_ge(w_summed, 3)
            for t in range(2):
                wlink(nc.vector.tensor_scalar(wmean[:, t:t + 1], ps_o[:, t:t + 1],
                                              1.0 / (C * (cols[t].stop - cols[t].start)), CLIP, ALU.mult, ALU.max))
            wlink(nc.vector.reciprocal(winv[:, :], wmean[:, :]))
            wlink(nc.vector.tensor_scalar(escale[:, :], wmean[:, 0:1], wmean[:, 0:1], ATT_SCALE, ALU.mult, ALU.mult))
            for t in range(2):
                w = wstage[:, :, cols[t]]
                wlink(nc.vector.tensor_scalar(w, w, winv[:, t:t + 1], ROUND, ALU.mult, ALU.add))
                wlink(nc.vector.tensor_scalar(w, w, ROUND, 1.0, ALU.subtract, ALU.min))
                nc.vector.tensor_scalar(wq[:, :, cols[t]], w, -1.0, None, ALU.max).then_inc(w_ready, 1)
            dve.wait_ge(gathered, 16 * B * NT)
            dve.wait_ge(consts_set, 5)

            def full(b, u):
                until(dve, front_full, b, u + 1)

            def less_maximum(b, use, src):
                nc.vector.tensor_reduce(cmax[:, :], src, axis=AX, op=ALU.max).then_inc(tok_step[0], 1)
                until(dve, tok_step, b, 3 * use + 1)
                nc.vector.tensor_tensor(xs[:, :, :], src, cmax[:, :].unsqueeze(2).to_broadcast([P, NT, CH]),
                                        ALU.subtract).then_inc(xs_ready[0], 1)

            def normalised(b, use):
                until(dve, ex_ready, b, use + 1)
                nc.vector.tensor_reduce(csum[:, :], xs[:, :, :], axis=AX, op=ALU.add).then_inc(tok_step[0], 1)
                until(dve, tok_step, b, 3 * use + 2)
                nc.vector.reciprocal(crec[:, :], csum[:, :]).then_inc(tok_step[0], 1)
                until(dve, tok_step, b, 3 * use + 3)
                nc.vector.tensor_tensor(xs[:, :, :], xs[:, :, :], crec[:, :].unsqueeze(2).to_broadcast([P, NT, CH]),
                                        ALU.mult).then_inc(sel_ready[0], 1)

            def turned(b, u):
                full(b, u)
                nc.vector.tensor_copy(selT[:, :], ps_f[:, :]).then_inc(selT_ready[0], 1)

            def statistics(b, rows, src, asked, step, given_):
                for r in range(NT):
                    until(dve, asked, b, r + 1)
                    nc.vector.bn_stats(rows.stats[:, r, :], src[r]).then_inc(step[0], 1)
                until(dve, step, b, NT)
                dve.sem_inc(passed, 1)
                for r in range(NT):
                    last = nc.vector.bn_aggr(rows.mv[:, r, :], rows.stats[:, r, :])
                last.then_inc(step[0], 1)
                until(dve, step, b, NT + 1)
                nc.vector.tensor_scalar(rows.negmean[:, :], rows.mv[:, :, 0], -1.0, None, ALU.mult)
                nc.vector.tensor_scalar(rows.vare[:, :], rows.mv[:, :, 1], EPS, None, ALU.add).then_inc(given_[0], 1)

            def largest(b, rows, asked, step, k):
                for r in range(NT):
                    until(dve, asked, b, r + 1)
                    last = nc.vector.tensor_reduce(rows.amax[:, r:r + 1], rows.hc[:, r, :], axis=AX, op=ALU.max,
                                                   apply_absolute_value=True)
                last.then_inc(step[0], 1)
                until(dve, step, b, k)

            def front_at(b, s):
                if s == 0:
                    nc.vector.scalar_tensor_tensor(x_tm[:, :, :], emb_all[:, bass.ds(b * NT, NT), :],
                                                   float(np.sqrt(np.float32(CH))), pe_tm[:, :, :],
                                                   ALU.mult, ALU.add).then_inc(x_ready[0], 1)
                    until(dve, x_ready, b, 1)
                    less_maximum(b, 0, x_tm[:, :, :])
                    normalised(b, 0)
                if s == 1:
                    turned(b, U_SELT0)
                if s == 3:
                    full(b, U_CONVT)
                    less_maximum(b, 1, ps_f[:, :].rearrange("p (t c) -> p t c", t=NT))
                    normalised(b, 1)
                if s == 4:
                    turned(b, U_SELT1)
                if s == 5:
                    statistics(b, fr, [h[:, r, PAD:] for r in range(NT)], h_ready, fr_step, fvar_ready)
                    largest(b, fr, fc_ready, fr_step, NT + 2)
                    until(dve, frstd_ready, b, 1)
                    nc.vector.tensor_tensor(tmp4[:, :], fr.amax[:, :], fr.rstd[:, :], ALU.mult).then_inc(fr_step[0], 1)
                    until(dve, fr_step, b, NT + 3)
                    nc.vector.tensor_scalar(fr.aval[:, :], tmp4[:, :], CLIP, None, ALU.max).then_inc(fr_step[0], 1)
                    until(dve, fr_step, b, NT + 4)
                    nc.vector.reciprocal(fr.arec[:, :], fr.aval[:, :]).then_inc(fr_step[0], 1)
                    until(dve, fr_step, b, NT + 5)
                    nc.vector.tensor_scalar(fr.astep[:, :], fr.aval[:, :], 1.0 / QMAX, None, ALU.mult)
                    nc.vector.scalar_tensor_tensor(fr.fscale[:, :], fr.arec[:, :], QMAX, fr.rstd[:, :], ALU.mult,
                                                   ALU.mult).then_inc(ff_ready[0], 1)
                    until(dve, ff_ready, b, 1)
                    for r in range(NT):
                        last = nc.vector.tensor_scalar(diag[:, r, :], ident[:, :], fr.astep[:, r:r + 1], None, ALU.mult)
                    last.then_inc(diag_ready[0], 1)
                if s in (8, 10):
                    if s == 8:
                        until(dve, abc_ready, b, 1)
                        if not (isinstance(b, int) and b == 0):
                            until(dve, parts_ready, b - 1, 2 * G)
                    for n in range(4 * (s // 10), 4 * (s // 10) + 4):
                        full(b, U_QK + n)
                        if n >= 2:
                            until(dve, parts_ready, b, n - 1)
                        nc.vector.tensor_tensor(qk32[:, n % 2, :], ps_f[:, :], abc[:, :],
                                                ALU.mult).then_inc(qk32_ready[0], 1)

            def row_maxima(b, g, i):
                if i == 0 and not (isinstance(b, int) and b == 0 and g < 2):
                    until(dve, mm_ready, b, g - 1)
                for pr in range(2):
                    until(dve, s1_ready, b, 8 * g + 2 * i + pr + 1)
                    nc.vector.tensor_reduce(mx[:, g % 2, i, 2 * pr:2 * pr + 2], ps_s1[:, :, 0:(i + 1) * P], axis=AX,
                                            op=ALU.max).then_inc(s1_read[0], 1)

            def attention_step(b, s, more):
                g = s // NT + 1
                if more:
                    row_maxima(b + g // G, g % G, s % NT)
                if s % NT == NT - 1:
                    until(dve, pv_done, b, NT * g)
                    nc.vector.reciprocal(rden[:, :], ps_den[:, :]).then_inc(norm_step[0], 1)
                    until(dve, norm_step, b, g)
                    nc.vector.tensor_tensor(oT[:, g - 1, :], ps_o[:, :], rden[:, :], ALU.mult).then_inc(o_normed[0], 1)

            def back_at(b, s):
                if s == 0:
                    largest(b, bk, bc_ready, bk_step, 1)
                    nc.vector.tensor_scalar(bk.aval[:, :], bk.amax[:, :], wmean[:, 0:1], CLIP, ALU.mult,
                                            ALU.max).then_inc(bk_step[0], 1)
                    until(dve, bk_step, b, 2)
                    nc.vector.reciprocal(bk.arec[:, :], bk.aval[:, :]).then_inc(bk_step[0], 1)
                    until(dve, bk_step, b, 3)
                    nc.vector.tensor_scalar(bk.astep[:, :], bk.aval[:, :], wmean[:, 1:2], 1.0 / QMAX, ALU.mult, ALU.mult)
                    nc.vector.tensor_scalar(bk.fscale[:, :], bk.arec[:, :], wmean[:, 0:1], QMAX, ALU.mult,
                                            ALU.mult).then_inc(bf_ready[0], 1)
                if s in (3, 4, 5, 6):
                    i = s - 3
                    if i == 0:
                        until(dve, h_fetched, b, 16)
                    until(dve, back_full, b, B_PROJ + i + 1)
                    nc.vector.scalar_tensor_tensor(h1[:, i, :], ps_b[:, :], bk.astep[:, i:i + 1], h1[:, i, :],
                                                   ALU.mult, ALU.add).then_inc(h1_ready[0], 1)
                if s == 7:
                    statistics2(b)
                if s == 9:
                    until(dve, brstd_ready, b, 1)
                    if not (isinstance(b, int) and b == 0):
                        until(dve, x2p_ready, b - 1, NT)
                    for r in range(NT):
                        nc.vector.tensor_scalar(x2[:, r, :], h1[:, r, :], bk.mv[:, r, 0:1], bk.rstd[:, r:r + 1],
                                                ALU.subtract, ALU.mult).then_inc(x2_ready[0], 1)

            def statistics2(b):
                for r in range(NT):
                    until(dve, h1_ready, b, r + 1)
                    nc.vector.bn_stats(bk.stats[:, r, :], h1[:, r, :]).then_inc(bk_step[0], 1)
                until(dve, bk_step, b, 3 + NT)
                dve.sem_inc(passed, 1)
                for r in range(NT):
                    last = nc.vector.bn_aggr(bk.mv[:, r, :], bk.stats[:, r, :])
                last.then_inc(bk_step[0], 1)
                until(dve, bk_step, b, 4 + NT)
                nc.vector.tensor_scalar(bk.vare[:, :], bk.mv[:, :, 1], EPS, None, ALU.add).then_inc(bvar_ready[0], 1)

            def front_all(b):
                for s in range(16):
                    front_at(b, s)
                for i in range(NT):
                    row_maxima(b, 0, i)

            def back_all(b):
                for s in range(16):
                    back_at(b, s)

            sequences(dve, attention_step, front_at, back_at, front_all, back_all)

        @block.tensor
        def _(pe):
            start_at_one(pe, "pe")
            pe.wait_ge(consts_set, 5)
            pe.wait_ge(idents_cast, 3)
            pe.wait_ge(w_summed, 2)
            nc.tensor.matmul(ps_o[:, 0:2], ones[:, :], wsum[:, :], start=True, stop=True).then_inc(w_summed, 1)
            pe.wait_ge(w_ready, 2)

            def bank_free(b, u):
                if u:
                    until(pe, DRAINED[u - 1][0], b, DRAINED[u - 1][1])
                elif not (isinstance(b, int) and b == 0):
                    until(pe, DRAINED[FU - 1][0], b - 1, DRAINED[FU - 1][1])

            def done(ins):
                ins.then_inc(front_full[0], 1)

            def transposes(b, u, src):
                bank_free(b, u)
                for t in range(NT):
                    last = nc.tensor.transpose(ps_f[:, t * P:(t + 1) * P], src(t), ident[:, :])
                done(last)

            def turn_integers(b, rows, half, bank, asked):
                if half == 0:
                    until(pe, asked, b, NT)
                for r in range(NT):
                    for kk in range(2):
                        k = 2 * half + kk
                        last = nc.tensor.transpose(bank[:, :].bitcast(BF16)[:, kk * N + r * P:kk * N + (r + 1) * P],
                                                   rows.xqi[:, r, k * P:(k + 1) * P], identb[:, :])
                return last

            def project(b, u):
                bank_free(b, u)
                if u < U_V:
                    g, w = (u - U_QK) // 2, (u - U_QK) % 2
                for k in range(KT):
                    if u < U_V:
                        lhsT, rhs = wq[:, k, w * C + g * P:w * C + (g + 1) * P], fr.xqT[:, k, :]
                    else:
                        lhsT, rhs = fr.xqT[:, k, (u - U_V) * P:(u - U_V + 1) * P], wq[:, k, 2 * C:3 * C]
                    last = nc.tensor.matmul(ps_f[:, :], lhsT, rhs, start=(k == 0), stop=(k == KT - 1))
                done(last)

            def front_at(b, s):
                if s == 0:
                    until(pe, x_ready, b, 1)
                    transposes(b, U_XT, lambda t: x_tm[:, t, :])
                    until(pe, sel_ready, b, 1)
                    transposes(b, U_SELT0, lambda t: xs[:, t, :])
                if s == 1:
                    bank_free(b, U_EXT0)
                    done(nc.tensor.matmul(ps_f[:, :], sp0[:, :], selT[:, :], start=True, stop=True))
                if s == 2:
                    bank_free(b, U_CONV)
                    for k in range(TAPS):
                        last = nc.tensor.matmul(ps_f[:, :], convw[:, k, :], h[:, 0, k:k + T],
                                                start=(k == 0), stop=(k == TAPS - 1))
                    done(last)
                if s == 3:
                    transposes(b, U_CONVT, lambda t: h[:, 2, PAD + t * P:PAD + (t + 1) * P])
                if s == 4:
                    until(pe, sel_ready, b, 2)
                    transposes(b, U_SELT1, lambda t: xs[:, t, :])
                    bank_free(b, U_EXT1)
                    done(nc.tensor.matmul(ps_f[:, :], sp1[:, :], selT[:, :], start=True, stop=True))
                if s == 7:
                    for half in range(2):
                        bank_free(b, U_QIT + half)
                        done(turn_integers(b, fr, half, ps_f, fi_ready))
                    bank_free(b, U_ABC)
                    until(pe, diag_ready, b, 1)
                    for r in range(NT):
                        last = nc.tensor.matmul(ps_f[:, r * P:(r + 1) * P], ones[:, :], diag[:, r, :],
                                                start=True, stop=True)
                    done(last)
                if s == 8:
                    for u in range(U_QK, U_QK + 4):
                        project(b, u)
                if s == 10:
                    for u in range(U_QK + 4, U_QK + 8):
                        project(b, u)
                if s == 11:
                    for u in range(U_V, U_V + NT):
                        project(b, u)

            def scores_for_maxima(b, g, i):
                if i == 0 and g % 2 == 0:
                    until(pe, stacked[g // 2], b, stacked[0][1])
                for pr in range(2):
                    if not (isinstance(b, int) and b == 0 and g == 0 and i == 0 and pr == 0):
                        until(pe, s1_read, b, 8 * g + 2 * i + pr)
                    for e in range(2):
                        j = 2 * pr + e
                        nc.tensor.matmul(ps_s1[:, e, 0:(i + 1) * P], QS[0:KPARTS, g, j, i * P:(i + 1) * P],
                                         KS[0:KPARTS, g, j, 0:(i + 1) * P], start=True, stop=False)
                        last = nc.tensor.matmul(ps_s1[:, e, i * P:(i + 1) * P], identb[:, :], maskb[:, 0, :],
                                                start=False, stop=True)
                    last.then_inc(s1_ready[0], 1)

            def maxima_rows(b, g, waits):
                for what in waits:
                    until(pe, *what)
                until(pe, mm_ready, b, g + 1)
                for i in range(NT):
                    last = nc.tensor.transpose(ps_b[:, :].bitcast(F16)[:, i * P:(i + 1) * P],
                                               mm[:, i, :, :].rearrange("p j r -> p (j r)"), identh[:, :])
                last.then_inc(m_full[0], 1)

            def scores(b, g, s):
                k = NT * g + s
                w = N - s * P
                if s == 0:
                    until(pe, m_stacked, b, 16 * HG * (g + 1))
                for pr in range(2):
                    if not (isinstance(b, int) and b == 0 and k + pr == 0):
                        until(pe, p_ready, b, 2 * k + pr)
                    for e in range(2):
                        j = 2 * pr + e
                        nc.tensor.matmul(ps_s2[:, e, 0:w], KS[0:KPARTS + MROWS, g, j, s * P:(s + 1) * P],
                                         QS[0:KPARTS + MROWS, g, j, s * P:N], start=True, stop=False)
                        last = nc.tensor.matmul(ps_s2[:, e, 0:P], identb[:, :], maskb[:, 1, :],
                                                start=False, stop=True)
                    last.then_inc(s2_ready[0], 1)

            def values(b, g, s):
                k = NT * g + s
                w = N - s * P
                until(pe, p_ready, b, 2 * k + 2)
                if s == 0:
                    if g == 0:
                        until(pe, v_moved, b, 16)
                    if not (isinstance(b, int) and b == 0 and g == 0):
                        until(pe, o_normed, b, g)
                for j in range(HG):
                    nc.tensor.matmul(ps_o[DH * j:DH * j + DH, s * P:N],
                                     V[:, s, (HG * g + j) * DH:(HG * g + j + 1) * DH], pT[:, k % 2, j, 0:w],
                                     start=(s == 0), stop=(s == NT - 1))
                for j in range(HG):
                    last = nc.tensor.matmul(ps_den[DH * j:DH * j + DH, s * P:N], ones[:, 0:DH],
                                            pT[:, k % 2, j, 0:w], start=(s == 0), stop=(s == NT - 1))
                last.then_inc(pv_done[0], 1)

            def attention_step(b, s, more):
                g, t = s // NT, s % NT
                nb, ng = b + (g + 1) // G, (g + 1) % G
                if more:
                    scores_for_maxima(nb, ng, t)
                scores(b, g, t)
                if t:
                    values(b, g, t - 1)
                if t == NT - 1:
                    values(b, g, t)
                    if more:
                        waits = [(mT_ready, nb, ng)]
                        if g == 0 and not (isinstance(b, int) and b == 0):
                            waits.append((bT_ready, b - 1, 2))
                        if g == 1 and not (isinstance(b, int) and b == 0):
                            waits.append((h1_ready, b - 1, NT))
                        maxima_rows(nb, ng, waits)

            def back_free(b, u, m):
                if u:
                    until(pe, B_DRAINED[u - 1][0], b, B_DRAINED[u - 1][1])
                if m is not None:
                    until(pe, mT_ready, *m)

            def back_at(b, s, alone=False):
                if s == 0:
                    until(pe, o_normed, b, G)
                    for i in range(NT):
                        back_free(b, B_OT + i, None if i else (b, G) if alone else (b + 1, 1))
                        for g in range(G):
                            last = nc.tensor.transpose(ps_b[:, g * P:(g + 1) * P], oT[:, g, i * P:(i + 1) * P], ident[:, :])
                        last.then_inc(back_full[0], 1)
                if s == 2:
                    for half in range(2):
                        back_free(b, B_QT + half, None)
                        turn_integers(b, bk, half, ps_b, bi_ready).then_inc(back_full[0], 1)
                if s in (3, 4, 5, 6):
                    i = s - 3
                    back_free(b, B_PROJ + i, None if i or alone else (b + 1, 2))
                    for k in range(KT):
                        last = nc.tensor.matmul(ps_b[:, :], bk.xqT[:, k, i * P:(i + 1) * P], wq[:, k, 3 * C:],
                                                start=(k == 0), stop=(k == KT - 1))
                    last.then_inc(back_full[0], 1)

            def front_all(b):
                for s in range(16):
                    front_at(b, s)
                for i in range(NT):
                    scores_for_maxima(b, 0, i)
                maxima_rows(b, 0, [])

            def back_all(b):
                for s in range(16):
                    back_at(b, s, True)

            sequences(pe, attention_step, front_at, back_at, front_all, back_all)


def ffn_phase(nc, ident_in, tri_in, lanes_in, gate_w, w1, b1, w2, b2, sw1, sb1, sw2, sb2, h1_dram, x2_dram, out):
    TT = B * N // P
    TILES = 2 * TT + E_
    FS = SH // P
    FE = HID // P
    W1N, W2N = KT * 2 * HID, FE * 2 * C
    WROW = (W1N + W2N) // 2 + FE
    D = 4
    TOP = 2.0 ** 10
    base_dram = nc.dram_tensor("base_rows", [B * N, C], F32, kind="Internal").ap()
    y_dram = nc.dram_tensor("expert_rows", [TILES * P, C], F32, kind="Internal").ap()
    ctx = ExitStack()
    with ctx:
        def sb(name, shape, dt):
            return ctx.enter_context(nc.sbuf_tensor(name, shape, dt))

        def sem(name):
            return ctx.enter_context(nc.semaphore(name))

        identf = sb("f_identf", [P, P], F32)
        ident = sb("f_ident", [P, P], F16)
        trif = sb("f_trif", [P, P], F32)
        lanes = sb("f_lanes", [P, P], F32)
        part = sb("f_part", [P, 1], F32)
        ones = sb("f_ones", [P, P], BF16)
        tri = sb("f_tri", [P, P], BF16)
        ew = sb("f_ew", [P, E_, WROW], I32)
        sw1p = sb("f_sw1p", [P, KT, 2, SH], F16)
        sw2p = sb("f_sw2p", [P, FS, 2, C], F16)
        gwp = sb("f_gwp", [P, KT, 2, E_], F16)
        gws = sb("f_gws", [P, KT, E_], F32)
        sb1c = sb("f_sb1c", [P, FS], F32)
        sb2r = sb("f_sb2r", [P, C], F32)
        b2r = sb("f_b2r", [P, E_, C], F32)
        base = sb("f_base", [P, NT, C], F32)
        big = sb("f_big", [P, 8704], F32)
        lo_hot = big[:, 0:4096].bitcast(BF16).rearrange("p (n m) -> p n m", m=P)
        hi_hot = big[:, 4096:8704].bitcast(BF16).rearrange("p (n a m) -> p n a m", a=2, m=TILES)
        wmax = sb("f_wmax", [P, 8], F32)
        wall = sb("f_wall", [P, 8], F32)
        wpow = sb("f_wpow", [P, 8], F32)
        wup = sb("f_wup", [P, 8], F32)
        wdown = sb("f_wdown", [P, 8], F32)
        hb = sb("f_hb", [P, 2], F32)
        hpow = sb("f_hpow", [P, 2], F32)
        hup = sb("f_hup", [P, 2], F32)
        hdn = sb("f_hdn", [P, 2], F32)
        ydn = sb("f_ydn", [P, 2], F32)

        x2t = sb("f_x2t", [P, NT, 2 * C], F16)
        h1t = sb("f_h1t", [P, NT, C], F32)
        xT = sb("f_xT", [P, KT, 2, N], F16)
        act_h = sb("f_act", [P, 2, N], F32)
        gp = sb("f_gp", [P, FS, 2, N], F16)

        L = sb("f_L", [P, TT, E_], F32)
        eqs = sb("f_eqs", [P, TT, E_], F32)
        oh = sb("f_oh", [P, 2, TT, E_], F32)
        L2 = sb("f_L2", [P, TT, E_], F32)
        v12 = sb("f_v12", [P, 2, TT], F32)
        m12 = sb("f_m12", [P, 2, TT], F32)
        dlt = sb("f_dlt", [P, TT], F32)
        exd = sb("f_exd", [P, TT], F32)
        gate = sb("f_gate", [P, 2, TT], F32)
        prior = sb("f_prior", [P, E_], F32)
        both = sb("f_both", [P, TT, E_], BF16)
        pre = sb("f_pre", [P, TT, E_], F32)
        scan = sb("f_scan", [P, 2, TT, E_], F32)
        ntile = sb("f_ntile", [P, E_], F32)
        nt2 = sb("f_nt2", [P, E_], F32)
        tend = sb("f_tend", [P, 2, E_], F32)
        posn = sb("f_posn", [P, TT, E_], F32)
        slot = sb("f_slot", [P, 2, TT], F32)
        hi = sb("f_hi", [P, 2, TT], F32)
        lo = sb("f_lo", [P, 2, TT], F32)
        slot_i = sb("f_slot_i", [P, 2, TT], I32)
        tsel = sb("f_tsel", [P, TILES, E_], F32)
        texp = sb("f_texp", [P, TILES], F32)
        texp_i = sb("f_texp_i", [P, TILES], I32)
        tok_i = sb("f_tok_i", [P, TILES + D], I32)
        tok_f = sb("f_tok_f", [P, TILES], F32)

        now = sb("f_now", [P, D], I32)
        now2 = sb("f_now2", [P, D, 2], I32)
        xg = x2t
        xgT = sb("f_xgT", [P, 2, KT, 2, P], F16)
        wcur = big[:, 0:2 * WROW].bitcast(I32).rearrange("p (z w) -> p z w", z=2)
        ga = act_h[:, :, :].rearrange("p a n -> p (a n)").rearrange("p (z f n) -> p z f n", z=D, f=FE)
        gq = gp[:, 0:2, :, :].rearrange("p f a n -> p (f a n)").rearrange("p (z f a n) -> p z f a n", z=D, f=FE, a=2)
        yt = big[:, 4608:4608 + D * C].rearrange("p (z c) -> p z c", z=D)
        yg = ew[:, 0:5, :].rearrange("p e w -> p (e w)").bitcast(F32)[:, 0:D * 2 * C].rearrange(
            "p (z k c) -> p z k c", z=D, k=2)
        bt = h1t
        PS = ctx.enter_context(nc.psum_tensor("f_ps", [P, 8, 512], F32))

        loaded = sem("f_loaded")
        gated = sem("f_gated")
        set_up = sem("f_set_up")
        cast = sem("f_cast")
        passed = sem("f_passed")
        max_ready = sem("f_max_ready")
        all_max = sem("f_all_max")
        vstep = sem("f_vstep")
        scaled = sem("f_scaled")
        high_ready = sem("f_high_ready")
        stage_free = sem("f_stage_free")
        routed = sem("f_routed")
        route_pe = sem("f_route_pe")
        route_dve = sem("f_route_dve")
        route_act = sem("f_route_act")

        given = {"pe": [], "act": [], "dve": [], "pool": [], "sp": []}

        def signal(name, per, giver):
            s = sem(name)
            if giver is None:
                return s, per, 0
            given[giver].append(s)
            return s, per, 1

        x2_loaded = signal("f_x2_loaded", 16, "sp")
        h1_loaded = signal("f_h1_loaded", 16, "sp")
        tr_done = signal("f_tr_done", KT, "pe")
        xT_even = signal("f_xT_even", 2, "act")
        xT_odd = signal("f_xT_odd", 2, "dve")
        lg_done = signal("f_lg_done", 1, "pe")
        lg_read = signal("f_lg_read", 1, "dve")
        up_done = signal("f_up_done", FS, "pe")
        gelu_done = signal("f_gelu_done", FS, "act")
        ghi_done = signal("f_ghi_done", FS, "pool")
        glo_done = signal("f_glo_done", FS, "dve")
        down_done = signal("f_down_done", NT, "pe")
        h1b_done = signal("f_h1b_done", NT, "pool")
        base_done = signal("f_base_done", NT, "dve")
        base_stored = signal("f_base_stored", 16, "sp")
        c_now = signal("c_now", 1, "pool")
        d_now = signal("d_now", 1, "pool")
        c_gather = [signal("c_gather%d" % z, 16, None) for z in range(D)]
        c_tr = signal("c_tr", 1, "pe")
        c_xT = signal("c_xT", 1, "act")
        c_w1 = signal("c_w1", 1, "dve")
        c_w2 = signal("c_w2", 1, "dve")
        c_up = signal("c_up", 1, "pe")
        c_gelu = signal("c_gelu", 1, "act")
        c_hi = signal("c_hi", 1, "act")
        c_lo = signal("c_lo", 1, "dve")
        c_down = signal("c_down", 1, "pe")
        c_y = signal("c_y", 1, "dve")
        c_store = [signal("c_store%d" % z, 16, "sp") for z in range(D)]
        d_gather = [signal("d_gather%d" % z, 32, None) for z in range(D)]
        d_base = [signal("d_base%d" % z, 16, "sp") for z in range(D)]
        d_acc = signal("d_acc", 1, "dve")
        d_done = [signal("d_done%d" % z, 1, "dve") for z in range(D)]
        d_store = [signal("d_store%d" % z, 16, "sp") for z in range(D)]

        def start_at_one(eng, giver):
            for s in given[giver]:
                eng.sem_inc(s, 1)

        def until(eng, signal, b, k):
            s, per, start = signal
            eng.wait_ge(s, b * per + k + start)
            if eng in (nc.gpsimd, nc.sync) and not isinstance(b, int):
                eng.sem_inc(passed, 1)

        def weights(row):
            w1v = row[:, 0:W1N // 2].bitcast(F16).rearrange("p (k a n) -> p k a n", k=KT, a=2)
            w2v = row[:, W1N // 2:(W1N + W2N) // 2].bitcast(F16).rearrange("p (f a n) -> p f a n", f=FE, a=2)
            b1v = row[:, (W1N + W2N) // 2:WROW].bitcast(F32)
            return w1v, w2v, b1v

        def tile(t, z):
            return t + z // D, z % D

        def in_steps(eng, step):
            for k in (-2, -1, 0):
                step(0, k, True, False)
            with eng.Fori(0, TILES // D - 1) as t:
                for k in range(1, D + 1):
                    step(t, k, False, False)
            for k in range(1, D + 1):
                step(TILES // D - 1, k, False, True)

        block = ctx.enter_context(nc.Block())
        stage = {0: big[:, 0:8192].rearrange("p (e k n) -> p e k n", e=E_, k=KT),
                 1: big[:, 0:8192].rearrange("p (e f n) -> p e f n", e=E_, f=FE),
                 2: big[:, 0:KT * SH].rearrange("p (k n) -> p k n", k=KT),
                 3: big[:, KT * SH:KT * SH + FS * C].rearrange("p (f n) -> p f n", f=FS),
                 4: gws[:, :, :]}

        @block.sync
        def _(sp):
            start_at_one(sp, "sp")
            for dst, src in ((identf[:, :], ident_in), (trif[:, :], tri_in), (lanes[:, :], lanes_in),
                             (gws[:, :, :], gate_w.rearrange("(k p) e -> p k e", p=P)),
                             (sb1c[:, :], sb1), (ew[:, :, WROW - FE:].bitcast(F32), b1),
                             (sb2r[:, :], sb2.rearrange("(a n) -> a n", a=1).to_broadcast([P, C])),
                             (b2r[:, :, :].rearrange("p e n -> p (e n)"),
                              b2.rearrange("(a e) n -> a (e n)", a=1).to_broadcast([P, E_ * C]))):
                sp.dma_start(dst, src).then_inc(loaded, 16)
            for e in range(E_):
                sp.dma_start(stage[0][:, e, :, :], w1[e, :, :].rearrange("(k p) n -> p k n", p=P)).then_inc(gated, 16)
            sp.wait_ge(stage_free, 1)
            for e in range(E_):
                sp.dma_start(stage[1][:, e, :, :], w2[e, :, :].rearrange("(f p) n -> p f n", p=P)).then_inc(gated, 16)
            sp.wait_ge(stage_free, 2)
            sp.dma_start(stage[2], sw1.rearrange("(k p) n -> p k n", p=P)).then_inc(gated, 16)
            sp.dma_start(stage[3], sw2.rearrange("(f p) n -> p f n", p=P)).then_inc(gated, 16)
            with sp.Fori(0, B) as b:
                until(sp, tr_done, b, 0)
                sp.dma_start(x2t[:, :, :],
                             x2_dram[bass.ds(b * N, N), :].rearrange("(i p) c -> p i c", p=P)).then_inc(x2_loaded[0], 16)
                until(sp, base_done, b, 0)
                sp.dma_start(h1t[:, :, :],
                             h1_dram[bass.ds(b * N, N), :].rearrange("(i p) c -> p i c", p=P)).then_inc(h1_loaded[0], 16)
                until(sp, base_done, b, NT)
                sp.dma_start(base_dram[bass.ds(b * N, N), :].rearrange("(i p) c -> p i c", p=P),
                             base[:, :, :]).then_inc(base_stored[0], 16)
            with sp.Fori(0, TILES // D) as t:
                for z in range(D):
                    until(sp, c_y, D * t, z + 1)
                    sp.dma_start(y_dram[bass.ds((D * t + z) * P, P), :], yt[:, z, :]).then_inc(c_store[z][0], 16)
            until(sp, base_stored, B, 0)
            with sp.Fori(0, TT // D) as t:
                for z in range(D):
                    until(sp, d_store[z], t, 0)
                    sp.dma_start(bt[:, z, :], base_dram[bass.ds((D * t + z) * P, P), :]).then_inc(d_base[z][0], 16)
                for z in range(D):
                    until(sp, d_done[z], t, 1)
                    sp.dma_start(out[bass.ds((D * t + z) * P, P), :], bt[:, z, :]).then_inc(d_store[z][0], 16)
            for z in range(D):
                until(sp, c_store[z], TILES // D, 0)
                until(sp, d_store[z], TT // D, 0)

        @block.gpsimd
        def _(pool):
            start_at_one(pool, "pool")
            nc.gpsimd.iota(part[:, :], pattern=[[0, 1]], base=0, channel_multiplier=1,
                           allow_small_or_imprecise_dtypes=True).then_inc(set_up, 1)
            nc.gpsimd.memset(ones[:, :], 1.0).then_inc(set_up, 1)
            nc.gpsimd.memset(tok_i[:, TILES:], 0).then_inc(set_up, 1)
            for k, (c0, c1) in enumerate(((0, 1), (1, 2), (2, 7))):
                pool.wait_ge(max_ready, k + 1)
                nc.gpsimd.partition_all_reduce(wall[:, c0:c1], wmax[:, c0:c1], P,
                                               bass.bass_isa.ReduceOp.max).then_inc(all_max, 1)
            pool.wait_ge(loaded, 16 * 8)
            pool.wait_ge(route_dve, 1)
            with pool.Fori(0, B) as b:
                until(pool, h1_loaded, b, 16)
                for f in range(FS):
                    nc.gpsimd.tensor_tensor(h1t[:, f, :], h1t[:, f, :], sb2r[:, :], ALU.add).then_inc(h1b_done[0], 1)
                    until(pool, gelu_done, b, f + 1)
                    nc.gpsimd.tensor_scalar(gp[:, f, 0, :], act_h[:, f % 2, :], hup[:, 1:2], None,
                                            ALU.mult).then_inc(ghi_done[0], 1)

            def gather(t, z):
                nc.gpsimd.tensor_copy(now[:, z:z + 1], tok_i[:, bass.ds(D * t + z, 1)]).then_inc(c_now[0], 1)
                until(pool, c_now, D * t, z + 1)
                nc.gpsimd.indirect_dma_start(
                    out=xg[:, z, :], out_offset=None, in_=x2_dram,
                    in_offset=bass.IndirectOffsetOnAxis(ap=now[:, z:z + 1], axis=0)).then_inc(c_gather[z][0], 16)

            pool.wait_ge(set_up, 3)
            pool.wait_ge(routed, 2)
            for z in range(D):
                gather(0, z)
            with pool.Fori(0, TILES // D) as t:
                for z in range(D):
                    until(pool, c_tr, D * t, z + 1)
                    gather(t + 1, z)
            for z in range(D):
                until(pool, c_store[z], TILES // D, 0)
            with pool.Fori(0, TT // D) as t:
                for z in range(D):
                    until(pool, d_done[z], t, 0)
                    nc.gpsimd.tensor_copy(now2[:, z, :], slot_i[:, :, bass.ds(D * t + z, 1)].rearrange(
                        "p k o -> p (k o)")).then_inc(d_now[0], 1)
                    until(pool, d_now, D * t, z + 1)
                    for k in range(2):
                        nc.gpsimd.indirect_dma_start(
                            out=yg[:, z, k, :], out_offset=None, in_=y_dram,
                            in_offset=bass.IndirectOffsetOnAxis(ap=now2[:, z, k:k + 1], axis=0)
                        ).then_inc(d_gather[z][0], 16)
            for z in range(D):
                pool.wait_ge(c_gather[z][0], 16 * (TILES // D + 1))

        @block.scalar
        def _(act):
            start_at_one(act, "act")
            act.wait_ge(scaled, 1)
            for e in range(E_):
                nc.scalar.activation(weights(ew[:, e, :])[0][:, :, 0, :], stage[0][:, e, :, :], ACT.Copy,
                                     scale=wup[:, 0:1]).then_inc(high_ready, 1)
            act.wait_ge(scaled, 2)
            for e in range(E_):
                nc.scalar.activation(weights(ew[:, e, :])[1][:, :, 0, :], stage[1][:, e, :, :], ACT.Copy,
                                     scale=wup[:, 1:2]).then_inc(high_ready, 1)
            act.wait_ge(scaled, 3)
            for dst, src, col in ((sw1p[:, :, 0, :], stage[2], 2), (sw2p[:, :, 0, :], stage[3], 3), (gwp[:, :, 0, :], stage[4], 4)):
                nc.scalar.activation(dst, src, ACT.Copy, scale=wup[:, col:col + 1]).then_inc(high_ready, 1)
            act.wait_ge(loaded, 16 * 8)
            with act.Fori(0, B) as b:
                for k in (0, 2):
                    until(act, tr_done, b, k + 1)
                    nc.scalar.copy(xT[:, k, :, :].rearrange("p a n -> p (a n)"),
                                   PS[:, k, :].bitcast(F16)).then_inc(xT_even[0], 1)
                for f in range(FS):
                    until(act, up_done, b, f + 1)
                    if f >= 2:
                        until(act, glo_done, b, f - 1)
                    nc.scalar.activation(act_h[:, f % 2, :], PS[:, 4 + f % 2, :], ACT.Gelu, bias=sb1c[:, f:f + 1],
                                         scale=wdown[:, 2:3]).then_inc(gelu_done[0], 1)
            act.wait_ge(routed, 1)
            nc.scalar.activation(exd[:, :], dlt[:, :], ACT.Exp).then_inc(route_act, 1)

            def rows_out(t, z):
                until(act, c_tr, D * t, z + 1)
                nc.scalar.copy(xgT[:, z % 2, :, :, :].rearrange("p k a n -> p (k a n)"),
                               PS[:, z % 2, :].bitcast(F16)).then_inc(c_xT[0], 1)

            def gelus(t, z):
                expert = act.value_load(texp_i[0:1, bass.ds(D * t + z, 1)], min_val=0, max_val=E_ - 1)
                until(act, c_up, D * t, z + 1)
                for f in range(FE):
                    last = nc.scalar.activation(ga[:, z, f, :], PS[:, 2 + z % 2, f * P:(f + 1) * P], ACT.Gelu,
                                                bias=ew[:, bass.ds(expert, 1), WROW - FE + f].bitcast(F32),
                                                scale=wdown[:, 0:1])
                last.then_inc(c_gelu[0], 1)
                until(act, c_gelu, D * t, z + 1)
                nc.scalar.activation(gq[:, z, :, 0, :], ga[:, z, :, :], ACT.Copy, scale=hup[:, 0:1]).then_inc(c_hi[0], 1)

            def step(t, k, first, last):
                if not last or k + 2 < D:
                    rows_out(*tile(t, k + 2))
                if k >= -1 and (not last or k + 1 < D):
                    gelus(*tile(t, k + 1))

            act.wait_ge(routed, 2)
            in_steps(act, step)

        @block.vector
        def _(dve):
            start_at_one(dve, "dve")
            n = [0]

            def link(ins):
                n[0] += 1
                ins.then_inc(vstep, 1)
                dve.wait_ge(vstep, n[0])

            def powers(src, pw):
                link(nc.vector.tensor_scalar(pw, src, 2.0 ** -100, None, ALU.max))
                link(nc.vector.tensor_scalar(pw.bitcast(I32), pw.bitcast(I32), 0x7F800000, None, ALU.bitwise_and))

            def scales(k, c0, c1):
                dve.wait_ge(all_max, k)
                powers(wall[:, c0:c1], wpow[:, c0:c1])
                link(nc.vector.reciprocal(wup[:, c0:c1], wpow[:, c0:c1]))
                link(nc.vector.tensor_scalar(wup[:, c0:c1], wup[:, c0:c1], TOP, None, ALU.mult))
                nc.vector.tensor_scalar(wdown[:, c0:c1], wpow[:, c0:c1], 1.0 / TOP, None, ALU.mult).then_inc(scaled, 1)

            def largest(src, col, axis=mybir.AxisListType.XY):
                return nc.vector.tensor_reduce(wmax[:, col:col + 1], src, axis=axis, op=ALU.max, apply_absolute_value=True)

            dve.wait_ge(loaded, 16 * 8)
            nc.vector.tensor_copy(ident[:, :], identf[:, :])
            nc.vector.tensor_copy(tri[:, :], trif[:, :]).then_inc(cast, 1)
            for k in range(2):
                dve.wait_ge(gated, 16 * E_ * (k + 1))
                largest(big[:, 0:8192], k, AX).then_inc(max_ready, 1)
                scales(k + 1, k, k + 1)
                for e in range(E_):
                    dve.wait_ge(high_ready, k * E_ + e + 1)
                    w = weights(ew[:, e, :])[k]
                    last = nc.vector.scalar_tensor_tensor(w[:, :, 1, :], stage[k][:, e, :, :], wup[:, k:k + 1],
                                                          w[:, :, 0, :], ALU.mult, ALU.subtract)
                last.then_inc(stage_free, 1)
            dve.wait_ge(gated, 16 * (2 * E_ + 2))
            largest(stage[2], 2)
            largest(stage[3], 3)
            largest(stage[4], 4)
            largest(ew[:, :, WROW - FE:WROW].bitcast(F32), 5)
            largest(sb1c[:, :], 6, AX).then_inc(max_ready, 1)
            scales(3, 2, 7)
            for col, (dst, src) in ((2, (sw1p, stage[2])), (3, (sw2p, stage[3])), (4, (gwp, stage[4]))):
                dve.wait_ge(high_ready, 2 * E_ + col - 1)
                last = nc.vector.scalar_tensor_tensor(dst[:, :, 1, :], src, wup[:, col:col + 1], dst[:, :, 0, :],
                                                      ALU.mult, ALU.subtract)
            last.then_inc(stage_free, 1)
            link(nc.vector.scalar_tensor_tensor(hb[:, 0:1], wall[:, 0:1], float(C), wall[:, 5:6], ALU.mult, ALU.add))
            link(nc.vector.scalar_tensor_tensor(hb[:, 1:2], wall[:, 2:3], float(C), wall[:, 6:7], ALU.mult, ALU.add))
            powers(hb[:, :], hpow[:, :])
            link(nc.vector.reciprocal(hup[:, :], hpow[:, :]))
            link(nc.vector.tensor_scalar(hup[:, :], hup[:, :], 2.0 ** 14, None, ALU.mult))
            link(nc.vector.tensor_scalar(hdn[:, :], hpow[:, :], 2.0 ** -14, None, ALU.mult))
            link(nc.vector.tensor_tensor(ydn[:, 0:1], hdn[:, 0:1], wdown[:, 1:2], ALU.mult))
            nc.vector.tensor_tensor(ydn[:, 1:2], hdn[:, 1:2], wdown[:, 3:4], ALU.mult).then_inc(route_dve, 1)
            dve.wait_ge(route_dve, 1)

            with dve.Fori(0, B) as b:
                for k in (1, 3):
                    until(dve, tr_done, b, k + 1)
                    nc.vector.tensor_copy(xT[:, k, :, :].rearrange("p a n -> p (a n)"),
                                          PS[:, k, :].bitcast(F16)).then_inc(xT_odd[0], 1)
                until(dve, lg_done, b, 1)
                nc.vector.tensor_scalar(L[:, bass.ds(b * NT, NT), :], PS[:, 5, 0:NT * E_].rearrange("p (i e) -> p i e", e=E_),
                                        wdown[:, 4:5], None, ALU.mult).then_inc(lg_read[0], 1)
                for f in range(FS):
                    until(dve, ghi_done, b, f + 1)
                    nc.vector.scalar_tensor_tensor(gp[:, f, 1, :], act_h[:, f % 2, :], hup[:, 1:2], gp[:, f, 0, :],
                                                   ALU.mult, ALU.subtract).then_inc(glo_done[0], 1)
                until(dve, base_stored, b, 0)
                for i in range(NT):
                    until(dve, down_done, b, i + 1)
                    until(dve, h1b_done, b, i + 1)
                    nc.vector.scalar_tensor_tensor(base[:, i, :], PS[:, 6 + i % 2, :], ydn[:, 1:2], h1t[:, i, :],
                                                   ALU.mult, ALU.add).then_inc(base_done[0], 1)
            until(dve, lg_read, B, 0)
            dve.wait_ge(set_up, 3)
            def bc(ap):
                return ap.unsqueeze(2).to_broadcast([P, TT, E_])

            for e in range(E_):
                nc.vector.memset(prior[:, e:e + 1], float(E_ - e)).then_inc(vstep, 1)
            n[0] += E_
            dve.wait_ge(vstep, n[0])
            pr = prior[:, :].unsqueeze(1).to_broadcast([P, TT, E_])
            for k, src in enumerate((L, L2)):
                link(nc.vector.tensor_reduce(v12[:, k, :], src[:, :, :], axis=AX, op=ALU.max))
                link(nc.vector.tensor_tensor(eqs[:, :, :], src[:, :, :], bc(v12[:, k, :]), ALU.is_equal))
                link(nc.vector.tensor_tensor(eqs[:, :, :], eqs[:, :, :], pr, ALU.mult))
                link(nc.vector.tensor_reduce(m12[:, k, :], eqs[:, :, :], axis=AX, op=ALU.max))
                link(nc.vector.tensor_tensor(oh[:, k, :, :], eqs[:, :, :], bc(m12[:, k, :]), ALU.is_equal))
                if k == 0:
                    link(nc.vector.scalar_tensor_tensor(L2[:, :, :], oh[:, 0, :, :], MASKED, L[:, :, :], ALU.mult, ALU.add))
            nc.vector.tensor_tensor(dlt[:, :], v12[:, 1, :], v12[:, 0, :], ALU.subtract).then_inc(routed, 1)
            nc.vector.tensor_tensor(both[:, :, :], oh[:, 0, :, :], oh[:, 1, :, :], ALU.add).then_inc(route_dve, 1)
            dve.wait_ge(route_pe, 1)
            link(nc.vector.tensor_copy(pre[:, :, :], PS[:, 0, 0:TT * E_].rearrange("p (t e) -> p t e", e=E_)))
            link(nc.vector.tensor_copy(scan[:, 0, :, :], PS[:, 1, 0:TT * E_].rearrange("p (t e) -> p t e", e=E_)))
            link(nc.vector.tensor_tensor(pre[:, :, :], pre[:, :, :], scan[:, 0, :, :], ALU.subtract))
            cur, d = 0, 1
            while d < TT:
                nc.vector.tensor_copy(scan[:, 1 - cur, 0:d, :], scan[:, cur, 0:d, :])
                link(nc.vector.tensor_tensor(scan[:, 1 - cur, d:, :], scan[:, cur, d:, :], scan[:, cur, 0:TT - d, :], ALU.add))
                cur, d = 1 - cur, 2 * d
            link(nc.vector.tensor_scalar(ntile[:, :], scan[:, cur, TT - 1, :], 1.0 / P, (P - 1.0) / P - 0.5 + 0.5 / P, ALU.mult, ALU.add))
            link(nc.vector.tensor_scalar(nt2[:, :], ntile[:, :], ROUND, ROUND, ALU.add, ALU.subtract))
            link(nc.vector.tensor_copy(tend[:, 0, :], nt2[:, :]))
            tc, d = 0, 1
            while d < E_:
                nc.vector.tensor_copy(tend[:, 1 - tc, 0:d], tend[:, tc, 0:d])
                link(nc.vector.tensor_tensor(tend[:, 1 - tc, d:], tend[:, tc, d:], tend[:, tc, 0:E_ - d], ALU.add))
                tc, d = 1 - tc, 2 * d
            link(nc.vector.tensor_tensor(ntile[:, :], tend[:, tc, :], nt2[:, :], ALU.subtract))
            link(nc.vector.tensor_tensor(posn[:, :, :], pre[:, :, :], scan[:, cur, :, :], ALU.add))
            link(nc.vector.scalar_tensor_tensor(posn[:, :, :], ntile[:, :].unsqueeze(1).to_broadcast([P, TT, E_]), float(P),
                                                posn[:, :, :], ALU.mult, ALU.add))
            for k in range(2):
                link(nc.vector.tensor_tensor(eqs[:, :, :], oh[:, k, :, :], posn[:, :, :], ALU.mult))
                link(nc.vector.tensor_reduce(slot[:, k, :], eqs[:, :, :], axis=AX, op=ALU.add))
            link(nc.vector.tensor_copy(slot_i[:, :, :], slot[:, :, :]))
            link(nc.vector.tensor_scalar(hi[:, :, :], slot[:, :, :], 1.0 / P, 0.5 / P - 0.5, ALU.mult, ALU.add))
            link(nc.vector.tensor_scalar(hi[:, :, :], hi[:, :, :], ROUND, ROUND, ALU.add, ALU.subtract))
            link(nc.vector.scalar_tensor_tensor(lo[:, :, :], hi[:, :, :], -float(P), slot[:, :, :], ALU.mult, ALU.add))
            K2 = 2 * TT
            link(nc.vector.tensor_tensor(lo_hot, lanes[:, :].unsqueeze(1).to_broadcast([P, K2, P]),
                                         lo[:, :, :].rearrange("p k t -> p (k t)").unsqueeze(2).to_broadcast([P, K2, P]), ALU.is_equal))
            link(nc.vector.tensor_tensor(hi_hot[:, :, 1, :], lanes[:, 0:TILES].unsqueeze(1).to_broadcast([P, K2, TILES]),
                                         hi[:, :, :].rearrange("p k t -> p (k t)").unsqueeze(2).to_broadcast([P, K2, TILES]), ALU.is_equal))
            link(nc.vector.tensor_scalar(hi_hot[:, :, 0, :], hi_hot[:, :, 1, :], part[:, 0:1], None, ALU.mult))
            for k in range(2):
                half = hi_hot[:, k * TT:(k + 1) * TT, 1, :]
                last = nc.vector.tensor_tensor(half, half, lanes[:, 0:TT].unsqueeze(2).to_broadcast([P, TT, TILES]), ALU.mult)
            last.then_inc(route_dve, 1)
            link(nc.vector.tensor_tensor(tsel[:, :, 0:E_ - 1], lanes[:, 0:TILES].unsqueeze(2).to_broadcast([P, TILES, E_ - 1]),
                                         tend[:, tc, 0:E_ - 1].unsqueeze(1).to_broadcast([P, TILES, E_ - 1]), ALU.is_ge))
            link(nc.vector.tensor_reduce(texp[:, :], tsel[:, :, 0:E_ - 1], axis=AX, op=ALU.add))
            link(nc.vector.tensor_copy(texp_i[:, :], texp[:, :]))
            dve.wait_ge(route_pe, 2)
            link(nc.vector.tensor_copy(tok_f[:, :], PS[:, 2, 0:TILES]))
            link(nc.vector.scalar_tensor_tensor(tok_f[:, :], PS[:, 2, TILES:2 * TILES], float(P), tok_f[:, :], ALU.mult, ALU.add))
            nc.vector.tensor_copy(tok_i[:, 0:TILES], tok_f[:, :]).then_inc(routed, 1)
            dve.wait_ge(route_act, 1)
            link(nc.vector.tensor_scalar(gate[:, 0, :], exd[:, :], 1.0, None, ALU.add))
            link(nc.vector.reciprocal(gate[:, 0, :], gate[:, 0, :]))
            link(nc.vector.tensor_tensor(gate[:, 1, :], exd[:, :], gate[:, 0, :], ALU.mult))
            dve.wait_ge(routed, 2)

            def load_w(t, z, which, used, tu, zu):
                expert = dve.value_load(texp_i[0:1, bass.ds(D * t + z, 1)], min_val=0, max_val=E_ - 1)
                a, c = ((0, W1N // 2), (W1N // 2, (W1N + W2N) // 2))[which]
                if used is not None:
                    until(dve, used, D * tu, zu + 1)
                nc.vector.tensor_copy(wcur[:, z % 2, a:c], ew[:, bass.ds(expert, 1), a:c].rearrange("p o w -> p (o w)")
                                      ).then_inc((c_w1, c_w2)[which][0], 1)

            def low(t, z):
                until(dve, c_hi, D * t, z + 1)
                nc.vector.scalar_tensor_tensor(gq[:, z, :, 1, :], ga[:, z, :, :], hup[:, 0:1], gq[:, z, :, 0, :],
                                               ALU.mult, ALU.subtract).then_inc(c_lo[0], 1)

            def rows(t, z):
                expert = dve.value_load(texp_i[0:1, bass.ds(D * t + z, 1)], min_val=0, max_val=E_ - 1)
                until(dve, c_down, D * t, z + 1)
                until(dve, c_store[z], t, 0)
                nc.vector.scalar_tensor_tensor(yt[:, z, :], PS[:, 4 + z % 2, :], ydn[:, 0:1],
                                               b2r[:, bass.ds(expert, 1), :].rearrange("p o n -> p (o n)"),
                                               ALU.mult, ALU.add).then_inc(c_y[0], 1)

            def step(t, k, first, last):
                if not last or k + 2 < D:
                    load_w(*tile(t, k + 2), 0, None if k < 0 else c_up, *tile(t, k))
                if k >= 0 and (not last or k < D):
                    low(*tile(t, k))
                if k >= 1:
                    rows(*tile(t, k - 1))
                if k >= -1 and (not last or k + 1 < D):
                    load_w(*tile(t, k + 1), 1, None if k < 1 else c_down, *tile(t, k - 1))

            in_steps(dve, step)

            with dve.Fori(0, TT // D) as t:
                for z in range(D):
                    until(dve, d_gather[z], t, 32)
                    until(dve, d_base[z], t, 16)
                    nc.vector.scalar_tensor_tensor(bt[:, z, :], yg[:, z, 0, :], gate[:, 0, bass.ds(D * t + z, 1)],
                                                   bt[:, z, :], ALU.mult, ALU.add).then_inc(d_acc[0], 1)
                    until(dve, d_acc, D * t, z + 1)
                    nc.vector.scalar_tensor_tensor(bt[:, z, :], yg[:, z, 1, :], gate[:, 1, bass.ds(D * t + z, 1)],
                                                   bt[:, z, :], ALU.mult, ALU.add).then_inc(d_done[z][0], 1)

        @block.tensor
        def _(pe):
            start_at_one(pe, "pe")
            PAIRS = ((0, 0), (0, 1), (1, 0))
            pe.wait_ge(set_up, 3)
            pe.wait_ge(cast, 1)
            pe.wait_ge(stage_free, 3)
            with pe.Fori(0, B) as b:
                until(pe, x2_loaded, b, 16)
                for k in range(KT):
                    for i in range(NT):
                        for a in range(2):
                            last = nc.tensor.transpose(PS[:, k, :].bitcast(F16)[:, a * N + i * P:a * N + (i + 1) * P],
                                                       x2t[:, i, a * C + k * P:a * C + (k + 1) * P], ident[:, :])
                    last.then_inc(tr_done[0], 1)
                until(pe, xT_even, b, 2)
                until(pe, xT_odd, b, 2)
                until(pe, gelu_done, b, 0)
                for i in range(NT):
                    m = 0
                    for k in range(KT):
                        for xa, wa in PAIRS:
                            last = nc.tensor.matmul(PS[:, 5, i * E_:(i + 1) * E_], xT[:, k, xa, i * P:(i + 1) * P],
                                                    gwp[:, k, wa, :], start=(m == 0), stop=(m == 3 * KT - 1))
                            m += 1
                last.then_inc(lg_done[0], 1)
                for f in range(FS):
                    if f == 1:
                        until(pe, lg_read, b, 1)
                    if f >= 2:
                        until(pe, gelu_done, b, f - 1)
                    m = 0
                    for k in range(KT):
                        for xa, wa in PAIRS:
                            last = nc.tensor.matmul(PS[:, 4 + f % 2, :], sw1p[:, k, wa, f * P:(f + 1) * P], xT[:, k, xa, :],
                                                    start=(m == 0), stop=(m == 3 * KT - 1))
                            m += 1
                    last.then_inc(up_done[0], 1)
                until(pe, glo_done, b, FS)
                for i in range(NT):
                    if i < 2:
                        until(pe, base_done, b, 0)
                    else:
                        until(pe, base_done, b, i - 1)
                    m = 0
                    for f in range(FS):
                        for ga_, wa in PAIRS:
                            last = nc.tensor.matmul(PS[:, 6 + i % 2, :], gp[:, f, ga_, i * P:(i + 1) * P], sw2p[:, f, wa, :],
                                                    start=(m == 0), stop=(m == 3 * FS - 1))
                            m += 1
                    last.then_inc(down_done[0], 1)
            pe.wait_ge(route_dve, 2)
            te = both[:, :, :].rearrange("p t e -> p (t e)")
            nc.tensor.matmul(PS[:, 0, 0:TT * E_], tri[:, :], te, start=True, stop=True)
            nc.tensor.matmul(PS[:, 1, 0:TT * E_], ones[:, :], te, start=True, stop=True).then_inc(route_pe, 1)
            pe.wait_ge(route_dve, 3)
            for m in range(2 * TT):
                last = nc.tensor.matmul(PS[:, 2, 0:2 * TILES], lo_hot[:, m, :], hi_hot[:, m, :, :].rearrange("p a m -> p (a m)"),
                                        start=(m == 0), stop=(m == 2 * TT - 1))
            last.then_inc(route_pe, 1)
            pe.wait_ge(routed, 2)

            def turn(t, z):
                until(pe, c_gather[z], t, 16)
                for k in range(KT):
                    for a in range(2):
                        q = (2 * k + a) * P
                        last = nc.tensor.transpose(PS[:, z % 2, :].bitcast(F16)[:, q:q + P],
                                                   xg[:, z, a * C + k * P:a * C + (k + 1) * P], ident[:, :])
                last.then_inc(c_tr[0], 1)

            def up(t, z, fresh):
                w1v = weights(wcur[:, z % 2, :])[0]
                until(pe, c_xT, D * t, z + 1)
                until(pe, c_w1, D * t, z + 1)
                if not fresh:
                    until(pe, c_gelu, D * t, z - 1)
                for f in range(FE):
                    m = 0
                    for k in range(KT):
                        for xa, wa in PAIRS:
                            last = nc.tensor.matmul(PS[:, 2 + z % 2, f * P:(f + 1) * P], w1v[:, k, wa, f * P:(f + 1) * P],
                                                    xgT[:, z % 2, k, xa, :], start=(m == 0), stop=(m == 3 * KT - 1))
                            m += 1
                last.then_inc(c_up[0], 1)

            def down(t, z):
                w2v = weights(wcur[:, z % 2, :])[1]
                until(pe, c_lo, D * t, z + 1)
                until(pe, c_w2, D * t, z + 1)
                m = 0
                for f in range(FE):
                    for ga_, wa in PAIRS:
                        last = nc.tensor.matmul(PS[:, 4 + z % 2, :], gq[:, z, f, ga_, :], w2v[:, f, wa, :],
                                                start=(m == 0), stop=(m == 3 * FE - 1))
                        m += 1
                last.then_inc(c_down[0], 1)

            def step(t, k, first, last):
                if not last or k + 2 < D:
                    turn(*tile(t, k + 2))
                if k >= -1 and (not last or k + 1 < D):
                    up(*tile(t, k + 1), k < 1)
                if k >= 1:
                    down(*tile(t, k - 1))

            in_steps(pe, step)


def kernel(**inputs):
    import numpy as _np
    import concourse.bacc as _bacc
    from concourse import mybir as _mybir
    from concourse.bass_utils import run_bass_kernel_spmd as _run

    t = {k.replace("L0_", ""): _np.asarray(v) for k, v in inputs.items()}
    depth = CH // 2
    pos = _np.arange(T, dtype=_np.float32)[:, None]
    rate = (1.0 / _np.power(_np.float32(10000.0), _np.arange(depth, dtype=_np.float32)[None, :] / _np.float32(depth))).astype(_np.float32)
    ang = (pos * rate).astype(_np.float32)
    tri = _np.triu(_np.ones((P, P), _np.float32), 1) * _np.float32(MASKED)
    arrays = {
        "ids": t["x"].reshape(B * NT, P).T,
        "emb": t["tok_emb_table"],
        "pe_tab": _np.concatenate([_np.sin(ang), _np.cos(ang)], axis=1).astype(_np.float32),
        "conv_w": t["tok_conv_w"].transpose(1, 2, 0),
        "conv_b": t["tok_conv_b"].reshape(CH, 1),
        "spos0": t["tok_spos0"],
        "spos1": t["tok_spos1"],
        "wqkv": t["attn_w_qkv"].T,
        "wproj": t["attn_w_proj"].T,
        "gate_w": t["ffn_gate_w"],
        "w1": t["ffn_w1"],
        "b1": t["ffn_b1"].reshape(E_, HID // P, P).transpose(2, 0, 1),
        "w2": t["ffn_w2"],
        "b2": t["ffn_b2"],
        "sw1": t["ffn_shared_w1"],
        "sb1": t["ffn_shared_b1"].reshape(SH // P, P).T,
        "sw2": t["ffn_shared_w2"],
        "sb2": t["ffn_shared_b2"],
        "ident_in": _np.eye(P, dtype=_np.float32),
        "mask_in": tri,
        "maskT_in": tri.T,
        "tri_in": _np.triu(_np.ones((P, P), _np.float32), 1),
        "lanes_in": _np.tile(_np.arange(P, dtype=_np.float32), (P, 1)),
    }
    nc = _bacc.Bacc("TRN2", target_bir_lowering=False, num_devices=1)
    sent, args = {}, []
    for name, a in arrays.items():
        a = _np.ascontiguousarray(a)
        sent[f"in_{name}"] = a
        args.append(nc.dram_tensor(f"in_{name}", a.shape, _mybir.dt.from_np(a.dtype), kind="ExternalInput").ap())
    args.append(nc.dram_tensor("out_h", (B * N, C), _mybir.dt.float32, kind="ExternalOutput").ap())
    build(nc, *args)
    r = _run(nc, [sent], core_ids=[0])
    return r.results[0]["out_h"].reshape(B, N, C)
```

```python
from contextlib import ExitStack

import numpy as np

import concourse.bass as bass
from concourse import mybir

P = 128
ALU = mybir.AluOpType
ACT = mybir.ActivationFunctionType
AX = mybir.AxisListType.X
F32 = mybir.dt.float32
F16 = mybir.dt.float16
BF16 = mybir.dt.bfloat16
I32 = mybir.dt.int32

B, T = 8, 512
CH = 128
N = 4 * CH
C = T
H, DH = 16, 32
NT, KT = N // P, C // P
G, HG = 4, 4
E_, HID = 8, 256
SH = 512
TAPS = 3
PAD = TAPS - 1
EPS = 1e-5
QMAX = 127.0
CLIP = 1e-5
ROUND = 1.5 * 2.0 ** 23
MASKED = -(2.0 ** 100)
ATT_SCALE = DH ** -0.5
KPARTS = 3 * DH
MROWS = 5
MUNIT = 2.0 ** 15


def build(nc, ids, emb, pe_tab, conv_w, conv_b, spos0, spos1, wqkv, wproj, gate_w, w1, b1, w2, b2,
          sw1, sb1, sw2, sb2, ident_in, mask_in, maskT_in, tri_in, lanes_in, out):
    h1_dram = nc.dram_tensor("h1_rows", [B * N, C], F32, kind="Internal").ap()
    x2_dram = nc.dram_tensor("x2_rows", [B * N, 2 * C], F16, kind="Internal").ap()
    qk_dram = nc.dram_tensor("qk_rows", [2, DH, 2 * 2 * 2, HG, N], F16, kind="Internal").ap()
    with ExitStack() as ctx:
        big = ctx.enter_context(nc.sbuf_tensor("big", [P, 8704], F32))
        gws = ctx.enter_context(nc.sbuf_tensor("f_gws", [P, KT, E_], F32))
        sb1c = ctx.enter_context(nc.sbuf_tensor("f_sb1c", [P, SH // P], F32))
        wmax = ctx.enter_context(nc.sbuf_tensor("f_wmax", [P, 4], F32))
        sw_loaded = ctx.enter_context(nc.semaphore("sw_loaded"))
        max_ready = ctx.enter_context(nc.semaphore("max_ready"))
        stage_sw1 = big[:, 0:KT * SH].rearrange("p (k n) -> p k n", k=KT)
        stage_sw2 = big[:, KT * SH:KT * SH + SH // P * C].rearrange("p (f n) -> p f n", f=SH // P)
        ahead = ((stage_sw1, sw1.rearrange("(k p) n -> p k n", p=P)),
                 (stage_sw2, sw2.rearrange("(f p) n -> p f n", p=P)),
                 (gws[:, :, :], gate_w.rearrange("(k p) e -> p k e", p=P)), (sb1c[:, :], sb1))
        attention_phase(nc, ids, emb, pe_tab, conv_w, conv_b, spos0, spos1, wqkv, wproj,
                        ident_in, mask_in, maskT_in, h1_dram, x2_dram, qk_dram, big, ahead, wmax, sw_loaded, max_ready)
        ffn_phase(nc, ident_in, tri_in, lanes_in, gate_w, w1, b1, w2, b2, sw1, sb1, sw2, sb2, h1_dram, x2_dram, out,
                  big, gws, sb1c, wmax, sw_loaded, max_ready)


def attention_phase(nc, ids, emb, pe_tab, conv_w, conv_b, spos0, spos1, wqkv, wproj,
                    ident_in, mask_in, maskT_in, h1_dram, x2_dram, qk_dram, big, ahead_loads, wmax, sw_loaded, max_ready):
    ctx = ExitStack()
    with ctx:
        def sb(name, shape, dt):
            return ctx.enter_context(nc.sbuf_tensor(name, shape, dt))

        def ps(name, shape, dt):
            return ctx.enter_context(nc.psum_tensor(name, shape, dt))

        def sem(name):
            return ctx.enter_context(nc.semaphore(name))

        idx = sb("idx", [P, B * NT], I32)
        emb_all = sb("emb_all", [P, B * NT, CH], F32)
        pe_tm = sb("pe_tm", [P, NT, CH], F32)
        convw = sb("convw", [P, TAPS, CH], F32)
        convb = sb("convb", [P, 1], F32)
        sp0 = sb("sp0", [P, CH], F32)
        sp1 = sb("sp1", [P, CH], F32)
        ident = sb("ident", [P, P], F32)
        identb = sb("identb", [P, P], BF16)
        identh = sb("identh", [P, P], F16)
        maskf = sb("maskf", [P, 2, P], F32)
        maskb = sb("maskb", [P, 2, P], BF16)
        ones = sb("ones", [P, P], F32)
        neghalf = sb("neghalf", [P, NT], F32)
        wstage = sb("wstage", [P, KT, 4 * C], F32)
        wq = sb("wq", [P, KT, 4 * C], BF16)
        wsum = sb("wsum", [P, 2 * KT], F32)
        wtot = sb("wtot", [P, 2], F32)
        wmean = sb("wmean", [P, 2], F32)
        winv = sb("winv", [P, 2], F32)
        escale = sb("escale", [P, 1], F32)

        x_tm = sb("x_tm", [P, NT, CH], F32)
        cmax = sb("cmax", [P, NT], F32)
        tmp4 = sb("tmp4", [P, NT], F32)
        xs = sb("xs", [P, NT, CH], F32)
        csum = sb("csum", [P, NT], F32)
        crec = sb("crec", [P, NT], F32)
        selT = sb("selT", [P, T], F32)
        h = sb("h", [P, NT, PAD + C], F32)

        class Rows:
            def __init__(self, tag, hc):
                self.stats = sb(tag + "stats", [P, NT, 6], F32)
                self.mv = sb(tag + "mv", [P, NT, 2], F32)
                self.vare = sb(tag + "vare", [P, NT], F32)
                self.rstd = sb(tag + "rstd", [P, NT], F32)
                self.negmean = sb(tag + "negmean", [P, NT], F32)
                self.hc = hc
                self.amax = sb(tag + "amax", [P, NT], F32)
                self.aval = sb(tag + "aval", [P, NT], F32)
                self.arec = sb(tag + "arec", [P, NT], F32)
                self.astep = sb(tag + "astep", [P, NT], F32)
                self.fscale = sb(tag + "fscale", [P, NT], F32)
                self.xqi = sb(tag + "xqi", [P, NT, C], BF16)
                self.xqT = sb(tag + "xqT", [P, KT, N], BF16)

        fr = Rows("f", sb("fhc", [P, NT, C], F32))
        bk = Rows("b", wstage[:, 2, :].rearrange("p (r c) -> p r c", r=NT))
        vstep = sb("vstep", [P, NT], F32)
        abc = sb("abc", [P, N], F32)
        diag = sb("diag", [P, NT, P], F32)

        qk32 = sb("qk32", [P, 2, N], F32)
        parts = sb("parts", [P, 2, 2, 2, 2, N], F16)
        QS, KS = (big[:, w * G * HG * N // 2:(w + 1) * G * HG * N // 2].bitcast(F16).rearrange(
            "p (g j n) -> p g j n", g=G, j=HG) for w in range(2))
        V = sb("V", [P, NT, C], F32)
        mx = sb("mx", [P, 2, NT, HG], F32)
        mh = sb("mh", [P, NT, HG], F16)
        mr = sb("mr", [P, NT, HG], F32)
        mr2 = sb("mr2", [P, NT, HG], F32)
        mm = sb("mm", [P, NT, HG, DH], F16)
        mT = sb("mT", [P, N], F16)
        pT = sb("pT", [P, 2, HG, N], F32)
        head_of = sb("head_of", [P, G, DH], F32)
        den = sb("den", [P, N], F32)
        rden = sb("rden", [P, NT, HG, G], F32)
        oT = wstage[:, 3, :].rearrange("p (g n) -> p g n", g=G)

        h1 = wstage[:, 0, :].rearrange("p (r c) -> p r c", r=NT)
        x2 = wstage[:, 1, :].rearrange("p (r c) -> p r c", r=NT)
        x2p = sb("x2p", [P, NT, 2, C], F16)

        ps_s1 = ps("ps_s1", [P, 2, 512], F32)
        ps_s2 = ps("ps_s2", [P, 2, 512], F32)
        ps_o = ps("ps_o", [P, 512], F32)
        ps_den = ps("ps_den", [P, 512], F32)
        ps_f = ps("ps_f", [P, 512], F32)
        ps_b = ps("ps_b", [P, 512], F32)

        loaded = sem("loaded")
        w_loaded = sem("w_loaded")
        gathered = [sem("gathered_%s" % what) for what in ("first", "second", "rest")]
        consts_set = sem("consts_set")
        idents_cast = sem("idents_cast")
        w_step = sem("w_step")
        passed = sem("passed")
        w_summed = sem("w_summed")
        w_ready = sem("w_ready")

        def signal(name, per, giver):
            given[giver].append(sem(name))
            return given[giver][-1], per

        given = {"pe": [], "act": [], "dve": [], "pool": [], "sp": []}
        t_full = signal("t_full", 7, "pe")
        q_full = signal("q_full", 3 + 2 * G, "pe")
        v_full = signal("v_full", NT, "pe")
        vstep_ready = signal("vstep_ready", 1, "dve")
        parts_out = signal("parts_out", 16 * 2 * HG, "sp")
        x_ready = signal("x_ready", 1, "dve")
        xs_ready = signal("xs_ready", 2, "dve")
        ex_ready = signal("ex_ready", 2, "act")
        sel_ready = signal("sel_ready", 2, "dve")
        selT_ready = signal("selT_ready", 2, "dve")
        h_ready = signal("h_ready", NT, "act")
        h_kept = signal("h_kept", 16, "sp")
        h_fetched = signal("h_fetched", 16, "sp")
        tok_step = signal("tok_step", 6, "dve")
        fr_step = signal("fr_step", NT + 1 + 4, "dve")
        bk_step = signal("bk_step", NT + 1 + 3, "dve")
        den_ready = signal("den_ready", 1, "act")
        bd_ready = signal("bd_ready", 1, "dve")
        part_step = signal("part_step", 2 * G, "act")
        max_step = signal("max_step", 3 * G, "pool")
        x2_step = signal("x2_step", NT, "act")
        fvar_ready = signal("fvar_ready", 1, "dve")
        frstd_ready = signal("frstd_ready", 1, "pool")
        fc_ready = signal("fc_ready", NT, "act")
        ff_ready = signal("ff_ready", 1, "dve")
        fq_ready = signal("fq_ready", NT, "act")
        fi_ready = signal("fi_ready", NT, "act")
        fT_ready = signal("fT_ready", 2, "act")
        diag_ready = signal("diag_ready", 1, "dve")
        abc_ready = signal("abc_ready", 1, "act")
        qk32_ready = signal("qk32_ready", 2 * G, "dve")
        parts_ready = signal("parts_ready", 2 * G, "pool")
        v_ready = signal("v_ready", NT, "act")
        stacked = [signal("stacked0", 16 * 6, "sp"), signal("stacked1", 16 * 6, "sp")]
        s1_ready = signal("s1_ready", 32, "pe")
        s1_read = signal("s1_read", 32, "dve")
        mm_ready = signal("mm_ready", G, "pool")
        m_full = signal("m_full", G, "pe")
        mT_ready = signal("mT_ready", G, "act")
        m_stacked = signal("m_stacked", 16 * G * HG, "sp")
        s2_ready = signal("s2_ready", 32, "pe")
        p_ready = signal("p_ready", 32, "act")
        pv_done = signal("pv_done", 16, "pe")
        o_ready = signal("o_ready", G, "act")
        back_full = signal("back_full", 11, "pe")
        bc_ready = signal("bc_ready", NT, "dve")
        bf_ready = signal("bf_ready", 1, "dve")
        bq_ready = signal("bq_ready", NT, "act")
        bi_ready = signal("bi_ready", NT, "act")
        bT_ready = signal("bT_ready", 2, "act")
        h1_ready = signal("h1_ready", NT, "dve")
        bvar_ready = signal("bvar_ready", 1, "dve")
        brstd_ready = signal("brstd_ready", 1, "pool")
        x2_ready = signal("x2_ready", NT, "dve")
        x2p_ready = signal("x2p_ready", NT, "pool")
        h1_stored = signal("h1_stored", 16 * NT, "sp")
        x2_stored = signal("x2_stored", 16 * NT, "sp")

        def start_at_one(eng, giver):
            for s in given[giver]:
                eng.sem_inc(s, 1)

        def until(eng, signal, b, k):
            s, per = signal
            eng.wait_ge(s, b * per + k + 1)
            if eng in (nc.gpsimd, nc.sync) and not isinstance(b, int):
                eng.sem_inc(passed, 1)

        T_XT, T_CONV, T_SELT0, T_EXT0, T_CONVT, T_SELT1, T_EXT1 = range(7)
        T_DRAINED = ((h_ready, 1), (h_ready, 2), (selT_ready, 1), (h_ready, 3), (xs_ready, 2), (selT_ready, 2),
                     (h_ready, 4))
        Q_IT, Q_ABC, Q_QK = 0, 2, 3
        Q_DRAINED = [(fT_ready, 1), (fT_ready, 2), (abc_ready, 1)] + [(qk32_ready, n + 1) for n in range(2 * G)]
        B_DEN, B_OT, B_QT, B_PROJ = 0, 1, 1 + NT, 3 + NT
        B_DRAINED = [(bd_ready, 1)] + [(bc_ready, n + 1) for n in range(NT)] + [(bT_ready, 1), (bT_ready, 2)] \
            + [(h1_ready, n + 1) for n in range(NT)]
        H_ORDER = (0, 2, 1, 3)
        LEAD = 6

        def sequences(eng, prepare, finish, maxima_at, scores_at, v_at, q_at, tokens_at, back_at, group_at):
            def ahead(b, k):
                return b + k // 16, k % 16 // NT, k % NT

            def one(b, tokens, front, back):
                for hs in range(32):
                    s, q = hs // 2, hs % 2
                    if front or s + LEAD < 16:
                        maxima_at(*ahead(b, s + LEAD), q)
                    scores_at(b, s, q)
                    v_at(b, hs)
                    if back:
                        back_at(b - 1, hs, False)
                    if front:
                        q_at(b + 1, hs)
                    if tokens:
                        tokens_at(b + 2, hs)
                    if hs % 8 == (3 if eng is nc.gpsimd else 5) and (front or hs < 24):
                        group_at(b + (hs // 8 + 1) // G, (hs // 8 + 1) % G, back)

            for hs in range(32):
                tokens_at(0, hs)
                prepare(hs)
            for hs in range(32):
                q_at(0, hs)
            for hs in range(32):
                tokens_at(1, hs)
                k = hs - 20
                if k in range(2 * LEAD):
                    maxima_at(*ahead(0, k // 2), k % 2)
                if k == 2 * NT + 1:
                    group_at(0, 0, False)
            one(0, True, True, False)
            with eng.Fori(1, B - 2) as b:
                one(b, True, True, True)
            one(B - 2, False, True, True)
            one(B - 1, False, False, True)
            scores_at(B, 0, 0, True)
            for hs in range(1, 32):
                if hs == 1:
                    scores_at(B, 0, 1, True)
                    finish(0)
                back_at(B - 1, hs, True)
                if hs == 9:
                    finish(1)

        def nothing(k):
            pass

        def at_start(b):
            return isinstance(b, int) and b == 0

        block = ctx.enter_context(nc.Block())

        @block.sync
        def _(sp):
            start_at_one(sp, "sp")
            for dst, src in ((idx[:, :], ids), (ident[:, :], ident_in), (maskf[:, 0, :], mask_in),
                             (maskf[:, 1, :], maskT_in),
                             (pe_tm[:, :, :], pe_tab.rearrange("(t p) c -> p t c", p=P)),
                             (sp0[:, :], spos0), (sp1[:, :], spos1), (convw[:, :, :], conv_w), (convb[:, :], conv_b)):
                sp.dma_start(dst, src).then_inc(loaded, 16)
            sp.dma_start(wstage[:, :, 0:3 * C], wqkv.rearrange("(k p) o -> p k o", p=P)).then_inc(w_loaded, 16)
            sp.dma_start(wstage[:, :, 3 * C:], wproj.rearrange("(k p) o -> p k o", p=P)).then_inc(w_loaded, 16)

            def load_ahead(k):
                if k == 0:
                    until(sp, s2_ready, B - 1, 32)
                    for dst, src in ahead_loads:
                        sp.dma_start(dst, src).then_inc(sw_loaded, 16)

            def prepare(hs):
                pass

            def spread(b, half):
                until(sp, parts_ready, b, G * (half + 1))
                if not at_start(b):
                    until(sp, stacked[half], b - 1, stacked[half][1])
                for j in range(HG):
                    sp.dma_start(qk_dram[half, :, :, j, :],
                                 parts[DH * j:DH * j + DH, half, :, :, :, :].rearrange("d w a g n -> d (w a g) n")
                                 ).then_inc(parts_out[0], 16)

            def stack(b, half):
                until(sp, parts_out, b, 16 * HG * (half + 1))
                if not at_start(b):
                    until(sp, s2_ready, b - 1, 16 * (half + 1))
                for st, w, order in ((QS, 0, (0, 0, 1)), (KS, 1, (0, 1, 0))):
                    for r, part in enumerate(order):
                        sp.dma_start(st[DH * r:DH * r + DH, 2 * half:2 * half + 2, :, :],
                                     qk_dram[half, :, 4 * w + 2 * part:4 * w + 2 * part + 2, :, :]
                                     ).then_inc(stacked[half][0], 16)

            def rows_of(b):
                return h1_dram[bass.ds(b * N, N), :].rearrange("(r p) c -> p r c", p=P)

            def maxima_at(b, g, i, q):
                pass

            def scores_at(b, s, q, tail=False):
                pass

            def v_at(b, hs):
                pass

            def q_at(b, hs):
                if hs == 14:
                    spread(b, 0)
                if hs == 16:
                    stack(b, 0)
                if hs == 18:
                    spread(b, 1)
                if hs == 31:
                    stack(b, 1)

            def tokens_at(b, hs):
                if hs == 27:
                    until(sp, h_ready, b, NT)
                    sp.dma_start(rows_of(b), h[:, :, PAD:]).then_inc(h_kept[0], 16)

            def group_at(b, g, back):
                until(sp, mT_ready, b, g + 1)
                for j in range(HG):
                    sp.dma_start(QS[KPARTS:KPARTS + MROWS, g, j, :],
                                 mT[DH * j:DH * j + MROWS, :]).then_inc(m_stacked[0], 16)

            def back_at(b, hs, alone):
                if hs == 1:
                    until(sp, h_kept, b, 16)
                    if at_start(b):
                        sp.wait_ge(w_ready, 2 * KT)
                    else:
                        until(sp, h1_stored, b - 1, 16 * NT)
                    sp.dma_start(h1[:, :, :], rows_of(b)).then_inc(h_fetched[0], 16)
                if hs in range(15, 19):
                    i = hs - 15
                    until(sp, h1_ready, b, i + 1)
                    sp.dma_start(h1_dram[bass.ds(b * N + i * P, P), :], h1[:, i, :]).then_inc(h1_stored[0], 16)
                if hs in range(22, 26):
                    i = hs - 22
                    until(sp, x2p_ready, b, i + 1)
                    sp.dma_start(x2_dram[bass.ds(b * N + i * P, P), :],
                                 x2p[:, i, :, :].rearrange("p a c -> p (a c)")).then_inc(x2_stored[0], 16)

            sequences(sp, prepare, load_ahead, maxima_at, scores_at, v_at, q_at, tokens_at, back_at, group_at)
            until(sp, h1_stored, B - 1, h1_stored[1])
            until(sp, x2_stored, B - 1, x2_stored[1])

        @block.gpsimd
        def _(pool):
            start_at_one(pool, "pool")
            nc.gpsimd.memset(neghalf[:, :], -0.5).then_inc(consts_set, 1)
            nc.gpsimd.memset(ones[:, :], 1.0).then_inc(consts_set, 1)
            nc.gpsimd.memset(h[:, :, 0:PAD], 0.0).then_inc(consts_set, 1)
            nc.gpsimd.memset(mm[:, :, :, :], 0.0).then_inc(consts_set, 1)
            pool.wait_ge(consts_set, 4)
            nc.gpsimd.memset(KS[KPARTS:P, :, :, :], MUNIT).then_inc(consts_set, 1)
            pool.wait_ge(consts_set, 5)
            nc.gpsimd.memset(head_of[:, :, :], 0.0).then_inc(consts_set, 1)
            pool.wait_ge(consts_set, 6)
            for g in range(G):
                nc.gpsimd.memset(head_of[:, g, g:g + 1], 1.0).then_inc(consts_set, 1)
            pool.wait_ge(loaded, 16 * 9)

            def embed(tiles, done):
                for t in tiles:
                    nc.gpsimd.indirect_dma_start(
                        out=emb_all[:, t, :], out_offset=None, in_=emb,
                        in_offset=bass.IndirectOffsetOnAxis(ap=idx[:, t:t + 1], axis=0)).then_inc(done, 16)

            embed(range(NT), gathered[0])
            embed(range(NT, 2 * NT), gathered[1])

            def prepare(hs):
                pass

            def rsqrt(rows, asked, given_, b):
                until(pool, asked, b, 1)
                nc.gpsimd.tensor_tensor(rows.rstd[:, :], rows.vare[:, :], neghalf[:, :], ALU.pow).then_inc(given_[0], 1)

            def parts_of(b, n):
                g, w = n // 2, n % 2
                until(pool, part_step, b, n + 1)
                nc.gpsimd.tensor_tensor(parts[:, g // 2, w, 1, g % 2, :], qk32[:, w, :], parts[:, g // 2, w, 0, g % 2, :],
                                        ALU.subtract).then_inc(parts_ready[0], 1)

            def maxima_at(b, g, i, q):
                pass

            def scores_at(b, s, q, tail=False):
                pass

            def v_at(b, hs):
                pass

            def group_at(b, g, back):
                until(pool, s1_read, b, 8 * g + 8)
                m = mx[:, g % 2, :, :]
                nc.gpsimd.tensor_scalar(mh[:, :, :], m, -1.0 / (4 * MUNIT), None, ALU.mult).then_inc(max_step[0], 1)
                until(pool, max_step, b, 3 * g + 1)
                nc.gpsimd.tensor_scalar(mr[:, :, :], mh[:, :, :], -4.0 * MUNIT, None, ALU.mult).then_inc(max_step[0], 1)
                until(pool, max_step, b, 3 * g + 2)
                nc.gpsimd.tensor_tensor(mr2[:, :, :], mr[:, :, :], m, ALU.subtract).then_inc(max_step[0], 1)
                until(pool, max_step, b, 3 * g + 3)
                until(pool, m_full, b, g)
                nc.gpsimd.tensor_scalar(mm[:, :, :, 4], mr2[:, :, :], 1.0 / MUNIT, None, ALU.mult)
                nc.gpsimd.tensor_copy(mm[:, :, :, 0:4],
                                      mh[:, :, :].unsqueeze(3).to_broadcast([P, NT, HG, 4])).then_inc(mm_ready[0], 1)

            def tokens_at(b, hs):
                if hs == 26:
                    rsqrt(fr, fvar_ready, frstd_ready, b)

            def q_at(b, hs):
                if hs in range(8, 8 + 2 * G):
                    parts_of(b, hs - 8)
                if hs == 31 and at_start(b):
                    embed(range(2 * NT, B * NT), gathered[2])

            def halves(b, r):
                until(pool, x2_step, b, r + 1)
                nc.gpsimd.tensor_tensor(x2p[:, r, 1, :], x2[:, r, :], x2p[:, r, 0, :],
                                        ALU.subtract).then_inc(x2p_ready[0], 1)

            def back_at(b, hs, alone):
                if hs == 19:
                    rsqrt(bk, bvar_ready, brstd_ready, b)
                if hs in range(22, 26):
                    halves(b, hs - 22)

            sequences(pool, prepare, nothing, maxima_at, scores_at, v_at, q_at, tokens_at, back_at, group_at)

        @block.scalar
        def _(act):
            start_at_one(act, "act")
            act.wait_ge(consts_set, 6 + G)
            act.wait_ge(loaded, 16 * 9)

            def prepare(hs):
                pass

            def full(b, u):
                until(act, t_full, b, u + 1)

            def exps(b, use):
                until(act, xs_ready, b, use + 1)
                nc.scalar.activation(xs[:, :, :], xs[:, :, :], ACT.Exp).then_inc(ex_ready[0], 1)

            def to_integers(rows, rounded, given_, b, rs):
                for r in rs:
                    until(act, rounded, b, r + 1)
                    nc.scalar.activation(rows.xqi[:, r, :], rows.hc[:, r, :], ACT.Copy,
                                         bias=-ROUND).then_inc(given_[0], 1)

            def integers_out(rows, half, bank, given_):
                nc.scalar.copy(rows.xqT[:, 2 * half:2 * half + 2, :].rearrange("p k n -> p (k n)"),
                               bank[:, :].bitcast(BF16)).then_inc(given_[0], 1)

            def tokens_at(b, hs):
                if hs == 16:
                    full(b, T_XT)
                    if not at_start(b):
                        until(act, h_kept, b - 1, 16)
                    nc.scalar.copy(h[:, 0, PAD:], ps_f[:, :]).then_inc(h_ready[0], 1)
                if hs == 17:
                    exps(b, 0)
                if hs == 18:
                    full(b, T_CONV)
                    nc.scalar.activation(h[:, 2, PAD:], ps_f[:, :], ACT.Identity,
                                         bias=convb[:, 0:1]).then_inc(h_ready[0], 1)
                if hs in (20, 25):
                    full(b, (T_EXT0, T_EXT1)[hs // 25])
                    nc.scalar.copy(h[:, (1, 3)[hs // 25], PAD:], ps_f[:, :]).then_inc(h_ready[0], 1)
                if hs == 22:
                    exps(b, 1)
                if hs in (27, 28):
                    if hs == 27:
                        until(act, fvar_ready, b, 1)
                    for r in range(2 * hs - 54, 2 * hs - 52):
                        nc.scalar.activation(fr.hc[:, r, :], h[:, r, PAD:], ACT.Identity,
                                             bias=fr.negmean[:, r:r + 1]).then_inc(fc_ready[0], 1)

            def q_at(b, hs):
                if hs in (1, 2):
                    if hs == 1:
                        until(act, ff_ready, b, 1)
                    for r in range(2 * hs - 2, 2 * hs):
                        nc.scalar.activation(fr.hc[:, r, :], fr.hc[:, r, :], ACT.Copy, bias=ROUND,
                                             scale=fr.fscale[:, r:r + 1]).then_inc(fq_ready[0], 1)
                if hs in (2, 3):
                    to_integers(fr, fq_ready, fi_ready, b, range(2 * hs - 4, 2 * hs - 2))
                if hs in (5, 6):
                    until(act, q_full, b, Q_IT + hs - 5 + 1)
                    integers_out(fr, hs - 5, ps_f, fT_ready)
                if hs == 7:
                    until(act, q_full, b, Q_ABC + 1)
                    nc.scalar.copy(abc[:, :], ps_f[:, :]).then_inc(abc_ready[0], 1)
                if hs in range(8, 8 + 2 * G):
                    g, w = (hs - 8) // 2, hs % 2
                    if hs == 8 and not at_start(b):
                        until(act, parts_out, b - 1, parts_out[1])
                    until(act, qk32_ready, b, hs - 8 + 1)
                    nc.scalar.copy(parts[:, g // 2, w, 0, g % 2, :], qk32[:, w, :]).then_inc(part_step[0], 1)

            def v_at(b, hs):
                if hs in range(1, 1 + NT):
                    i = hs - 1
                    if i == 0:
                        until(act, vstep_ready, b, 1)
                        if not at_start(b):
                            until(act, pv_done, b - 1, 16)
                    until(act, v_full, b, i + 1)
                    nc.scalar.activation(V[:, i, :], ps_f[:, :], ACT.Copy,
                                         scale=vstep[:, i:i + 1]).then_inc(v_ready[0], 1)

            def maxima_at(b, g, i, q):
                pass

            def group_at(b, g, back):
                until(act, m_full, b, g + 1)
                if not (at_start(b) and g == 0):
                    until(act, m_stacked, b, 16 * HG * g)
                nc.scalar.copy(mT[:, :], ps_b[:, :].bitcast(F16)[:, 0:N]).then_inc(mT_ready[0], 1)

            def output(b, k, q):
                if k % NT == 0 and q == 1 and not (at_start(b) and k == 0):
                    seq, g = (b, k // NT) if k else (b - 1, G)
                    until(act, pv_done, seq, NT * g)
                    nc.scalar.copy(oT[:, g - 1, :], ps_o[:, :]).then_inc(o_ready[0], 1)
                    if g == G:
                        nc.scalar.copy(den[:, :], ps_den[:, :]).then_inc(den_ready[0], 1)

            def scores_at(b, k, q, tail=False):
                output(b, k, q)
                if tail:
                    return
                w = N - (k % NT) * P
                if q == 0 and not (at_start(b) and k < 2):
                    until(act, pv_done, b, k - 1)
                until(act, s2_ready, b, 2 * k + q + 1)
                nc.scalar.activation(pT[:, k % 2, 2 * q:2 * q + 2, 0:w], ps_s2[:, :, 0:w], ACT.Exp,
                                     scale=escale[:, 0:1]).then_inc(p_ready[0], 1)

            def back_at(b, hs, alone):
                if hs in (8, 9):
                    if hs == 8:
                        until(act, bf_ready, b, 1)
                    for r in range(2 * hs - 16, 2 * hs - 14):
                        nc.scalar.activation(bk.hc[:, r, :], bk.hc[:, r, :], ACT.Copy, bias=ROUND,
                                             scale=bk.fscale[:, r:r + 1]).then_inc(bq_ready[0], 1)
                if hs in (9, 10):
                    to_integers(bk, bq_ready, bi_ready, b, range(2 * hs - 18, 2 * hs - 16))
                if hs in (11, 12):
                    until(act, back_full, b, B_QT + hs - 11 + 1)
                    integers_out(bk, hs - 11, ps_b, bT_ready)
                if hs in range(21, 21 + NT):
                    r = hs - 21
                    until(act, x2_ready, b, r + 1)
                    if r == 0 and not at_start(b):
                        until(act, x2_stored, b - 1, 16 * NT)
                    nc.scalar.copy(x2p[:, r, 0, :], x2[:, r, :]).then_inc(x2_step[0], 1)

            sequences(act, prepare, nothing, maxima_at, scores_at, v_at, q_at, tokens_at, back_at, group_at)

        @block.vector
        def _(dve):
            start_at_one(dve, "dve")
            nw = [0]

            def wlink(ins):
                nw[0] += 1
                ins.then_inc(w_step, 1)
                dve.wait_ge(w_step, nw[0])

            dve.wait_ge(loaded, 16 * 9)
            nc.vector.tensor_copy(identb[:, :], ident[:, :]).then_inc(idents_cast, 1)
            nc.vector.tensor_copy(identh[:, :], ident[:, :]).then_inc(idents_cast, 1)
            nc.vector.tensor_copy(maskb[:, :, :], maskf[:, :, :]).then_inc(idents_cast, 1)
            cols = (slice(0, 3 * C), slice(3 * C, 4 * C))

            def largest_ahead(k):
                if k == 1:
                    dve.wait_ge(sw_loaded, 16 * len(ahead_loads))
                    for col, (src, _) in enumerate(ahead_loads):
                        last = nc.vector.tensor_reduce(wmax[:, col:col + 1], src, axis=AX if col == 3 else mybir.AxisListType.XY,
                                                       op=ALU.max, apply_absolute_value=True)
                    last.then_inc(max_ready, 1)

            def prepare(hs):
                if hs in range(16, 16 + KT):
                    k = hs - 16
                    if k == 0:
                        dve.wait_ge(w_loaded, 16 * 2)
                    for t in range(2):
                        nc.vector.tensor_reduce(wsum[:, KT * t + k:KT * t + k + 1], wstage[:, k, cols[t]], axis=AX,
                                                op=ALU.add, apply_absolute_value=True).then_inc(w_summed, 1)
                if hs == 16 + KT:
                    dve.wait_ge(w_summed, 2 * KT + 1)
                    wlink(nc.vector.tensor_reduce(wtot[:, :], ps_o[:, 0:2 * KT].rearrange("p (t k) -> p t k", t=2),
                                                  axis=AX, op=ALU.add))
                    for t in range(2):
                        wlink(nc.vector.tensor_scalar(wmean[:, t:t + 1], wtot[:, t:t + 1],
                                                      1.0 / (C * (cols[t].stop - cols[t].start)), CLIP, ALU.mult, ALU.max))
                    wlink(nc.vector.reciprocal(winv[:, :], wmean[:, :]))
                    wlink(nc.vector.tensor_scalar(escale[:, :], wmean[:, 0:1], wmean[:, 0:1], ATT_SCALE, ALU.mult, ALU.mult))
                if hs in range(22, 22 + 2 * KT):
                    k, t = (hs - 22) // 2, hs % 2
                    w = wstage[:, k, cols[t]]
                    wlink(nc.vector.tensor_scalar(w, w, winv[:, t:t + 1], ROUND, ALU.mult, ALU.add))
                    wlink(nc.vector.tensor_scalar(w, w, ROUND, 1.0, ALU.subtract, ALU.min))
                    nc.vector.tensor_scalar(wq[:, k, cols[t]], w, -1.0, None, ALU.max).then_inc(w_ready, 1)

            dve.wait_ge(consts_set, 6 + G)

            def full(b, u):
                until(dve, t_full, b, u + 1)

            def less_maximum(b, use, src):
                nc.vector.tensor_reduce(cmax[:, :], src, axis=AX, op=ALU.max).then_inc(tok_step[0], 1)
                until(dve, tok_step, b, 3 * use + 1)
                nc.vector.tensor_tensor(xs[:, :, :], src, cmax[:, :].unsqueeze(2).to_broadcast([P, NT, CH]),
                                        ALU.subtract).then_inc(xs_ready[0], 1)

            def normalised(b, use):
                until(dve, ex_ready, b, use + 1)
                nc.vector.tensor_reduce(csum[:, :], xs[:, :, :], axis=AX, op=ALU.add).then_inc(tok_step[0], 1)
                until(dve, tok_step, b, 3 * use + 2)
                nc.vector.reciprocal(crec[:, :], csum[:, :]).then_inc(tok_step[0], 1)
                until(dve, tok_step, b, 3 * use + 3)
                nc.vector.tensor_tensor(xs[:, :, :], xs[:, :, :], crec[:, :].unsqueeze(2).to_broadcast([P, NT, CH]),
                                        ALU.mult).then_inc(sel_ready[0], 1)

            def turned(b, u):
                full(b, u)
                nc.vector.tensor_copy(selT[:, :], ps_f[:, :]).then_inc(selT_ready[0], 1)

            def largest(b, rows, asked, rs):
                for r in rs:
                    until(dve, asked, b, r + 1)
                    last = nc.vector.tensor_reduce(rows.amax[:, r:r + 1], rows.hc[:, r, :], axis=AX, op=ALU.max,
                                                   apply_absolute_value=True)
                return last

            def statistic(b, rows, src, r, asked, n, step):
                until(dve, asked, b, n)
                nc.vector.bn_stats(rows.stats[:, r, :], src).then_inc(step[0], 1)

            def aggregate(b, rows, step, n, given_):
                until(dve, step, b, n)
                dve.sem_inc(passed, 1)
                for r in range(NT):
                    last = nc.vector.bn_aggr(rows.mv[:, r, :], rows.stats[:, r, :])
                last.then_inc(step[0], 1)
                until(dve, step, b, n + 1)
                nc.vector.tensor_scalar(rows.negmean[:, :], rows.mv[:, :, 0], -1.0, None, ALU.mult)
                nc.vector.tensor_scalar(rows.vare[:, :], rows.mv[:, :, 1], EPS, None, ALU.add).then_inc(given_[0], 1)

            def tokens_at(b, hs):
                if hs == 15:
                    if isinstance(b, int) and b < 3:
                        dve.wait_ge(gathered[b], 16 * (NT if b < 2 else (B - 2) * NT))
                    nc.vector.scalar_tensor_tensor(x_tm[:, :, :], emb_all[:, bass.ds(b * NT, NT), :],
                                                   float(np.sqrt(np.float32(CH))), pe_tm[:, :, :],
                                                   ALU.mult, ALU.add).then_inc(x_ready[0], 1)
                if hs == 16:
                    until(dve, x_ready, b, 1)
                    less_maximum(b, 0, x_tm[:, :, :])
                if hs in (18, 23):
                    normalised(b, hs // 23)
                if hs in (19, 24):
                    turned(b, (T_SELT0, T_SELT1)[hs // 24])
                if hs == 21:
                    full(b, T_CONVT)
                    less_maximum(b, 1, ps_f[:, :].rearrange("p (t c) -> p t c", t=NT))
                if hs in (20, 22, 24, 26):
                    n = hs // 2 - 10
                    r = H_ORDER[n]
                    statistic(b, fr, h[:, r, PAD:], r, h_ready, n + 1, fr_step)
                if hs == 26:
                    aggregate(b, fr, fr_step, NT, fvar_ready)
                if hs in (28, 29):
                    last = largest(b, fr, fc_ready, range(2 * hs - 56, 2 * hs - 54))
                    if hs == 29:
                        last.then_inc(fr_step[0], 1)
                if hs == 30:
                    until(dve, fr_step, b, NT + 2)
                    until(dve, frstd_ready, b, 1)
                    nc.vector.tensor_tensor(tmp4[:, :], fr.amax[:, :], fr.rstd[:, :], ALU.mult).then_inc(fr_step[0], 1)
                    until(dve, fr_step, b, NT + 3)
                    nc.vector.tensor_scalar(fr.aval[:, :], tmp4[:, :], CLIP, None, ALU.max).then_inc(fr_step[0], 1)
                    until(dve, fr_step, b, NT + 4)
                    nc.vector.reciprocal(fr.arec[:, :], fr.aval[:, :]).then_inc(fr_step[0], 1)
                    until(dve, fr_step, b, NT + 5)
                    nc.vector.tensor_scalar(fr.astep[:, :], fr.aval[:, :], 1.0 / QMAX, None, ALU.mult)
                    nc.vector.scalar_tensor_tensor(fr.fscale[:, :], fr.arec[:, :], QMAX, fr.rstd[:, :], ALU.mult,
                                                   ALU.mult).then_inc(ff_ready[0], 1)
                if hs == 31:
                    until(dve, ff_ready, b, 1)
                    for r in range(NT):
                        last = nc.vector.tensor_scalar(diag[:, r, :], ident[:, :], fr.astep[:, r:r + 1], None, ALU.mult)
                    last.then_inc(diag_ready[0], 1)

            def q_at(b, hs):
                if hs in range(8, 8 + 2 * G):
                    n = hs - 8
                    if n == 0:
                        until(dve, abc_ready, b, 1)
                        if not at_start(b):
                            until(dve, parts_ready, b - 1, 2 * G)
                    until(dve, q_full, b, Q_QK + n + 1)
                    if n >= 2:
                        until(dve, parts_ready, b, n - 1)
                    nc.vector.tensor_tensor(qk32[:, n % 2, :], ps_f[:, :], abc[:, :],
                                            ALU.mult).then_inc(qk32_ready[0], 1)
                if hs == 16:
                    if not at_start(b):
                        until(dve, v_ready, b - 1, NT)
                    nc.vector.tensor_copy(vstep[:, :], fr.astep[:, :]).then_inc(vstep_ready[0], 1)

            def v_at(b, hs):
                pass

            def group_at(b, g, back):
                pass

            def maxima_at(b, g, i, q):
                if i == 0 and q == 0 and not (at_start(b) and g < 2):
                    until(dve, mm_ready, b, g - 1)
                until(dve, s1_ready, b, 8 * g + 2 * i + q + 1)
                nc.vector.tensor_reduce(mx[:, g % 2, i, 2 * q:2 * q + 2], ps_s1[:, :, 0:(i + 1) * P], axis=AX,
                                        op=ALU.max).then_inc(s1_read[0], 1)

            def scores_at(b, s, q, tail=False):
                pass

            def back_at(b, hs, alone):
                if hs == 2:
                    until(dve, back_full, b, B_DEN + 1)
                    nc.vector.reciprocal(rden[:, :, :, :], ps_b[:, :].rearrange(
                        "p (i j c) -> p i j c", i=NT, j=HG)[:, :, :, 0:G]).then_inc(bd_ready[0], 1)
                if hs in range(3, 3 + NT):
                    i = hs - 3
                    if i == 0:
                        until(dve, bd_ready, b, 1)
                    until(dve, back_full, b, B_OT + i + 1)
                    for j in range(HG):
                        last = nc.vector.tensor_tensor(
                            bk.hc[:, i, :].rearrange("p (g j d) -> p g j d", g=G, j=HG)[:, :, j, :],
                            ps_b[:, :].rearrange("p (g j d) -> p g j d", g=G, j=HG)[:, :, j, :],
                            rden[:, i, j, :].unsqueeze(2).to_broadcast([P, G, DH]), ALU.mult)
                    last.then_inc(bc_ready[0], 1)
                    last = largest(b, bk, bc_ready, [i])
                    if hs == 2 + NT:
                        last.then_inc(bk_step[0], 1)
                if hs == 7:
                    until(dve, bk_step, b, 1)
                    nc.vector.tensor_scalar(bk.aval[:, :], bk.amax[:, :], wmean[:, 0:1], CLIP, ALU.mult,
                                            ALU.max).then_inc(bk_step[0], 1)
                    until(dve, bk_step, b, 2)
                    nc.vector.reciprocal(bk.arec[:, :], bk.aval[:, :]).then_inc(bk_step[0], 1)
                    until(dve, bk_step, b, 3)
                    nc.vector.tensor_scalar(bk.astep[:, :], bk.aval[:, :], wmean[:, 1:2], 1.0 / QMAX, ALU.mult, ALU.mult)
                    nc.vector.tensor_scalar(bk.fscale[:, :], bk.arec[:, :], wmean[:, 0:1], QMAX, ALU.mult,
                                            ALU.mult).then_inc(bf_ready[0], 1)
                if hs in range(14, 14 + NT):
                    i = hs - 14
                    if i == 0:
                        until(dve, h_fetched, b, 16)
                    until(dve, back_full, b, B_PROJ + i + 1)
                    nc.vector.scalar_tensor_tensor(h1[:, i, :], ps_b[:, :], bk.astep[:, i:i + 1], h1[:, i, :],
                                                   ALU.mult, ALU.add).then_inc(h1_ready[0], 1)
                if hs in range(15, 15 + NT):
                    i = hs - 15
                    statistic(b, bk, h1[:, i, :], i, h1_ready, i + 1, bk_step)
                if hs == 18:
                    aggregate(b, bk, bk_step, NT + 3, bvar_ready)
                if hs in (20, 21):
                    if hs == 20:
                        until(dve, brstd_ready, b, 1)
                        if not at_start(b):
                            until(dve, x2p_ready, b - 1, NT)
                    for r in range(2 * hs - 40, 2 * hs - 38):
                        nc.vector.tensor_scalar(x2[:, r, :], h1[:, r, :], bk.mv[:, r, 0:1], bk.rstd[:, r:r + 1],
                                                ALU.subtract, ALU.mult).then_inc(x2_ready[0], 1)

            sequences(dve, prepare, largest_ahead, maxima_at, scores_at, v_at, q_at, tokens_at, back_at, group_at)

        @block.tensor
        def _(pe):
            start_at_one(pe, "pe")
            pe.wait_ge(consts_set, 6 + G)
            pe.wait_ge(idents_cast, 3)

            def prepare(hs):
                if hs == 16 + KT:
                    pe.wait_ge(w_summed, 2 * KT)
                    nc.tensor.matmul(ps_o[:, 0:2 * KT], ones[:, :], wsum[:, :], start=True, stop=True).then_inc(w_summed, 1)
                if hs == 31:
                    pe.wait_ge(w_ready, 2 * KT)

            def transposes(src):
                for t in range(NT):
                    last = nc.tensor.transpose(ps_f[:, t * P:(t + 1) * P], src(t), ident[:, :])
                return last

            def turn_integers(b, rows, half, bank, asked):
                if half == 0:
                    until(pe, asked, b, NT)
                for r in range(NT):
                    for kk in range(2):
                        k = 2 * half + kk
                        last = nc.tensor.transpose(bank[:, :].bitcast(BF16)[:, kk * N + r * P:kk * N + (r + 1) * P],
                                                   rows.xqi[:, r, k * P:(k + 1) * P], identb[:, :])
                return last

            def tokens_at(b, hs):
                uses = {16: T_XT, 18: T_CONV, 19: T_SELT0, 20: T_EXT0, 21: T_CONVT, 24: T_SELT1, 25: T_EXT1}
                if hs not in uses:
                    return
                u = uses[hs]
                if u:
                    until(pe, T_DRAINED[u - 1][0], b, T_DRAINED[u - 1][1])
                elif not at_start(b):
                    until(pe, qk32_ready, b - 1, 2 * G)
                if u == T_XT:
                    until(pe, x_ready, b, 1)
                    last = transposes(lambda t: x_tm[:, t, :])
                if u == T_CONV:
                    until(pe, h_ready, b, 1)
                    for k in range(TAPS):
                        last = nc.tensor.matmul(ps_f[:, :], convw[:, k, :], h[:, 0, k:k + T],
                                                start=(k == 0), stop=(k == TAPS - 1))
                if u in (T_SELT0, T_SELT1):
                    until(pe, sel_ready, b, 1 if u == T_SELT0 else 2)
                    last = transposes(lambda t: xs[:, t, :])
                if u in (T_EXT0, T_EXT1):
                    last = nc.tensor.matmul(ps_f[:, :], (sp0 if u == T_EXT0 else sp1)[:, :], selT[:, :],
                                            start=True, stop=True)
                if u == T_CONVT:
                    last = transposes(lambda t: h[:, 2, PAD + t * P:PAD + (t + 1) * P])
                last.then_inc(t_full[0], 1)

            def q_at(b, hs):
                if hs not in range(5, 8 + 2 * G):
                    return
                u = hs - 5
                if u:
                    until(pe, Q_DRAINED[u - 1][0], b, Q_DRAINED[u - 1][1])
                elif at_start(b):
                    until(pe, h_ready, b, NT)
                else:
                    until(pe, v_ready, b - 1, NT)
                if u < Q_ABC:
                    last = turn_integers(b, fr, u, ps_f, fi_ready)
                elif u == Q_ABC:
                    until(pe, diag_ready, b, 1)
                    for r in range(NT):
                        last = nc.tensor.matmul(ps_f[:, r * P:(r + 1) * P], ones[:, :], diag[:, r, :],
                                                start=True, stop=True)
                else:
                    g, w = (u - Q_QK) // 2, (u - Q_QK) % 2
                    for k in range(KT):
                        last = nc.tensor.matmul(ps_f[:, :], wq[:, k, w * C + g * P:w * C + (g + 1) * P],
                                                fr.xqT[:, k, :], start=(k == 0), stop=(k == KT - 1))
                last.then_inc(q_full[0], 1)

            def v_at(b, hs):
                if hs not in range(1, 1 + NT):
                    return
                i = hs - 1
                if i:
                    until(pe, v_ready, b, i)
                elif isinstance(b, int) and b == B - 1:
                    until(pe, qk32_ready, b, 2 * G)
                else:
                    until(pe, h_ready, b + 1, NT)
                for k in range(KT):
                    last = nc.tensor.matmul(ps_f[:, :], fr.xqT[:, k, i * P:(i + 1) * P], wq[:, k, 2 * C:3 * C],
                                            start=(k == 0), stop=(k == KT - 1))
                last.then_inc(v_full[0], 1)

            def maxima_at(b, g, i, q):
                if i == 0 and g % 2 == 0 and q == 0:
                    until(pe, stacked[g // 2], b, stacked[0][1])
                if not (at_start(b) and g == 0 and i == 0 and q == 0):
                    until(pe, s1_read, b, 8 * g + 2 * i + q)
                for e in range(2):
                    j = 2 * q + e
                    nc.tensor.matmul(ps_s1[:, e, 0:(i + 1) * P], QS[0:KPARTS, g, j, i * P:(i + 1) * P],
                                     KS[0:KPARTS, g, j, 0:(i + 1) * P], start=True, stop=False)
                    last = nc.tensor.matmul(ps_s1[:, e, i * P:(i + 1) * P], identb[:, :], maskb[:, 0, :],
                                            start=False, stop=True)
                last.then_inc(s1_ready[0], 1)

            def group_at(b, g, back):
                if back and g in (1, 2, 3):
                    until(pe, *((bc_ready, b - 1, NT - 1), (bT_ready, b - 1, 2), (h1_ready, b - 1, NT))[g - 1])
                if not (at_start(b) and g == 0):
                    until(pe, mT_ready, b, g)
                until(pe, mm_ready, b, g + 1)
                for i in range(NT):
                    last = nc.tensor.transpose(ps_b[:, :].bitcast(F16)[:, i * P:(i + 1) * P],
                                               mm[:, i, :, :].rearrange("p j r -> p (j r)"), identh[:, :])
                last.then_inc(m_full[0], 1)

            def scores(b, k, q):
                g, s = k // NT, k % NT
                w = N - s * P
                if s == 0 and q == 0:
                    until(pe, m_stacked, b, 16 * HG * (g + 1))
                if not (at_start(b) and k + q == 0):
                    until(pe, p_ready, b, 2 * k + q)
                for e in range(2):
                    j = 2 * q + e
                    nc.tensor.matmul(ps_s2[:, e, 0:w], KS[0:KPARTS + MROWS, g, j, s * P:(s + 1) * P],
                                     QS[0:KPARTS + MROWS, g, j, s * P:N], start=True, stop=False)
                    last = nc.tensor.matmul(ps_s2[:, e, 0:P], identb[:, :], maskb[:, 1, :],
                                            start=False, stop=True)
                last.then_inc(s2_ready[0], 1)

            def values(b, k):
                g, s = k // NT, k % NT
                w = N - s * P
                until(pe, p_ready, b, 2 * k + 2)
                if g == 0:
                    until(pe, v_ready, b, s + 1)
                if s == 0 and not (at_start(b) and g == 0):
                    until(pe, o_ready, b, g)
                    if g == 0:
                        until(pe, den_ready, b - 1, 1)
                for j in range(HG):
                    nc.tensor.matmul(ps_o[DH * j:DH * j + DH, s * P:N],
                                     V[:, s, (HG * g + j) * DH:(HG * g + j + 1) * DH], pT[:, k % 2, j, 0:w],
                                     start=(s == 0), stop=(s == NT - 1))
                for j in range(HG):
                    last = nc.tensor.matmul(ps_den[DH * j:DH * j + DH, s * P:N], head_of[:, g, :],
                                            pT[:, k % 2, j, 0:w], start=(k == 0), stop=(k == G * NT - 1))
                last.then_inc(pv_done[0], 1)

            def scores_at(b, s, q, tail=False):
                if not tail:
                    scores(b, s, q)
                if s == 0:
                    if q == 0 and not at_start(b):
                        values(b - 1, 15)
                elif q == (1 if s % NT == 1 else 0):
                    values(b, s - 1)

            def back_at(b, hs, alone):
                uses = {2: B_DEN, 3: B_OT, 4: B_OT + 1, 5: B_OT + 2, 6: B_OT + 3, 11: B_QT, 12: B_QT + 1,
                        14: B_PROJ, 15: B_PROJ + 1, 16: B_PROJ + 2, 17: B_PROJ + 3}
                if hs not in uses:
                    return
                u = uses[hs]
                if u:
                    until(pe, B_DRAINED[u - 1][0], b, B_DRAINED[u - 1][1])
                if u in (B_DEN, B_OT + 3, B_PROJ) and not alone:
                    until(pe, mT_ready, b + 1, {B_DEN: 1, B_OT + 3: 2, B_PROJ: 3}[u])
                if u == B_DEN and alone:
                    until(pe, mT_ready, b, G)
                if u == B_DEN:
                    until(pe, den_ready, b, 1)
                    for i in range(NT):
                        last = nc.tensor.transpose(ps_b[:, i * P:(i + 1) * P], den[:, i * P:(i + 1) * P], ident[:, :])
                elif u < B_QT:
                    i = u - B_OT
                    for g in range(G):
                        last = nc.tensor.transpose(ps_b[:, g * P:(g + 1) * P], oT[:, g, i * P:(i + 1) * P], ident[:, :])
                elif u < B_PROJ:
                    last = turn_integers(b, bk, u - B_QT, ps_b, bi_ready)
                else:
                    i = u - B_PROJ
                    for k in range(KT):
                        last = nc.tensor.matmul(ps_b[:, :], bk.xqT[:, k, i * P:(i + 1) * P], wq[:, k, 3 * C:],
                                                start=(k == 0), stop=(k == KT - 1))
                last.then_inc(back_full[0], 1)

            sequences(pe, prepare, nothing, maxima_at, scores_at, v_at, q_at, tokens_at, back_at, group_at)


def ffn_phase(nc, ident_in, tri_in, lanes_in, gate_w, w1, b1, w2, b2, sw1, sb1, sw2, sb2, h1_dram, x2_dram, out,
              big, gws, sb1c, wmax, sw_loaded, max_ready):
    TT = B * N // P
    TILES = 2 * TT + E_
    FS = SH // P
    FE = HID // P
    W1N, W2N = KT * 2 * HID, FE * 2 * C
    WB1 = (W1N + W2N) // 2
    WDOWN, WHUP, WYDN = WB1 + FE, WB1 + FE + 1, WB1 + FE + 2
    WROW = WB1 + FE + 3
    assert B == E_
    D = 4
    TOP = 2.0 ** 10
    base_dram = nc.dram_tensor("base_rows", [B * N, C], F32, kind="Internal").ap()
    y_dram = nc.dram_tensor("expert_rows", [TILES * P, C], F32, kind="Internal").ap()
    ctx = ExitStack()
    with ctx:
        def sb(name, shape, dt):
            return ctx.enter_context(nc.sbuf_tensor(name, shape, dt))

        def sem(name):
            return ctx.enter_context(nc.semaphore(name))

        identf = sb("f_identf", [P, P], F32)
        ident = sb("f_ident", [P, P], F16)
        trif = sb("f_trif", [P, P], F32)
        lanes = sb("f_lanes", [P, P], F32)
        lanesb = sb("f_lanesb", [P, P], BF16)
        lohi = sb("f_lohi", [P, 2, 2 * TT], BF16)
        part = sb("f_part", [P, 1], F32)
        ones = sb("f_ones", [P, P], BF16)
        tri = sb("f_tri", [P, P], BF16)
        ew = sb("f_ew", [P, E_, WROW], I32)
        sw1p = sb("f_sw1p", [P, KT, 2, SH], F16)
        sw2p = sb("f_sw2p", [P, FS, 2, C], F16)
        gwp = sb("f_gwp", [P, KT, 2, E_], F16)
        sb2r = sb("f_sb2r", [P, C], F32)
        b2r = sb("f_b2r", [P, E_, C], F32)
        base = sb("f_base", [P, NT, C], F32)
        lo_hot = big[:, 0:4096].bitcast(BF16).rearrange("p (n m) -> p n m", m=P)
        hi_hot = big[:, 4096:8704].bitcast(BF16).rearrange("p (n a m) -> p n a m", a=2, m=TILES)
        wall = sb("f_wall", [P, 4], F32)
        wpow = sb("f_wpow", [P, 4], F32)
        wup = sb("f_wup", [P, 4], F32)
        wdown = sb("f_wdown", [P, 4], F32)
        hb = sb("f_hb", [P, 1], F32)
        hpow = sb("f_hpow", [P, 1], F32)
        hup = sb("f_hup", [P, 1], F32)
        hdn = sb("f_hdn", [P, 1], F32)
        ydn = sb("f_ydn", [P, 1], F32)
        emax = sb("f_emax", [P, 3], F32)
        eall = sb("f_eall", [P, 3], F32)
        etop = sb("f_etop", [3, 1], F32)
        ediag = sb("f_ediag", [3, 3], F32)
        eones = sb("f_eones", [3, P], F32)
        epow = sb("f_epow", [P, 3], F32)
        eup = sb("f_eup", [P, 3], F32)
        edown = sb("f_edown", [P, 3], F32)
        ehb = sb("f_ehb", [P, 1], F32)
        ehup = sb("f_ehup", [P, 1], F32)
        ehdn = sb("f_ehdn", [P, 1], F32)

        x2t = sb("f_x2t", [P, NT, 2 * C], F16)
        h1t = sb("f_h1t", [P, NT, C], F32)
        xT = sb("f_xT", [P, KT, 2, N], F16)
        act_h = sb("f_act", [P, 2, N], F32)
        gp = sb("f_gp", [P, FS, 2, N], F16)

        L = sb("f_L", [P, TT, E_], F32)
        eqs = sb("f_eqs", [P, TT, E_], F32)
        oh = sb("f_oh", [P, 2, TT, E_], F32)
        L2 = sb("f_L2", [P, TT, E_], F32)
        v12 = sb("f_v12", [P, 2, TT], F32)
        m12 = sb("f_m12", [P, 2, TT], F32)
        dlt = sb("f_dlt", [P, TT], F32)
        exd = sb("f_exd", [P, TT], F32)
        gate = sb("f_gate", [P, 2, TT], F32)
        prior = sb("f_prior", [P, E_], F32)
        both = sb("f_both", [P, TT, E_], BF16)
        pre = sb("f_pre", [P, TT, E_], F32)
        scan = sb("f_scan", [P, 2, TT, E_], F32)
        ntile = sb("f_ntile", [P, E_], F32)
        nt2 = sb("f_nt2", [P, E_], F32)
        tend = sb("f_tend", [P, 2, E_], F32)
        posn = sb("f_posn", [P, TT, E_], F32)
        slot = sb("f_slot", [P, 2, TT], F32)
        hi = sb("f_hi", [P, 2, TT], F32)
        lo = sb("f_lo", [P, 2, TT], F32)
        slot_i = sb("f_slot_i", [P, 2, TT], I32)
        tsel = sb("f_tsel", [P, TILES, E_], F32)
        texp = sb("f_texp", [P, TILES], F32)
        texp_i = sb("f_texp_i", [P, TILES], I32)
        tok_i = sb("f_tok_i", [P, TILES + D], I32)
        tok_f = sb("f_tok_f", [P, TILES], F32)

        now = sb("f_now", [P, D], I32)
        now2 = sb("f_now2", [P, D, 2], I32)
        xg = x2t
        xgT = sb("f_xgT", [P, 2, KT, 2, P], F16)
        wcur = big[:, 0:2 * WROW].bitcast(I32).rearrange("p (z w) -> p z w", z=2)
        ga = act_h[:, :, :].rearrange("p a n -> p (a n)").rearrange("p (z f n) -> p z f n", z=D, f=FE)
        gq = gp[:, 0:2, :, :].rearrange("p f a n -> p (f a n)").rearrange("p (z f a n) -> p z f a n", z=D, f=FE, a=2)
        yt = big[:, 4608:4608 + D * C].rearrange("p (z c) -> p z c", z=D)
        yg = ew[:, 0:5, :].rearrange("p e w -> p (e w)").bitcast(F32)[:, 0:D * 2 * C].rearrange(
            "p (z k c) -> p z k c", z=D, k=2)
        bt = h1t
        PS = ctx.enter_context(nc.psum_tensor("f_ps", [P, 8, 512], F32))

        loaded = sem("f_loaded")
        gated = sem("f_gated")
        set_up = sem("f_set_up")
        cast = sem("f_cast")
        passed = sem("f_passed")
        all_max = sem("f_all_max")
        vstep = sem("f_vstep")
        scaled = sem("f_scaled")
        high_ready = sem("f_high_ready")
        b1_loaded = sem("f_b1_loaded")
        stage_free = sem("f_stage_free")
        routed = sem("f_routed")
        route_pe = sem("f_route_pe")
        route_dve = sem("f_route_dve")
        route_act = sem("f_route_act")

        given = {"pe": [], "act": [], "dve": [], "pool": [], "sp": []}

        def signal(name, per, giver):
            s = sem(name)
            if giver is None:
                return s, per, 0
            given[giver].append(s)
            return s, per, 1

        x2_loaded = signal("f_x2_loaded", 16, "sp")
        h1_loaded = signal("f_h1_loaded", 16, "sp")
        tr_done = signal("f_tr_done", KT, "pe")
        xT_even = signal("f_xT_even", 2, "act")
        xT_odd = signal("f_xT_odd", 2, "dve")
        lg_done = signal("f_lg_done", 1, "pe")
        lg_read = signal("f_lg_read", 1, "dve")
        up_done = signal("f_up_done", FS, "pe")
        gelu_done = signal("f_gelu_done", FS, "act")
        ghi_done = signal("f_ghi_done", FS, "act")
        glo_done = signal("f_glo_done", FS, "dve")
        down_done = signal("f_down_done", NT, "pe")
        h1b_done = signal("f_h1b_done", NT, "pool")
        base_done = signal("f_base_done", NT, "dve")
        base_stored = signal("f_base_stored", 16, "sp")
        e_loaded = signal("e_loaded", 32, "sp")
        e_max = signal("e_max", 1, "dve")
        e_turned = signal("e_turned", 1, "pe")
        e_diag = signal("e_diag", 1, "dve")
        e_all = signal("e_all", 1, "pe")
        e_step = signal("e_step", 8, "dve")
        e_scaled = signal("e_scaled", 1, "dve")
        e_high = signal("e_high", 2, "act")
        e_low = signal("e_low", 1, "dve")
        c_now = signal("c_now", 1, "pool")
        d_now = signal("d_now", 1, "pool")
        c_gather = [signal("c_gather%d" % z, 16, None) for z in range(D)]
        c_tr = signal("c_tr", 1, "pe")
        c_xT = signal("c_xT", 1, "act")
        c_w1 = signal("c_w1", 1, "dve")
        c_w2 = signal("c_w2", 1, "dve")
        c_up = signal("c_up", 1, "pe")
        c_gelu = signal("c_gelu", 1, "act")
        c_hi = signal("c_hi", 1, "act")
        c_lo = signal("c_lo", 1, "dve")
        c_down = signal("c_down", 1, "pe")
        c_y = signal("c_y", 1, "dve")
        c_store = [signal("c_store%d" % z, 16, "sp") for z in range(D)]
        d_gather = [signal("d_gather%d" % z, 32, None) for z in range(D)]
        d_base = [signal("d_base%d" % z, 16, "sp") for z in range(D)]
        d_acc = signal("d_acc", 1, "dve")
        d_done = [signal("d_done%d" % z, 1, "dve") for z in range(D)]
        d_store = [signal("d_store%d" % z, 16, "sp") for z in range(D)]

        def start_at_one(eng, giver):
            for s in given[giver]:
                eng.sem_inc(s, 1)

        def until(eng, signal, b, k):
            s, per, start = signal
            eng.wait_ge(s, b * per + k + start)
            if eng in (nc.gpsimd, nc.sync) and not isinstance(b, int):
                eng.sem_inc(passed, 1)

        def weights(row):
            w1v = row[:, 0:W1N // 2].bitcast(F16).rearrange("p (k a n) -> p k a n", k=KT, a=2)
            w2v = row[:, W1N // 2:(W1N + W2N) // 2].bitcast(F16).rearrange("p (f a n) -> p f a n", f=FE, a=2)
            b1v = row[:, (W1N + W2N) // 2:WROW].bitcast(F32)
            return w1v, w2v, b1v

        def tile(t, z):
            return t + z // D, z % D

        def in_steps(eng, step):
            for k in (-2, -1, 0):
                step(0, k, True, False)
            with eng.Fori(0, TILES // D - 1) as t:
                for k in range(1, D + 1):
                    step(t, k, False, False)
            for k in range(1, D + 1):
                step(TILES // D - 1, k, False, True)

        block = ctx.enter_context(nc.Block())
        stage_sw1 = big[:, 0:KT * SH].rearrange("p (k n) -> p k n", k=KT)
        stage_sw2 = big[:, KT * SH:KT * SH + FS * C].rearrange("p (f n) -> p f n", f=FS)
        e0 = KT * SH + FS * C
        stage_e = (big[:, e0:e0 + KT * HID].rearrange("p (k n) -> p k n", k=KT),
                   big[:, e0 + KT * HID:e0 + KT * HID + FE * C].rearrange("p (f n) -> p f n", f=FE))

        def in_turns(eng, turn):
            turn(0, True, False)
            with eng.Fori(1, B - 1) as b:
                turn(b, False, False)
            turn(B - 1, False, True)

        @block.sync
        def _(sp):
            start_at_one(sp, "sp")
            for dst, src in ((identf[:, :], ident_in), (trif[:, :], tri_in), (lanes[:, :], lanes_in)):
                sp.dma_start(dst, src).then_inc(loaded, 16)

            def load_x2(b):
                sp.dma_start(x2t[:, :, :],
                             x2_dram[bass.ds(b * N, N), :].rearrange("(i p) c -> p i c", p=P)).then_inc(x2_loaded[0], 16)

            load_x2(0)
            for dst, src in ((ew[:, :, WB1:WB1 + FE].bitcast(F32), b1),
                             (sb2r[:, :], sb2.rearrange("(a n) -> a n", a=1).to_broadcast([P, C])),
                             (b2r[:, :, :].rearrange("p e n -> p (e n)"),
                              b2.rearrange("(a e) n -> a (e n)", a=1).to_broadcast([P, E_ * C]))):
                sp.dma_start(dst, src).then_inc(b1_loaded, 16)

            def turn(b, first, last):
                if not last:
                    until(sp, tr_done, b, KT)
                    load_x2(b + 1)
                if not first:
                    until(sp, base_done, b - 1, NT)
                sp.dma_start(h1t[:, :, :],
                             h1_dram[bass.ds(b * N, N), :].rearrange("(i p) c -> p i c", p=P)).then_inc(h1_loaded[0], 16)
                if not first:
                    until(sp, e_low, b - 1, 1)
                sp.dma_start(stage_e[0], w1[bass.ds(b, 1), :, :].rearrange("o (k p) n -> p (o k) n", p=P)).then_inc(e_loaded[0], 16)
                sp.dma_start(stage_e[1], w2[bass.ds(b, 1), :, :].rearrange("o (f p) n -> p (o f) n", p=P)).then_inc(e_loaded[0], 16)
                until(sp, base_done, b, NT)
                sp.dma_start(base_dram[bass.ds(b * N, N), :].rearrange("(i p) c -> p i c", p=P),
                             base[:, :, :]).then_inc(base_stored[0], 16)

            in_turns(sp, turn)
            with sp.Fori(0, TILES // D) as t:
                for z in range(D):
                    until(sp, c_y, D * t, z + 1)
                    sp.dma_start(y_dram[bass.ds((D * t + z) * P, P), :], yt[:, z, :]).then_inc(c_store[z][0], 16)
            until(sp, base_stored, B, 0)
            with sp.Fori(0, TT // D) as t:
                for z in range(D):
                    until(sp, d_store[z], t, 0)
                    sp.dma_start(bt[:, z, :], base_dram[bass.ds((D * t + z) * P, P), :]).then_inc(d_base[z][0], 16)
                for z in range(D):
                    until(sp, d_done[z], t, 1)
                    sp.dma_start(out[bass.ds((D * t + z) * P, P), :], bt[:, z, :]).then_inc(d_store[z][0], 16)
            for z in range(D):
                until(sp, c_store[z], TILES // D, 0)
                until(sp, d_store[z], TT // D, 0)

        @block.gpsimd
        def _(pool):
            start_at_one(pool, "pool")
            pool.wait_ge(max_ready, 1)
            nc.gpsimd.partition_all_reduce(wall[:, :], wmax[:, :], P, bass.bass_isa.ReduceOp.max).then_inc(all_max, 1)
            nc.gpsimd.iota(part[:, :], pattern=[[0, 1]], base=0, channel_multiplier=1,
                           allow_small_or_imprecise_dtypes=True).then_inc(set_up, 1)
            nc.gpsimd.memset(ones[:, :], 1.0).then_inc(set_up, 1)
            nc.gpsimd.memset(tok_i[:, TILES:], 0).then_inc(set_up, 1)
            nc.gpsimd.memset(eones[:, :], 1.0).then_inc(set_up, 1)
            pool.wait_ge(b1_loaded, 16 * 3)
            pool.wait_ge(route_dve, 1)

            def turn(b, first, last):
                until(pool, h1_loaded, b, 16)
                for i in range(NT):
                    nc.gpsimd.tensor_tensor(h1t[:, i, :], h1t[:, i, :], sb2r[:, :], ALU.add).then_inc(h1b_done[0], 1)

            in_turns(pool, turn)

            def gather(t, z):
                nc.gpsimd.tensor_copy(now[:, z:z + 1], tok_i[:, bass.ds(D * t + z, 1)]).then_inc(c_now[0], 1)
                until(pool, c_now, D * t, z + 1)
                nc.gpsimd.indirect_dma_start(
                    out=xg[:, z, :], out_offset=None, in_=x2_dram,
                    in_offset=bass.IndirectOffsetOnAxis(ap=now[:, z:z + 1], axis=0)).then_inc(c_gather[z][0], 16)

            pool.wait_ge(set_up, 4)
            pool.wait_ge(routed, 2)
            for z in range(D):
                gather(0, z)
            with pool.Fori(0, TILES // D) as t:
                for z in range(D):
                    until(pool, c_tr, D * t, z + 1)
                    gather(t + 1, z)
            for z in range(D):
                until(pool, c_store[z], TILES // D, 0)
            with pool.Fori(0, TT // D) as t:
                for z in range(D):
                    until(pool, d_done[z], t, 0)
                    nc.gpsimd.tensor_copy(now2[:, z, :], slot_i[:, :, bass.ds(D * t + z, 1)].rearrange(
                        "p k o -> p (k o)")).then_inc(d_now[0], 1)
                    until(pool, d_now, D * t, z + 1)
                    for k in range(2):
                        nc.gpsimd.indirect_dma_start(
                            out=yg[:, z, k, :], out_offset=None, in_=y_dram,
                            in_offset=bass.IndirectOffsetOnAxis(ap=now2[:, z, k:k + 1], axis=0)
                        ).then_inc(d_gather[z][0], 16)
            for z in range(D):
                pool.wait_ge(c_gather[z][0], 16 * (TILES // D + 1))

        @block.scalar
        def _(act):
            start_at_one(act, "act")
            act.wait_ge(scaled, 1)
            for dst, src, col in ((gwp[:, :, 0, :], gws[:, :, :], 2), (sw1p[:, :, 0, :], stage_sw1, 0),
                                  (sw2p[:, :, 0, :], stage_sw2, 1)):
                nc.scalar.activation(dst, src, ACT.Copy, scale=wup[:, col:col + 1]).then_inc(high_ready, 1)

            def columns(b):
                for k in (0, 2):
                    until(act, tr_done, b, k + 1)
                    nc.scalar.copy(xT[:, k, :, :].rearrange("p a n -> p (a n)"),
                                   PS[:, k, :].bitcast(F16)).then_inc(xT_even[0], 1)

            def turn(b, first, last):
                if first:
                    columns(0)
                for f in range(FS):
                    until(act, up_done, b, f + 1)
                    if f >= 2 or not first:
                        until(act, glo_done, b, f - 1)
                    nc.scalar.activation(act_h[:, f % 2, :], PS[:, 4 + f % 2, :], ACT.Gelu, bias=sb1c[:, f:f + 1],
                                         scale=wdown[:, 0:1]).then_inc(gelu_done[0], 1)
                    until(act, gelu_done, b, f + 1)
                    nc.scalar.activation(gp[:, f, 0, :], act_h[:, f % 2, :], ACT.Copy,
                                         scale=hup[:, 0:1]).then_inc(ghi_done[0], 1)
                if not last:
                    columns(b + 1)
                until(act, e_scaled, b, 1)
                row = ew[:, bass.ds(b, 1), :].rearrange("p o w -> p (o w)")
                for k in range(2):
                    nc.scalar.activation(weights(row)[k][:, :, 0, :], stage_e[k], ACT.Copy,
                                         scale=eup[:, k:k + 1]).then_inc(e_high[0], 1)

            in_turns(act, turn)
            act.wait_ge(routed, 1)
            nc.scalar.activation(exd[:, :], dlt[:, :], ACT.Exp).then_inc(route_act, 1)

            def rows_out(t, z):
                until(act, c_tr, D * t, z + 1)
                nc.scalar.copy(xgT[:, z % 2, :, :, :].rearrange("p k a n -> p (k a n)"),
                               PS[:, z % 2, :].bitcast(F16)).then_inc(c_xT[0], 1)

            def gelus(t, z):
                expert = act.value_load(texp_i[0:1, bass.ds(D * t + z, 1)], min_val=0, max_val=E_ - 1)
                until(act, c_up, D * t, z + 1)
                for f in range(FE):
                    last = nc.scalar.activation(ga[:, z, f, :], PS[:, 2 + z % 2, f * P:(f + 1) * P], ACT.Gelu,
                                                bias=ew[:, bass.ds(expert, 1), WB1 + f].bitcast(F32),
                                                scale=ew[:, bass.ds(expert, 1), WDOWN].bitcast(F32))
                last.then_inc(c_gelu[0], 1)
                until(act, c_gelu, D * t, z + 1)
                nc.scalar.activation(gq[:, z, :, 0, :], ga[:, z, :, :], ACT.Copy,
                                     scale=ew[:, bass.ds(expert, 1), WHUP].bitcast(F32)).then_inc(c_hi[0], 1)

            def step(t, k, first, last):
                if not last or k + 2 < D:
                    rows_out(*tile(t, k + 2))
                if k >= -1 and (not last or k + 1 < D):
                    gelus(*tile(t, k + 1))

            act.wait_ge(routed, 2)
            in_steps(act, step)

        @block.vector
        def _(dve):
            start_at_one(dve, "dve")
            n = [0]

            def link(ins):
                n[0] += 1
                ins.then_inc(vstep, 1)
                dve.wait_ge(vstep, n[0])

            def powers(src, pw):
                link(nc.vector.tensor_scalar(pw, src, 2.0 ** -100, None, ALU.max))
                link(nc.vector.tensor_scalar(pw.bitcast(I32), pw.bitcast(I32), 0x7F800000, None, ALU.bitwise_and))

            def largest(dst, src, axis=mybir.AxisListType.XY):
                return nc.vector.tensor_reduce(dst, src, axis=axis, op=ALU.max, apply_absolute_value=True)

            dve.wait_ge(sw_loaded, 16 * 4)
            dve.wait_ge(all_max, 1)
            powers(wall[:, :], wpow[:, :])
            link(nc.vector.reciprocal(wup[:, :], wpow[:, :]))
            link(nc.vector.tensor_scalar(wup[:, :], wup[:, :], TOP, None, ALU.mult))
            nc.vector.tensor_scalar(wdown[:, :], wpow[:, :], 1.0 / TOP, None, ALU.mult).then_inc(scaled, 1)
            for order, (dst, src, col) in enumerate(((gwp, gws[:, :, :], 2), (sw1p, stage_sw1, 0), (sw2p, stage_sw2, 1))):
                dve.wait_ge(high_ready, order + 1)
                nc.vector.scalar_tensor_tensor(dst[:, :, 1, :], src, wup[:, col:col + 1], dst[:, :, 0, :],
                                               ALU.mult, ALU.subtract).then_inc(stage_free, 1)
            dve.wait_ge(scaled, 1)
            dve.wait_ge(loaded, 16 * 3)
            nc.vector.tensor_copy(ident[:, :], identf[:, :])
            nc.vector.tensor_copy(tri[:, :], trif[:, :]).then_inc(cast, 1)
            link(nc.vector.tensor_copy(lanesb[:, :], lanes[:, :]))
            link(nc.vector.scalar_tensor_tensor(hb[:, :], wall[:, 0:1], float(C), wall[:, 3:4], ALU.mult, ALU.add))
            powers(hb[:, :], hpow[:, :])
            link(nc.vector.reciprocal(hup[:, :], hpow[:, :]))
            link(nc.vector.tensor_scalar(hup[:, :], hup[:, :], 2.0 ** 14, None, ALU.mult))
            link(nc.vector.tensor_scalar(hdn[:, :], hpow[:, :], 2.0 ** -14, None, ALU.mult))
            nc.vector.tensor_tensor(ydn[:, :], hdn[:, :], wdown[:, 1:2], ALU.mult).then_inc(route_dve, 1)
            dve.wait_ge(route_dve, 1)
            dve.wait_ge(b1_loaded, 16 * 3)

            def columns(b):
                for k in (1, 3):
                    until(dve, tr_done, b, k + 1)
                    nc.vector.tensor_copy(xT[:, k, :, :].rearrange("p a n -> p (a n)"),
                                          PS[:, k, :].bitcast(F16)).then_inc(xT_odd[0], 1)

            def expert_scales(b, row):
                n = [1]

                def step(ins):
                    n[0] += 1
                    ins.then_inc(e_step[0], 1)
                    until(dve, e_step, b, n[0])

                f = row.bitcast(F32)
                until(dve, e_all, b, 1)
                step(nc.vector.tensor_copy(eall[:, :], PS[:, 4, 2 * P:2 * P + 3]))
                step(nc.vector.tensor_scalar(epow[:, :], eall[:, :], 2.0 ** -100, None, ALU.max))
                nc.vector.scalar_tensor_tensor(ehb[:, :], eall[:, 0:1], float(C), eall[:, 2:3], ALU.mult, ALU.add)
                step(nc.vector.tensor_scalar(epow[:, :].bitcast(I32), epow[:, :].bitcast(I32), 0x7F800000, None, ALU.bitwise_and))
                nc.vector.tensor_scalar(edown[:, :], epow[:, :], 1.0 / TOP, None, ALU.mult)
                nc.vector.reciprocal(eup[:, :], epow[:, :])
                step(nc.vector.tensor_scalar(ehb[:, :], ehb[:, :], 2.0 ** -100, None, ALU.max))
                nc.vector.tensor_scalar(f[:, WDOWN:WDOWN + 1], epow[:, 0:1], 1.0 / TOP, None, ALU.mult)
                step(nc.vector.tensor_scalar(eup[:, :], eup[:, :], TOP, None, ALU.mult))
                step(nc.vector.tensor_scalar(ehb[:, :].bitcast(I32), ehb[:, :].bitcast(I32), 0x7F800000, None, ALU.bitwise_and))
                nc.vector.tensor_scalar(ehdn[:, :], ehb[:, :], 2.0 ** -14, None, ALU.mult)
                step(nc.vector.reciprocal(ehup[:, :], ehb[:, :]))
                nc.vector.tensor_scalar(f[:, WHUP:WHUP + 1], ehup[:, :], 2.0 ** 14, None, ALU.mult)
                nc.vector.tensor_tensor(f[:, WYDN:WYDN + 1], ehdn[:, :], edown[:, 1:2], ALU.mult).then_inc(e_scaled[0], 1)

            def turn(b, first, last):
                row = ew[:, bass.ds(b, 1), :].rearrange("p o w -> p (o w)")
                if first:
                    columns(0)
                for f in range(FS):
                    until(dve, ghi_done, b, f + 1)
                    nc.vector.scalar_tensor_tensor(gp[:, f, 1, :], act_h[:, f % 2, :], hup[:, 0:1], gp[:, f, 0, :],
                                                   ALU.mult, ALU.subtract).then_inc(glo_done[0], 1)
                until(dve, lg_done, b, 1)
                nc.vector.tensor_scalar(L[:, bass.ds(b * NT, NT), :], PS[:, 4, P:P + NT * E_].rearrange("p (i e) -> p i e", e=E_),
                                        wdown[:, 2:3], None, ALU.mult).then_inc(lg_read[0], 1)
                if not last:
                    columns(b + 1)
                until(dve, e_loaded, b, 32)
                for k in range(2):
                    largest(emax[:, k:k + 1], stage_e[k])
                largest(emax[:, 2:3], row[:, WB1:WB1 + FE].bitcast(F32), AX).then_inc(e_max[0], 1)
                if not first:
                    until(dve, base_stored, b, 0)
                for i in range(NT):
                    until(dve, down_done, b, i + 1)
                    until(dve, h1b_done, b, i + 1)
                    nc.vector.scalar_tensor_tensor(base[:, i, :], PS[:, 6 + i % 2, :], ydn[:, 0:1], h1t[:, i, :],
                                                   ALU.mult, ALU.add).then_inc(base_done[0], 1)
                    if i == 0:
                        until(dve, e_turned, b, 1)
                        nc.vector.tensor_reduce(etop[:, :], PS[0:3, 4, 0:P], axis=AX, op=ALU.max).then_inc(e_step[0], 1)
                        until(dve, e_step, b, 1)
                        nc.vector.tensor_scalar(ediag[:, :], identf[0:3, 0:3], etop[:, 0:1], None,
                                                ALU.mult).then_inc(e_diag[0], 1)
                    if i == 2:
                        expert_scales(b, row)
                until(dve, e_high, b, 2)
                for k in range(2):
                    w = weights(row)[k]
                    ins = nc.vector.scalar_tensor_tensor(w[:, :, 1, :], stage_e[k], eup[:, k:k + 1], w[:, :, 0, :],
                                                         ALU.mult, ALU.subtract)
                ins.then_inc(e_low[0], 1)

            in_turns(dve, turn)
            until(dve, lg_read, B, 0)
            dve.wait_ge(set_up, 4)
            def bc(ap):
                return ap.unsqueeze(2).to_broadcast([P, TT, E_])

            for e in range(E_):
                nc.vector.memset(prior[:, e:e + 1], float(E_ - e)).then_inc(vstep, 1)
            n[0] += E_
            dve.wait_ge(vstep, n[0])
            pr = prior[:, :].unsqueeze(1).to_broadcast([P, TT, E_])
            for k, src in enumerate((L, L2)):
                link(nc.vector.tensor_reduce(v12[:, k, :], src[:, :, :], axis=AX, op=ALU.max))
                link(nc.vector.tensor_tensor(eqs[:, :, :], src[:, :, :], bc(v12[:, k, :]), ALU.is_equal))
                link(nc.vector.tensor_tensor(eqs[:, :, :], eqs[:, :, :], pr, ALU.mult))
                link(nc.vector.tensor_reduce(m12[:, k, :], eqs[:, :, :], axis=AX, op=ALU.max))
                link(nc.vector.tensor_tensor(oh[:, k, :, :], eqs[:, :, :], bc(m12[:, k, :]), ALU.is_equal))
                if k == 0:
                    link(nc.vector.scalar_tensor_tensor(L2[:, :, :], oh[:, 0, :, :], MASKED, L[:, :, :], ALU.mult, ALU.add))
            nc.vector.tensor_tensor(dlt[:, :], v12[:, 1, :], v12[:, 0, :], ALU.subtract).then_inc(routed, 1)
            nc.vector.tensor_tensor(both[:, :, :], oh[:, 0, :, :], oh[:, 1, :, :], ALU.add).then_inc(route_dve, 1)
            dve.wait_ge(route_pe, 1)
            link(nc.vector.tensor_copy(pre[:, :, :], PS[:, 0, 0:TT * E_].rearrange("p (t e) -> p t e", e=E_)))
            link(nc.vector.tensor_copy(scan[:, 0, :, :], PS[:, 1, 0:TT * E_].rearrange("p (t e) -> p t e", e=E_)))
            link(nc.vector.tensor_tensor(pre[:, :, :], pre[:, :, :], scan[:, 0, :, :], ALU.subtract))
            cur, d = 0, 1
            while d < TT:
                nc.vector.tensor_copy(scan[:, 1 - cur, 0:d, :], scan[:, cur, 0:d, :])
                link(nc.vector.tensor_tensor(scan[:, 1 - cur, d:, :], scan[:, cur, d:, :], scan[:, cur, 0:TT - d, :], ALU.add))
                cur, d = 1 - cur, 2 * d
            link(nc.vector.tensor_scalar(ntile[:, :], scan[:, cur, TT - 1, :], 1.0 / P, (P - 1.0) / P - 0.5 + 0.5 / P, ALU.mult, ALU.add))
            link(nc.vector.tensor_scalar(nt2[:, :], ntile[:, :], ROUND, ROUND, ALU.add, ALU.subtract))
            link(nc.vector.tensor_copy(tend[:, 0, :], nt2[:, :]))
            tc, d = 0, 1
            while d < E_:
                nc.vector.tensor_copy(tend[:, 1 - tc, 0:d], tend[:, tc, 0:d])
                link(nc.vector.tensor_tensor(tend[:, 1 - tc, d:], tend[:, tc, d:], tend[:, tc, 0:E_ - d], ALU.add))
                tc, d = 1 - tc, 2 * d
            link(nc.vector.tensor_tensor(ntile[:, :], tend[:, tc, :], nt2[:, :], ALU.subtract))
            link(nc.vector.tensor_tensor(posn[:, :, :], pre[:, :, :], scan[:, cur, :, :], ALU.add))
            link(nc.vector.scalar_tensor_tensor(posn[:, :, :], ntile[:, :].unsqueeze(1).to_broadcast([P, TT, E_]), float(P),
                                                posn[:, :, :], ALU.mult, ALU.add))
            for k in range(2):
                link(nc.vector.tensor_tensor(eqs[:, :, :], oh[:, k, :, :], posn[:, :, :], ALU.mult))
                link(nc.vector.tensor_reduce(slot[:, k, :], eqs[:, :, :], axis=AX, op=ALU.add))
            link(nc.vector.tensor_copy(slot_i[:, :, :], slot[:, :, :]))
            link(nc.vector.tensor_scalar(hi[:, :, :], slot[:, :, :], 1.0 / P, 0.5 / P - 0.5, ALU.mult, ALU.add))
            link(nc.vector.tensor_scalar(hi[:, :, :], hi[:, :, :], ROUND, ROUND, ALU.add, ALU.subtract))
            link(nc.vector.scalar_tensor_tensor(lo[:, :, :], hi[:, :, :], -float(P), slot[:, :, :], ALU.mult, ALU.add))
            link(nc.vector.tensor_copy(lohi[:, 0, :], lo[:, :, :].rearrange("p k t -> p (k t)")))
            link(nc.vector.tensor_copy(lohi[:, 1, :], hi[:, :, :].rearrange("p k t -> p (k t)")))
            for k in range(2):
                of = slice(k * TT, (k + 1) * TT)
                nc.vector.tensor_tensor(lo_hot[:, of, :], lanesb[:, :].unsqueeze(1).to_broadcast([P, TT, P]),
                                        lohi[:, 0, of].unsqueeze(2).to_broadcast([P, TT, P]), ALU.is_equal)
                place = hi_hot[:, of, 1, :]
                link(nc.vector.tensor_tensor(place, lanesb[:, 0:TILES].unsqueeze(1).to_broadcast([P, TT, TILES]),
                                             lohi[:, 1, of].unsqueeze(2).to_broadcast([P, TT, TILES]), ALU.is_equal))
                link(nc.vector.tensor_scalar(hi_hot[:, of, 0, :], place, part[:, 0:1], None, ALU.mult))
                nc.vector.tensor_tensor(place, place, lanesb[:, 0:TT].unsqueeze(2).to_broadcast([P, TT, TILES]),
                                        ALU.mult).then_inc(route_dve, 1)
            link(nc.vector.tensor_tensor(tsel[:, :, 0:E_ - 1], lanes[:, 0:TILES].unsqueeze(2).to_broadcast([P, TILES, E_ - 1]),
                                         tend[:, tc, 0:E_ - 1].unsqueeze(1).to_broadcast([P, TILES, E_ - 1]), ALU.is_ge))
            link(nc.vector.tensor_reduce(texp[:, :], tsel[:, :, 0:E_ - 1], axis=AX, op=ALU.add))
            link(nc.vector.tensor_copy(texp_i[:, :], texp[:, :]))
            dve.wait_ge(route_pe, 2)
            link(nc.vector.tensor_copy(tok_f[:, :], PS[:, 2, 0:TILES]))
            link(nc.vector.scalar_tensor_tensor(tok_f[:, :], PS[:, 2, TILES:2 * TILES], float(P), tok_f[:, :], ALU.mult, ALU.add))
            nc.vector.tensor_copy(tok_i[:, 0:TILES], tok_f[:, :]).then_inc(routed, 1)
            dve.wait_ge(route_act, 1)
            link(nc.vector.tensor_scalar(gate[:, 0, :], exd[:, :], 1.0, None, ALU.add))
            link(nc.vector.reciprocal(gate[:, 0, :], gate[:, 0, :]))
            link(nc.vector.tensor_tensor(gate[:, 1, :], exd[:, :], gate[:, 0, :], ALU.mult))
            dve.wait_ge(routed, 2)

            def load_w(t, z, which, used, tu, zu):
                expert = dve.value_load(texp_i[0:1, bass.ds(D * t + z, 1)], min_val=0, max_val=E_ - 1)
                a, c = ((0, W1N // 2), (W1N // 2, WROW))[which]
                if used is not None:
                    until(dve, used, D * tu, zu + 1)
                nc.vector.tensor_copy(wcur[:, z % 2, a:c], ew[:, bass.ds(expert, 1), a:c].rearrange("p o w -> p (o w)")
                                      ).then_inc((c_w1, c_w2)[which][0], 1)

            def low(t, z):
                until(dve, c_hi, D * t, z + 1)
                until(dve, c_w2, D * t, z + 1)
                nc.vector.scalar_tensor_tensor(gq[:, z, :, 1, :], ga[:, z, :, :],
                                               wcur[:, z % 2, WHUP:WHUP + 1].bitcast(F32), gq[:, z, :, 0, :],
                                               ALU.mult, ALU.subtract).then_inc(c_lo[0], 1)

            def rows(t, z):
                expert = dve.value_load(texp_i[0:1, bass.ds(D * t + z, 1)], min_val=0, max_val=E_ - 1)
                until(dve, c_down, D * t, z + 1)
                until(dve, c_store[z], t, 0)
                nc.vector.scalar_tensor_tensor(yt[:, z, :], PS[:, 4 + z % 2, :],
                                               wcur[:, z % 2, WYDN:WYDN + 1].bitcast(F32),
                                               b2r[:, bass.ds(expert, 1), :].rearrange("p o n -> p (o n)"),
                                               ALU.mult, ALU.add).then_inc(c_y[0], 1)

            def step(t, k, first, last):
                if not last or k + 2 < D:
                    load_w(*tile(t, k + 2), 0, None if k < 0 else c_up, *tile(t, k))
                if k >= 0 and (not last or k < D):
                    low(*tile(t, k))
                if k >= 1:
                    rows(*tile(t, k - 1))
                if k >= -1 and (not last or k + 1 < D):
                    load_w(*tile(t, k + 1), 1, None if k < 1 else c_y, *tile(t, k - 1))

            in_steps(dve, step)

            with dve.Fori(0, TT // D) as t:
                for z in range(D):
                    until(dve, d_gather[z], t, 32)
                    until(dve, d_base[z], t, 16)
                    nc.vector.scalar_tensor_tensor(bt[:, z, :], yg[:, z, 0, :], gate[:, 0, bass.ds(D * t + z, 1)],
                                                   bt[:, z, :], ALU.mult, ALU.add).then_inc(d_acc[0], 1)
                    until(dve, d_acc, D * t, z + 1)
                    nc.vector.scalar_tensor_tensor(bt[:, z, :], yg[:, z, 1, :], gate[:, 1, bass.ds(D * t + z, 1)],
                                                   bt[:, z, :], ALU.mult, ALU.add).then_inc(d_done[z][0], 1)

        @block.tensor
        def _(pe):
            start_at_one(pe, "pe")
            PAIRS = ((0, 0), (0, 1), (1, 0))
            pe.wait_ge(set_up, 4)
            pe.wait_ge(cast, 1)
            pe.wait_ge(stage_free, 3)

            def columns(b):
                until(pe, x2_loaded, b, 16)
                for k in range(KT):
                    for i in range(NT):
                        for a in range(2):
                            last = nc.tensor.transpose(PS[:, k, :].bitcast(F16)[:, a * N + i * P:a * N + (i + 1) * P],
                                                       x2t[:, i, a * C + k * P:a * C + (k + 1) * P], ident[:, :])
                    last.then_inc(tr_done[0], 1)

            def turn(b, first, last_turn):
                if first:
                    columns(0)
                until(pe, xT_even, b, 2)
                until(pe, xT_odd, b, 2)
                if not first:
                    until(pe, gelu_done, b, 0)
                    until(pe, e_scaled, b - 1, 1)
                    until(pe, lg_read, b - 1, 1)
                for f in range(FS):
                    if f >= 2:
                        until(pe, gelu_done, b, f - 1)
                    m = 0
                    for k in range(KT):
                        for xa, wa in PAIRS:
                            last = nc.tensor.matmul(PS[:, 4 + f % 2, :], sw1p[:, k, wa, f * P:(f + 1) * P], xT[:, k, xa, :],
                                                    start=(m == 0), stop=(m == 3 * KT - 1))
                            m += 1
                    last.then_inc(up_done[0], 1)
                until(pe, gelu_done, b, 3)
                for i in range(NT):
                    m = 0
                    for k in range(KT):
                        for xa, wa in PAIRS:
                            last = nc.tensor.matmul(PS[:, 4, P + i * E_:P + (i + 1) * E_], xT[:, k, xa, i * P:(i + 1) * P],
                                                    gwp[:, k, wa, :], start=(m == 0), stop=(m == 3 * KT - 1))
                            m += 1
                last.then_inc(lg_done[0], 1)
                if not last_turn:
                    columns(b + 1)
                until(pe, glo_done, b, FS)
                for i in range(NT):
                    if i == 1:
                        until(pe, e_max, b, 1)
                        nc.tensor.transpose(PS[0:3, 4, 0:P], emax[:, :], identf[:, :]).then_inc(e_turned[0], 1)
                    if i == 2:
                        until(pe, e_diag, b, 1)
                        nc.tensor.matmul(PS[:, 4, 2 * P:2 * P + 3], eones[:, :], ediag[:, :], start=True,
                                         stop=True).then_inc(e_all[0], 1)
                    if i >= 2 or not first:
                        until(pe, base_done, b, i - 1)
                    m = 0
                    for f in range(FS):
                        for ga_, wa in PAIRS:
                            last = nc.tensor.matmul(PS[:, 6 + i % 2, :], gp[:, f, ga_, i * P:(i + 1) * P], sw2p[:, f, wa, :],
                                                    start=(m == 0), stop=(m == 3 * FS - 1))
                            m += 1
                    last.then_inc(down_done[0], 1)

            in_turns(pe, turn)
            pe.wait_ge(route_dve, 2)
            te = both[:, :, :].rearrange("p t e -> p (t e)")
            nc.tensor.matmul(PS[:, 0, 0:TT * E_], tri[:, :], te, start=True, stop=True)
            nc.tensor.matmul(PS[:, 1, 0:TT * E_], ones[:, :], te, start=True, stop=True).then_inc(route_pe, 1)
            for m in range(2 * TT):
                if m % TT == 0:
                    pe.wait_ge(route_dve, 3 + m // TT)
                last = nc.tensor.matmul(PS[:, 2, 0:2 * TILES], lo_hot[:, m, :], hi_hot[:, m, :, :].rearrange("p a m -> p (a m)"),
                                        start=(m == 0), stop=(m == 2 * TT - 1))
            last.then_inc(route_pe, 1)
            pe.wait_ge(routed, 2)

            def turn(t, z):
                until(pe, c_gather[z], t, 16)
                for k in range(KT):
                    for a in range(2):
                        q = (2 * k + a) * P
                        last = nc.tensor.transpose(PS[:, z % 2, :].bitcast(F16)[:, q:q + P],
                                                   xg[:, z, a * C + k * P:a * C + (k + 1) * P], ident[:, :])
                last.then_inc(c_tr[0], 1)

            def up(t, z, fresh):
                w1v = weights(wcur[:, z % 2, :])[0]
                until(pe, c_xT, D * t, z + 1)
                until(pe, c_w1, D * t, z + 1)
                if not fresh:
                    until(pe, c_gelu, D * t, z - 1)
                for f in range(FE):
                    m = 0
                    for k in range(KT):
                        for xa, wa in PAIRS:
                            last = nc.tensor.matmul(PS[:, 2 + z % 2, f * P:(f + 1) * P], w1v[:, k, wa, f * P:(f + 1) * P],
                                                    xgT[:, z % 2, k, xa, :], start=(m == 0), stop=(m == 3 * KT - 1))
                            m += 1
                last.then_inc(c_up[0], 1)

            def down(t, z):
                w2v = weights(wcur[:, z % 2, :])[1]
                until(pe, c_lo, D * t, z + 1)
                until(pe, c_w2, D * t, z + 1)
                m = 0
                for f in range(FE):
                    for ga_, wa in PAIRS:
                        last = nc.tensor.matmul(PS[:, 4 + z % 2, :], gq[:, z, f, ga_, :], w2v[:, f, wa, :],
                                                start=(m == 0), stop=(m == 3 * FE - 1))
                        m += 1
                last.then_inc(c_down[0], 1)

            def step(t, k, first, last):
                if not last or k + 2 < D:
                    turn(*tile(t, k + 2))
                if k >= -1 and (not last or k + 1 < D):
                    up(*tile(t, k + 1), k < 1)
                if k >= 1:
                    down(*tile(t, k - 1))

            in_steps(pe, step)


def kernel(**inputs):
    import numpy as _np
    import concourse.bacc as _bacc
    from concourse import mybir as _mybir
    from concourse.bass_utils import run_bass_kernel_spmd as _run

    t = {k.replace("L0_", ""): _np.asarray(v) for k, v in inputs.items()}
    depth = CH // 2
    pos = _np.arange(T, dtype=_np.float32)[:, None]
    rate = (1.0 / _np.power(_np.float32(10000.0), _np.arange(depth, dtype=_np.float32)[None, :] / _np.float32(depth))).astype(_np.float32)
    ang = (pos * rate).astype(_np.float32)
    tri = _np.triu(_np.ones((P, P), _np.float32), 1) * _np.float32(MASKED)
    arrays = {
        "ids": t["x"].reshape(B * NT, P).T,
        "emb": t["tok_emb_table"],
        "pe_tab": _np.concatenate([_np.sin(ang), _np.cos(ang)], axis=1).astype(_np.float32),
        "conv_w": t["tok_conv_w"].transpose(1, 2, 0),
        "conv_b": t["tok_conv_b"].reshape(CH, 1),
        "spos0": t["tok_spos0"],
        "spos1": t["tok_spos1"],
        "wqkv": t["attn_w_qkv"].T,
        "wproj": t["attn_w_proj"].T,
        "gate_w": t["ffn_gate_w"],
        "w1": t["ffn_w1"],
        "b1": t["ffn_b1"].reshape(E_, HID // P, P).transpose(2, 0, 1),
        "w2": t["ffn_w2"],
        "b2": t["ffn_b2"],
        "sw1": t["ffn_shared_w1"],
        "sb1": t["ffn_shared_b1"].reshape(SH // P, P).T,
        "sw2": t["ffn_shared_w2"],
        "sb2": t["ffn_shared_b2"],
        "ident_in": _np.eye(P, dtype=_np.float32),
        "mask_in": tri,
        "maskT_in": tri.T,
        "tri_in": _np.triu(_np.ones((P, P), _np.float32), 1),
        "lanes_in": _np.tile(_np.arange(P, dtype=_np.float32), (P, 1)),
    }
    nc = _bacc.Bacc("TRN2", target_bir_lowering=False, num_devices=1)
    sent, args = {}, []
    for name, a in arrays.items():
        a = _np.ascontiguousarray(a)
        sent[f"in_{name}"] = a
        args.append(nc.dram_tensor(f"in_{name}", a.shape, _mybir.dt.from_np(a.dtype), kind="ExternalInput").ap())
    args.append(nc.dram_tensor("out_h", (B * N, C), _mybir.dt.float32, kind="ExternalOutput").ap())
    build(nc, *args)
    r = _run(nc, [sent], core_ids=[0])
    return r.results[0]["out_h"].reshape(B, N, C)
```
